# Optimizing a Trainium2 kernel written in Bass

```python
import numpy as np
import jax
import jax.numpy as jnp

def _softmax(x, axis=-1):
    return jax.nn.softmax(x, axis=axis)

def _gelu(x):
    return jax.nn.gelu(x, approximate=True)

def _silu(x):
    return jax.nn.silu(x)

def _sigmoid(x):
    return jax.nn.sigmoid(x)

def _layernorm(x, axis=-1, eps=1e-05):
    m = jnp.mean(x, axis=axis, keepdims=True)
    v = jnp.var(x, axis=axis, keepdims=True)
    return (x - m) / jnp.sqrt(v + eps)

def _scatter_add(tgt, idx, src, axis=0):
    return tgt.at[idx].add(src)

def _segment_sum(src, seg, n):
    return jax.ops.segment_sum(src, seg, n)
kernel_name = 'mk_adaln_attn_ffn_d1_seqx_r4_7b1700'

def setup_inputs(seed: int=0):
    np.random.seed(seed)
    _w = jnp.asarray

    def _rec_inputs():
        import jax
        import jax.numpy as jnp
        _rk = jax.random.key(seed)
        x = -0.0003929 + 0.9999 * jax.random.normal(jax.random.fold_in(_rk, 1), (64, 64, 256), jnp.float32)
        _lenS = 64 - jax.random.randint(jax.random.fold_in(_rk, 7), (64,), 0, max(1, 64 // 4) + 1, jnp.int32)
        _lenS2 = 64 - jax.random.randint(jax.random.fold_in(_rk, 8), (64,), 0, max(1, 64 // 4) + 1, jnp.int32)
        itok_B_0_2 = jax.random.randint(jax.random.fold_in(_rk, 11), (64,), 0, 3, jnp.int32)
        return (x, itok_B_0_2)
    x, itok_B_0_2 = _rec_inputs()

    def _L0_cond_setup():
        import jax, jax.numpy as jnp
        import numpy as np
        D_MODEL = 256
        D_FF = 1024
        N_EXPERTS = 5
        BATCH = 8
        SEQ = 512

        def _gated_ffn(x, wi0, wi1, wo):
            g = jax.nn.gelu(x @ wi0, approximate=True)
            l = x @ wi1
            return g * l @ wo
        key = jax.random.key(seed)
        ks = jax.random.split(key, 12)
        s = 0.02
        inp = {'hidden_states': jax.random.normal(ks[0], (BATCH, SEQ, D_MODEL), jnp.float32), 'type_label': jax.random.randint(ks[1], (BATCH,), 0, N_EXPERTS, jnp.int32), 'Wi0': jax.random.normal(ks[2], (N_EXPERTS, D_MODEL, D_FF), jnp.float32) * s, 'Wi1': jax.random.normal(ks[3], (N_EXPERTS, D_MODEL, D_FF), jnp.float32) * s, 'Wo': jax.random.normal(ks[4], (N_EXPERTS, D_FF, D_MODEL), jnp.float32) * s, 'sWi0': jax.random.normal(ks[5], (D_MODEL, D_FF), jnp.float32) * s, 'sWi1': jax.random.normal(ks[6], (D_MODEL, D_FF), jnp.float32) * s, 'sWo': jax.random.normal(ks[7], (D_FF, D_MODEL), jnp.float32) * s, 'g0': jax.random.normal(ks[8], (2 * D_MODEL, D_MODEL), jnp.float32) * s, 'g1': jax.random.normal(ks[9], (D_MODEL, 2), jnp.float32) * s}
        return inp
    _L0_cond_all = _L0_cond_setup()
    _L0_cond_in = {k: v for k, v in _L0_cond_all.items() if k in ('Wi0', 'Wi1', 'Wo', 'sWi0', 'sWi1', 'sWo', 'g0', 'g1')}
    del _L0_cond_all

    def _L0_attn_setup():
        import jax, jax.numpy as jnp
        import numpy as np
        import math
        HIDDEN = 256
        HEADS = 16
        HEAD_DIM = HIDDEN // HEADS
        B, S = (2, 512)

        def _xavier(key, shape):
            fan_in, fan_out = (shape[1], shape[0])
            limit = math.sqrt(6.0 / (fan_in + fan_out))
            return jax.random.uniform(key, shape, jnp.float32, -limit, limit)
        key = jax.random.key(seed)
        ks = jax.random.split(key, 5)
        x = jax.random.normal(ks[0], (B, S, HIDDEN), jnp.float32)
        Wq = _xavier(ks[1], (HIDDEN, HIDDEN))
        Wk = _xavier(ks[2], (HIDDEN, HIDDEN))
        Wv = _xavier(ks[3], (HIDDEN, HIDDEN))
        Wo = _xavier(ks[4], (HIDDEN, HIDDEN))
        bq = jnp.zeros((HIDDEN,), jnp.float32)
        bk = jnp.zeros((HIDDEN,), jnp.float32)
        bv = jnp.zeros((HIDDEN,), jnp.float32)
        bo = jnp.zeros((HIDDEN,), jnp.float32)
        return {'x': x, 'Wq': Wq, 'bq': bq, 'Wk': Wk, 'bk': bk, 'Wv': Wv, 'bv': bv, 'Wo': Wo, 'bo': bo}
    _L0_attn_all = _L0_attn_setup()
    _L0_attn_in = {k: v for k, v in _L0_attn_all.items() if k in ('Wq', 'bq', 'Wk', 'bk', 'Wv', 'bv', 'Wo', 'bo')}
    del _L0_attn_all

    def _L0_cond2_setup():
        import jax, jax.numpy as jnp
        import numpy as np
        B, S, D, F, E = (8, 256, 256, 1024, 4)

        def _dense(x, wi, wo):
            return jax.nn.relu(x @ wi) @ wo
        key = jax.random.key(seed)
        ks = jax.random.split(key, 10)
        scale = 0.02
        return {'hidden_states': jax.random.normal(ks[0], (B, S, D), jnp.float32), 'type_idx': jax.random.randint(ks[1], (B,), 0, 3, jnp.int32), 'expert_wi': jax.random.normal(ks[2], (E, D, F), jnp.float32) * scale, 'expert_wo': jax.random.normal(ks[3], (E, F, D), jnp.float32) * scale, 'share_wi': jax.random.normal(ks[4], (3, D, F), jnp.float32) * scale, 'share_wo': jax.random.normal(ks[5], (3, F, D), jnp.float32) * scale, 'gate_vecs': jnp.array([[0.22, 0.22, 0.2, 0.2], [0.2, 0.22, 0.22, 0.2], [0.2, 0.2, 0.22, 0.22]], jnp.float32), 'gate_w1': jax.random.normal(ks[6], (4 * D, D), jnp.float32) * scale, 'gate_w2': jax.random.normal(ks[7], (D, 4), jnp.float32) * scale}
    _L0_cond2_all = _L0_cond2_setup()
    _L0_cond2_in = {k: v for k, v in _L0_cond2_all.items() if k in ('expert_wi', 'expert_wo', 'share_wi', 'share_wo', 'gate_vecs', 'gate_w1', 'gate_w2')}
    del _L0_cond2_all

    def _L0_ffn_setup():
        import jax, jax.numpy as jnp
        import numpy as np
        N_EMBD = 256
        N_EXPERTS = 8
        TOP_K = 2
        CAPACITY_FACTOR = 1.25
        key = jax.random.key(seed)
        ks = jax.random.split(key, 8)
        B, T, C, E, H = (8, 512, N_EMBD, N_EXPERTS, 4 * N_EMBD)
        w = lambda k, shape: jax.random.normal(k, shape, jnp.float32) * 0.02
        return {'x': jax.random.normal(ks[0], (B, T, C), jnp.float32), 'rW1': w(ks[1], (C, H)), 'rb1': jnp.zeros((H,), jnp.float32), 'rW2': w(ks[2], (H, H)), 'rb2': jnp.zeros((H,), jnp.float32), 'rW3': w(ks[3], (H, E)), 'rb3': jnp.zeros((E,), jnp.float32), 'eW1': w(ks[4], (E, C, H)), 'eb1': jnp.zeros((E, H), jnp.float32), 'eW2': w(ks[5], (E, H, C)), 'eb2': jnp.zeros((E, C), jnp.float32)}
    _L0_ffn_all = _L0_ffn_setup()
    _L0_ffn_in = {k: v for k, v in _L0_ffn_all.items() if k in ('rW1', 'rb1', 'rW2', 'rb2', 'rW3', 'rb3', 'eW1', 'eb1', 'eW2', 'eb2')}
    del _L0_ffn_all
    return {'x': x, 'itok_B_0_2': itok_B_0_2, 'L0_cond_Wi0': _L0_cond_in['Wi0'], 'L0_cond_Wi1': _L0_cond_in['Wi1'], 'L0_cond_Wo': _L0_cond_in['Wo'], 'L0_cond_sWi0': _L0_cond_in['sWi0'], 'L0_cond_sWi1': _L0_cond_in['sWi1'], 'L0_cond_sWo': _L0_cond_in['sWo'], 'L0_cond_g0': _L0_cond_in['g0'], 'L0_cond_g1': _L0_cond_in['g1'], 'L0_attn_Wq': _L0_attn_in['Wq'], 'L0_attn_bq': _L0_attn_in['bq'], 'L0_attn_Wk': _L0_attn_in['Wk'], 'L0_attn_bk': _L0_attn_in['bk'], 'L0_attn_Wv': _L0_attn_in['Wv'], 'L0_attn_bv': _L0_attn_in['bv'], 'L0_attn_Wo': _L0_attn_in['Wo'], 'L0_attn_bo': _L0_attn_in['bo'], 'L0_cond2_expert_wi': _L0_cond2_in['expert_wi'], 'L0_cond2_expert_wo': _L0_cond2_in['expert_wo'], 'L0_cond2_share_wi': _L0_cond2_in['share_wi'], 'L0_cond2_share_wo': _L0_cond2_in['share_wo'], 'L0_cond2_gate_vecs': _L0_cond2_in['gate_vecs'], 'L0_cond2_gate_w1': _L0_cond2_in['gate_w1'], 'L0_cond2_gate_w2': _L0_cond2_in['gate_w2'], 'L0_ffn_rW1': _L0_ffn_in['rW1'], 'L0_ffn_rb1': _L0_ffn_in['rb1'], 'L0_ffn_rW2': _L0_ffn_in['rW2'], 'L0_ffn_rb2': _L0_ffn_in['rb2'], 'L0_ffn_rW3': _L0_ffn_in['rW3'], 'L0_ffn_rb3': _L0_ffn_in['rb3'], 'L0_ffn_eW1': _L0_ffn_in['eW1'], 'L0_ffn_eb1': _L0_ffn_in['eb1'], 'L0_ffn_eW2': _L0_ffn_in['eW2'], 'L0_ffn_eb2': _L0_ffn_in['eb2']}

def reference(x, itok_B_0_2, L0_cond_Wi0, L0_cond_Wi1, L0_cond_Wo, L0_cond_sWi0, L0_cond_sWi1, L0_cond_sWo, L0_cond_g0, L0_cond_g1, L0_attn_Wq, L0_attn_bq, L0_attn_Wk, L0_attn_bk, L0_attn_Wv, L0_attn_bv, L0_attn_Wo, L0_attn_bo, L0_cond2_expert_wi, L0_cond2_expert_wo, L0_cond2_share_wi, L0_cond2_share_wo, L0_cond2_gate_vecs, L0_cond2_gate_w1, L0_cond2_gate_w2, L0_ffn_rW1, L0_ffn_rb1, L0_ffn_rW2, L0_ffn_rb2, L0_ffn_rW3, L0_ffn_rb3, L0_ffn_eW1, L0_ffn_eb1, L0_ffn_eW2, L0_ffn_eb2):
    import jax
    import jax.numpy as jnp

    def _L0_cond_ref(hidden_states, type_label, Wi0, Wi1, Wo, sWi0, sWi1, sWo, g0, g1):
        import jax, jax.numpy as jnp
        import numpy as np
        D_MODEL = 256
        D_FF = 1024
        N_EXPERTS = 5
        BATCH = 8
        SEQ = 512

        def _gated_ffn(x, wi0, wi1, wo):
            g = jax.nn.gelu(x @ wi0, approximate=True)
            l = x @ wi1
            return g * l @ wo
        share_out = _gated_ffn(hidden_states, sWi0, sWi1, sWo)
        wi0 = Wi0[type_label]
        wi1 = Wi1[type_label]
        wo = Wo[type_label]
        hg = jax.nn.gelu(jnp.einsum('bsd,bdf->bsf', hidden_states, wi0), approximate=True)
        hl = jnp.einsum('bsd,bdf->bsf', hidden_states, wi1)
        expert_out = jnp.einsum('bsf,bfd->bsd', hg * hl, wo)
        gate_in = jnp.concatenate([expert_out[:, 0], share_out[:, 0]], axis=-1)
        weights = jax.nn.softmax(jax.nn.relu(gate_in @ g0) @ g1, axis=-1)
        w0 = weights[:, 0][:, None, None]
        w1 = weights[:, 1][:, None, None]
        return expert_out * w0 + share_out * w1

    def _L0_attn_ref(x, Wq, bq, Wk, bk, Wv, bv, Wo, bo):
        import jax, jax.numpy as jnp
        import numpy as np
        import math
        HIDDEN = 256
        HEADS = 16
        HEAD_DIM = HIDDEN // HEADS
        B, S = (2, 512)

        def _xavier(key, shape):
            fan_in, fan_out = (shape[1], shape[0])
            limit = math.sqrt(6.0 / (fan_in + fan_out))
            return jax.random.uniform(key, shape, jnp.float32, -limit, limit)
        b, s, d = x.shape
        h, hd = (HEADS, HEAD_DIM)
        q = (x @ Wq.T + bq).reshape(b, s, h, hd).transpose(0, 2, 1, 3)
        k = (x @ Wk.T + bk).reshape(b, s, h, hd).transpose(0, 2, 1, 3)
        v = (x @ Wv.T + bv).reshape(b, s, h, hd).transpose(0, 2, 1, 3)
        scores = jnp.einsum('bhqd,bhkd->bhqk', q, k) / math.sqrt(hd)
        causal = jnp.tril(jnp.ones((s, s), bool))
        scores = jnp.where(causal, scores, -jnp.inf)
        attn = jax.nn.softmax(scores, axis=-1)
        out = jnp.einsum('bhqk,bhkd->bhqd', attn, v)
        out = out.transpose(0, 2, 1, 3).reshape(b, s, d)
        return out @ Wo.T + bo

    def _L0_cond2_ref(hidden_states, type_idx, expert_wi, expert_wo, share_wi, share_wo, gate_vecs, gate_w1, gate_w2):
        import jax, jax.numpy as jnp
        import numpy as np
        B, S, D, F, E = (8, 256, 256, 1024, 4)

        def _dense(x, wi, wo):
            return jax.nn.relu(x @ wi) @ wo
        s0 = _dense(hidden_states, share_wi[0], share_wo[0])
        s1 = _dense(hidden_states, share_wi[1], share_wo[1])
        s2 = _dense(hidden_states, share_wi[2], share_wo[2])
        idx_a = type_idx
        idx_b = type_idx + 1
        out_a = jnp.einsum('bsf,bfd->bsd', jax.nn.relu(jnp.einsum('bsd,bdf->bsf', hidden_states, expert_wi[idx_a])), expert_wo[idx_a])
        out_b = jnp.einsum('bsf,bfd->bsd', jax.nn.relu(jnp.einsum('bsd,bdf->bsf', hidden_states, expert_wi[idx_b])), expert_wo[idx_b])
        p = jax.nn.softmax(gate_vecs / 0.1, axis=-1)
        wa = p[type_idx, idx_a][:, None, None]
        wb = p[type_idx, idx_b][:, None, None]
        expert_out = out_a * wa + out_b * wb
        gi = jnp.concatenate([expert_out[:, 0], s0[:, 0], s1[:, 0], s2[:, 0]], axis=-1)
        g = jax.nn.softmax(jax.nn.relu(gi @ gate_w1) @ gate_w2, axis=-1)
        out = expert_out * g[:, 0, None, None] + s0 * g[:, 1, None, None] + s1 * g[:, 2, None, None] + s2 * g[:, 3, None, None]
        return out

    def _L0_ffn_ref(x, rW1, rb1, rW2, rb2, rW3, rb3, eW1, eb1, eW2, eb2):
        import jax, jax.numpy as jnp
        import numpy as np
        N_EMBD = 256
        N_EXPERTS = 8
        TOP_K = 2
        CAPACITY_FACTOR = 1.25
        B, T, C = x.shape
        E = rb3.shape[0]
        k = TOP_K
        capacity = int(T / E * CAPACITY_FACTOR)
        h = jax.nn.relu(x @ rW1 + rb1)
        h = jax.nn.relu(h @ rW2 + rb2)
        scales = jax.nn.softmax(h @ rW3 + rb3, axis=-1)
        topk_scales, topk_experts = jax.lax.top_k(scales, k)
        e_flat = topk_experts.reshape(B, T * k)
        onehot = jax.nn.one_hot(e_flat, E, dtype=jnp.int32)
        pos_excl = jnp.cumsum(onehot, axis=1) - onehot
        pos = jnp.take_along_axis(pos_excl, e_flat[..., None], axis=-1)[..., 0]
        keep = pos < capacity
        pos_c = jnp.where(keep, pos, capacity)
        b_idx = jnp.broadcast_to(jnp.arange(B)[:, None], (B, T * k))
        x_rep = jnp.repeat(x, k, axis=1)
        dispatched = jnp.zeros((E, B, capacity, C), x.dtype)
        dispatched = dispatched.at[e_flat, b_idx, pos_c].set(jnp.where(keep[..., None], x_rep, 0.0), mode='drop')
        hh = jax.nn.relu(jnp.einsum('ebnc,ech->ebnh', dispatched, eW1) + eb1[:, None, None, :])
        eout = jnp.einsum('ebnh,ehc->ebnc', hh, eW2) + eb2[:, None, None, :]
        gathered = eout[e_flat, b_idx, pos_c]
        gathered = jnp.where(keep[..., None], gathered, 0.0).reshape(B, T, k, C)
        out = jnp.sum(topk_scales[..., None] * gathered, axis=2)
        return out
    x = x + _L0_attn_ref(_L0_cond_ref(x, itok_B_0_2, L0_cond_Wi0, L0_cond_Wi1, L0_cond_Wo, L0_cond_sWi0, L0_cond_sWi1, L0_cond_sWo, L0_cond_g0, L0_cond_g1), L0_attn_Wq, L0_attn_bq, L0_attn_Wk, L0_attn_bk, L0_attn_Wv, L0_attn_bv, L0_attn_Wo, L0_attn_bo)
    x = x + _L0_ffn_ref(_L0_cond2_ref(x, itok_B_0_2, L0_cond2_expert_wi, L0_cond2_expert_wo, L0_cond2_share_wi, L0_cond2_share_wo, L0_cond2_gate_vecs, L0_cond2_gate_w1, L0_cond2_gate_w2), L0_ffn_rW1, L0_ffn_rb1, L0_ffn_rW2, L0_ffn_rb2, L0_ffn_rW3, L0_ffn_rb3, L0_ffn_eW1, L0_ffn_eb1, L0_ffn_eW2, L0_ffn_eb2)
    return x

_drawn_inputs = setup_inputs


def setup_inputs(seed=0):
    import zlib

    import numpy as np

    out = dict(_drawn_inputs(seed))
    spreads = {'L0_attn_bq': (0.0, 0.1),
     'L0_attn_bk': (0.0, 0.1),
     'L0_attn_bv': (0.0, 0.1),
     'L0_attn_bo': (0.0, 0.1),
     'L0_ffn_rb1': (0.0, 0.1),
     'L0_ffn_rb2': (0.0, 0.1),
     'L0_ffn_rb3': (0.0, 0.1),
     'L0_ffn_eb1': (0.0, 0.1),
     'L0_ffn_eb2': (0.0, 0.1)}
    factors = {}
    for name, (base, spread) in spreads.items():
        noise = np.random.default_rng([zlib.crc32(name.encode()), seed]).standard_normal(out[name].shape)
        drawn = base * np.exp(spread * noise) if base else spread * noise
        out[name] = jnp.asarray(drawn.astype(out[name].dtype))
    for name, factor in factors.items():
        out[name] = (out[name] * factor).astype(out[name].dtype)
    return out
```

```python
import numpy as np
import concourse.bass as bass
from concourse import mybir
from contextlib import ExitStack

F32, F16, BF16, I32, U32 = (mybir.dt.float32, mybir.dt.float16, mybir.dt.bfloat16,
                            mybir.dt.int32, mybir.dt.uint32)
ALU = mybir.AluOpType
ACT = mybir.ActivationFunctionType
AX = mybir.AxisListType
ds = bass.ds

B, S, D, F = 64, 64, 256, 1024
NT = B * S
KC, FC = D // 128, F // 128
H, HD = 16, 16
TYPES, E2 = 3, 4
NE, CAP = 8, int(S / 8 * 1.25)
GB = 4
CH = GB * S
NCH = (B + TYPES * (GB - 1)) // GB
NTP = NT + CH
MAT = 2048
SLOT = 2 * MAT
NSLOT = 15
SLOTS = NE * CAP
NA = B // GB
NP = B // 2
TILES = ((0, 1, 2), (3, 4))
PER_E = B * CAP

SX, SW = 4.0, 64.0
SH = SX * SW
SO = SH * SW
SY, SA = 16.0, 16.0
SQ = SY * SA
SZ = 8.0
SR = SZ * SW
SEO, SCW = 64.0, 16.0
MASKED = -1e30
KBD_DVE = 5

C_SHARE = (0, 1, 2)
C_EXP = 3
E_SHARE = ((12, 13), (1, 2), (11, 14))
E_EXP = 3
ATTN_W = 0
R_W1, R_W2 = 0, (12, 13, 1, 2)
MOE_W = ((11, 14), (10, 0))
ATTN_WORK = 3
HID_SLOT = 14
H1_SLOT, H2_SLOT, ZSRC_SLOT = 3, 5, 7
XE_SLOT, CT_SLOT, SEL_SLOT = 3, 8, 10


def build(nc, a):
    ctx = ExitStack()
    with ctx:
        def sb(name, shape, dt):
            return ctx.enter_context(nc.sbuf_tensor(name, shape, dt))

        def sem(name):
            return ctx.enter_context(nc.semaphore(name))

        def scratch(name, shape, dt):
            return nc.dram_tensor(name, shape, dt, kind="Internal").ap()

        arena = sb("arena", [128, NSLOT * SLOT], F16)
        xh = sb("xh", [128, 2, KC, NTP], F16)
        wstage = sb("wstage", [128, 2, MAT], F32)
        misc = sb("misc", [128, 6656], F32)
        row = sb("row", [128, 128], F32)
        pidx = sb("pidx", [128, 1], F32)
        ident = sb("ident", [128, 128], F32)
        ident16 = sb("ident16", [128, 128], F16)
        identb = sb("identb", [128, 128], BF16)
        upper = sb("upper", [128, 128], F32)
        upperb = sb("upperb", [128, 128], BF16)
        causal = sb("causal", [128, 8, S], BF16)
        head_mask = sb("head_mask", [128, 8], F32)
        half_mask = sb("half_mask", [128, 2], F32)
        tbl = sb("tbl", [128, 148], I32)
        wab = sb("wab", [128, 2, 20], F32)
        small = sb("small", [128, 232], F32)
        gate_in = sb("gate_in", [128, 4, KC, B + GB], F32)
        gates = sb("gates", [128, B, 4], F32)
        bias = sb("bias", [128, 8 + 16 + 64], F32)

        outb = misc[:, 0:1024].rearrange("p (m n) -> p m n", m=2)
        gt = misc[:, 1024:2048]
        hid = misc[:, 2560:4608].bitcast(F16).rearrange("p (s h n) -> p s h n", s=4, h=2)
        xf = misc[:, 4608:6656].rearrange("p (u k n) -> p u k n", u=2, k=KC)

        ps = ctx.enter_context(nc.psum_tensor("ps", [128, 8, 512], F32))

        def region(slot, nbytes, dt, at=0):
            lo = slot * SLOT + at // 2
            v = arena[:, lo:lo + nbytes // 2]
            return v if dt == F16 else v.bitcast(dt)

        hidden_f32 = region(HID_SLOT, 4096, F32)
        at = [0]

        def attn_buf(nbytes, dt):
            v = region(ATTN_WORK, nbytes, dt, at[0])
            at[0] += nbytes
            assert at[0] <= 8 * SLOT * 2
            return v
        ex = attn_buf(2048, F32).rearrange("p (k n) -> p k n", k=KC)
        sh = attn_buf(2048, F32).rearrange("p (k n) -> p k n", k=KC)
        xin = attn_buf(2048, F32).rearrange("p (k n) -> p k n", k=KC)
        x1 = attn_buf(2048, F32).rearrange("p (k n) -> p k n", k=KC)
        yd = attn_buf(4096, F16).rearrange("p (h k b r n) -> p h k b r n", h=2, k=KC, b=GB, r=2)
        qh = attn_buf(2048, F16).rearrange("p (h k n) -> p h k n", h=2, k=KC)
        kh = attn_buf(2048, F16).rearrange("p (h k n) -> p h k n", h=2, k=KC)
        kbd = attn_buf(16384, F16).rearrange("p (h m b e n) -> p h m b e n", h=2, m=KC, b=GB, e=8)
        vbd = attn_buf(4096, F16).rearrange("p (h b c) -> p h b c", h=2, b=GB)
        prob = attn_buf(8192, F32).rearrange("p (r n) -> p r n", r=2)
        pt = attn_buf(8192, F16).rearrange("p (r h n) -> p r h n", r=2, h=2)
        oh_ = attn_buf(2048, F16).rearrange("p (h k n) -> p h k n", h=2, k=KC)

        def vp(r, j):
            return ps[:, 6 + r, :].rearrange("p (g c) -> p g c", c=2 * HD)[:, :, j * HD:(j + 1) * HD]

        def vb(part, r, j):
            return vbd[:, part, 2 * r:2 * r + 2, :].rearrange("p b (g c) -> p (b g) c", c=2 * HD)[
                :, :, j * HD:(j + 1) * HD]
        mx = small[:, 0:32].rearrange("p (r n) -> p r n", r=2)
        sm = small[:, 32:64].rearrange("p (r n) -> p r n", r=2)
        rs = small[:, 64:96].rearrange("p (r n) -> p r n", r=2)

        h1 = region(H1_SLOT, 16384, F16).rearrange("p (f h n) -> p f h n", f=FC, h=2)
        h2 = region(H2_SLOT, 16384, F16).rearrange("p (f h n) -> p f h n", f=FC, h=2)
        zsrc = region(ZSRC_SLOT, 8192, F32).rearrange("p (j k n) -> p j k n", j=4, k=KC)
        w3 = small[:, 128:192].bitcast(F16).rearrange("p (h f e) -> p h f e", h=2, f=FC)
        def sel(i):
            return region(SEL_SLOT, 1024, F32, 1024 * i).rearrange("p (t e) -> p t e", t=NP)
        logit, score, top8, oh0, oh1, pos = (sel(i) for i in range(6))
        index8 = region(SEL_SLOT, 1024, U32, 1024 * 6).rearrange("p (t e) -> p t e", t=NP)
        oh16 = region(SEL_SLOT, 512, BF16, 1024 * 7).rearrange("p (t e) -> p t e", t=NP)
        d01 = misc[:, 0:2560].bitcast(F16).rearrange("p (t b s) -> p t b s", t=NP, b=2)
        dsc = misc[:, 2560:5120].bitcast(F16).rearrange("p (h t s) -> p h t s", h=2, t=NP)
        ztok = misc[:, 5120:5632].bitcast(F16).rearrange("p (u h k n) -> p u h k n", u=2, h=2, k=KC)
        dtmp = region(XE_SLOT, 10240, F32).rearrange("p (t s) -> p t s", t=NP)
        xe = region(XE_SLOT, 40960, F16).rearrange("p (h k n) -> p h k n", h=2, k=KC)
        ct = region(CT_SLOT, 16384, F16).rearrange("p (h t n) -> p h t n", h=2, t=NP)
        eo = misc[:, 0:1024].bitcast(F16).rearrange("p (u h n) -> p u h n", u=4, h=2)
        ev = misc[:, 2048:2048 + 2 * D].rearrange("p (u n) -> p u n", u=2)
        zt_ps = [ps[:, u, 0:256].bitcast(F16) for u in range(2)]
        ct_ps = [ps[0:SLOTS, 6 + u, 0:128].bitcast(F16) for u in range(2)]

        def xe_pair(part, k, t, u):
            v = xe[:, part, k, :].rearrange("p (e n) -> p e n", e=NE)
            return v[:, :, ds((t + u) * 2 * CAP, 2 * CAP)].rearrange("p e (b n) -> p e b n", b=2)

        def dp(u, part, k):
            return ps[:, 2 + 2 * u + part, k * 2 * SLOTS:(k + 1) * 2 * SLOTS].rearrange(
                "p (b e n) -> p e b n", b=2, e=NE)
        ebf = misc[:, 1024:2048].bitcast(F16).rearrange("p (u b h n) -> p u b h n", u=2, b=2, h=2)
        x1f = misc[:, 2560:3072].rearrange("p (u k n) -> p u k n", u=2, k=KC)
        yo = misc[:, 3072:3584].rearrange("p (u b k n) -> p u b k n", u=2, b=2, k=KC)

        ab = bias[:, 0:8].rearrange("p (w k) -> p w k", w=4)
        rb1, rb2 = bias[:, 8:16], bias[:, 16:24]
        eb1 = bias[:, 24:88]
        rb3 = small[:, 96:104]
        eb1_now = small[:, 104:112]
        itok_i, itok_f, rank = small[0:B, 192:193].bitcast(I32), small[0:B, 193:194], small[0:B, 194:195]
        gate_vec, type_oh, cnt = small[:, 196:208], small[0:B, 208:211], small[:, 212:215]
        starts, nchunks = small[:, 216:219], small[:, 220:223]
        gsum, tmp3 = small[:, 224:227], small[:, 228:231]
        scr = misc[:, 256:512]
        ones = misc[:, 0:128]
        batch_oh = misc[0:B, 128:192]
        gate_w1 = misc[:, 4608:6656].rearrange("p (k n) -> p k n", k=4 * KC)
        gate_w2 = misc[:, 1024:1032].rearrange("p (k j) -> p k j", k=2)
        gate_w2c = misc[:, 1024:1028].rearrange("p (k j) -> p k j", k=2)
        gate_hid = misc[:, 2048:2176].rearrange("p (k n) -> p k n", k=2)
        gate_rep = misc[:, 0:1024].rearrange("p (j k n) -> p j k n", j=4, k=2)
        gate_mx = misc[:, 2304:2368]
        T_START, T_OFFC, T_OFFE, T_POS, T_PERM = 0, 20, 40, 64, 84

        cshare_d = scratch("cshare_d", [128, KC, NTP], F32)
        cexp_d = scratch("cexp_d", [128, KC, NTP], F32)
        x1_d = scratch("x1_d", [128, KC, NT], F32)
        src_d = [scratch(f"src{j}_d", [128, KC, NTP], F32) for j in range(4)]
        eout_d = scratch("eout_d", [NE * PER_E, 2 * D], F16)

        s = {n: sem(n) for n in (
            "iotas", "dve", "small_in", "bias_in", "type_oh", "order_mm", "batch_oh", "perm_mm", "pexp",
            "tables", "consts",
            "w_in", "wchain", "w_ready", "x_in0", "x_in1", "x_hi", "x_lo",
            "gw_in", "grep", "ghid_mm", "ghid", "glog_mm", "gsub", "gexp", "gates",
            "exsh_in", "y_mul", "y_sum", "y_hi", "y_lo", "qk_mm", "qk_hi", "qk_lo", "kbd", "kbd_act", "s_mm",
            "mx", "sub", "exp", "norm", "p_ready", "t_mm", "pt_hi", "pt_lo", "pv_mm", "o_hi", "o_lo",
            "v_mm", "v_hi", "v_lo", "wo_mm", "xin_in", "xb", "x1", "x1_hi", "x1_lo", "x1_out",
            "z_in", "zchain", "z_sum", "z_hi", "z_lo", "r_mm", "r_t", "r_hi", "r_lo", "l_mm", "logit",
            "w3_in", "w3",
            "oh", "pos_mm", "ssub", "sexp", "slot_oh", "zt_mm", "zt", "dp_mm", "xe_hi", "xe_lo", "ct_mm", "ct",
            "eb1", "eb2_in", "eb2", "m_mm", "m_t", "m_hi", "m_lo", "m_out", "ev", "eo_hi", "eo_lo", "eo_st0", "eo_st1", "eo_st2", "eo_st3",
            "fin_in0", "fin_in1", "fin_mm", "fin", "fin_st0", "fin_st1")}

        class FfnPass:
            def __init__(self, name, iters, n, gated, dynamic, two_experts, slots, need_w, out_d, feat):
                self.name, self.iters, self.n, self.gated = name, iters, n, gated
                self.dynamic, self.two_experts, self.slots, self.need_w = dynamic, two_experts, slots, need_w
                self.out_d, self.feat = out_d, feat
                self.lead = 2 if gated and n == 512 else 3
                self.l1, self.hi, self.h, self.l2, self.ev, self.feat_done, self.st = (
                    sem(f"{name}_{x}") for x in ("l1", "hi", "hidden", "l2", "evac", "feat", "store"))
                if gated:
                    self.g, self.mul = sem(f"{name}_gelu"), sem(f"{name}_mul")
                self.nev = 2 * iters
                self.nst = iters if two_experts else 2 * iters

            def bank(self, st, gate):
                if self.gated and self.n == 512:
                    return 2 * (st % 2) + gate, 0
                return st % 4, gate * self.n

            def fbuf(self, st):
                u = st % (1024 // self.n)
                return hidden_f32[:, u * self.n:(u + 1) * self.n]

            def gbuf(self, st):
                return gt[:, (st % 2) * 512:(st % 2) * 512 + 512] if self.n == 512 \
                    else gt[:, (st % 4) * 256:(st % 4) * 256 + 256]

        cs = FfnPass("cs", B // 16, 512, True, False, False, C_SHARE, 3, cshare_d, 1)
        ce = FfnPass("ce", NCH // 2, CH, True, True, False, C_EXP, 12, cexp_d, 0)
        es = [FfnPass(f"s{j}", B // 16, 512, False, False, False, E_SHARE[j], 14 + (0, 3, 5)[j], src_d[1 + j], 1 + j)
              for j in range(3)]
        ee = FfnPass("ee", NCH, CH, False, True, True, E_EXP, 27, src_d[0], 0)
        passes = [cs, ce] + es + [ee]

        def before(p):
            return {"ce": cs, "s1": es[0], "s2": es[1], "ee": es[2]}.get(p.name)

        def w16(slot, part, col, width=128):
            lo = slot * SLOT + part * MAT + col
            return arena[:, lo:lo + width]

        SPLIT = ((0, 0), (0, 1), (1, 0))

        y_twice = ex.rearrange("p k (b n) -> p (k b) n", b=GB).unsqueeze(2).to_broadcast([128, KC * GB, 2, S])

        def kbd_head(h):
            return kbd.rearrange("p h m b e n -> p (h m b) e n")[:, :, h, :]
        kh_batches = kh.rearrange("p h k (b n) -> p (h k b) n", b=GB)

        def heads(x):
            return x.rearrange("p (h n) -> p h n", h=H)

        def weighted(engine, buf, b0, nb, j):
            b4 = buf.rearrange("p k (b n) -> p k b n", b=nb)
            g = gates[:, ds(b0, nb), j:j + 1].rearrange("p b j -> p (b j)").unsqueeze(1).unsqueeze(3)
            return engine.tensor_tensor(b4, b4, g.to_broadcast([128, KC, nb, S]), ALU.mult)

        block = ctx.enter_context(nc.Block())

        @block.gpsimd
        def _(pool):
            nc.gpsimd.iota(row[:, :], [[1, 128]], base=0, channel_multiplier=0,
                           allow_small_or_imprecise_dtypes=True).then_inc(s["iotas"], 1)
            nc.gpsimd.iota(pidx[:, :], [[1, 1]], base=0, channel_multiplier=1,
                           allow_small_or_imprecise_dtypes=True).then_inc(s["iotas"], 1)

            loads = [(a["c_swi0"], 0, SW, None), (a["c_swi1"], 1, SW, None), (a["c_swo"], 2, SW, None)]
            for t in range(TYPES):
                loads += [(a[n][t], C_EXP + 3 * t + i, SW, None) for i, n in enumerate(("c_wi0", "c_wi1", "c_wo"))]
            loads += [(a["e_swi"][0], 12, SW, None), (a["e_swo"][0], 13, SW, None)]
            loads += [(a["a_w"], ATTN_W, SA, (cs.l2, 2 * cs.iters))]
            loads += [(a["e_swi"][1], 1, SW, None), (a["e_swo"][1], 2, SW, None)]
            loads += [(a["e_swi"][2], 11, SW, (ce.l2, 2 * ce.iters)), (a["e_swo"][2], 14, SW, None)]
            for e in range(E2):
                loads += [(a["e_wi"][e], E_EXP + 2 * e, SW, (s["x1_out"], 16 * (B // GB)) if e == 0 else None),
                          (a["e_wo"][e], E_EXP + 2 * e + 1, SW, None)]
            loads += [(a["r_w1"], R_W1, SW, None)]
            loads += [(a["r_w2"][0], R_W2[0], SW, (es[0].l2, 2 * es[0].iters)), (a["r_w2"][1], R_W2[1], SW, None)]
            loads += [(a["r_w2"][2], R_W2[2], SW, (es[1].l2, 2 * es[1].iters)), (a["r_w2"][3], R_W2[3], SW, None)]
            loads += [(a["m_w1"][0], MOE_W[0][0], SW, (es[2].l2, 2 * es[2].iters)), (a["m_w2"][0], MOE_W[0][1], SW, None)]
            for e in range(1, NE):
                wait = (s["slot_oh"], 1) if e == 1 else (s["m_out"], 2 * (e - 1))
                loads += [(a["m_w1"][e], MOE_W[e % 2][0], SW, wait), (a["m_w2"][e], MOE_W[e % 2][1], SW, None)]

            def fetch(i):
                pool.dma_start(wstage[:, i % 2, :], loads[i][0]).then_inc(s["w_in"], 16)

            def cut_up(i):
                _, slot, scale, wait = loads[i]
                pool.wait_ge(s["w_in"], 16 * (i + 1))
                if i + 1 < len(loads):
                    if i >= 1:
                        pool.wait_ge(s["w_ready"], i)
                    fetch(i + 1)
                if wait is not None:
                    pool.wait_ge(*wait)
                st = wstage[:, i % 2, :]
                hi, lo = (arena[:, slot * SLOT + h * MAT:slot * SLOT + (h + 1) * MAT] for h in (0, 1))
                nc.gpsimd.tensor_scalar(st, st, scale, None, ALU.mult).then_inc(s["wchain"], 1)
                pool.wait_ge(s["wchain"], 2 * i + 1)
                nc.gpsimd.tensor_copy(hi, st).then_inc(s["wchain"], 1)
                pool.wait_ge(s["wchain"], 2 * i + 2)
                nc.gpsimd.tensor_tensor(lo, st, hi, ALU.subtract).then_inc(s["w_ready"], 1)

            fetch(0)
            for i in range(17):
                cut_up(i)

            def y_make(c):
                pool.wait_ge(s["exsh_in"], c * 32 + 32)
                weighted(nc.gpsimd, ex, c * GB, GB, 0)
                weighted(nc.gpsimd, sh, c * GB, GB, 1).then_inc(s["y_mul"], 1)
                pool.wait_ge(s["y_mul"], c + 1)
                nc.gpsimd.tensor_tensor(ex, ex, sh, ALU.add).then_inc(s["y_sum"], 1)

            def normalise(c, r):
                pool.wait_ge(s["norm"], c * 4 + (2 * r - 2))
                p_ = heads(prob[:, r, :])
                nc.gpsimd.tensor_tensor(p_, p_, rs[:, r, :].unsqueeze(2).to_broadcast([128, H, S]),
                                        ALU.mult).then_inc(s["p_ready"], 1)

            pool.wait_ge(s["gates"], 1)
            y_make(0)
            y_make(1)
            with pool.Fori(1, NA - 1) as c:
                y_make(c + 1)
                normalise(c, 0)
                normalise(c, 1)
            for c in (NA - 1, NA):
                normalise(c, 0)
                normalise(c, 1)

            for i in range(17, len(loads)):
                cut_up(i)

        @block.sync
        def _(sp):
            sp.dma_start(itok_i, a["itok"]).then_inc(s["small_in"], 16)
            sp.dma_start(gate_vec, a["gv"].partition_broadcast(128)).then_inc(s["small_in"], 16)
            sp.dma_start(bias[:, :], a["bias"]).then_inc(s["bias_in"], 16)
            sp.dma_start(rb3, a["rb3"].partition_broadcast(128)).then_inc(s["bias_in"], 16)
            sp.wait_ge(s["tables"], 1)

            def load_x(dst, position):
                b = sp.value_load(tbl[0:1, ds(position + T_PERM, 1)], min_val=0, max_val=B - 1)
                return sp.dma_start(dst, a["x"][ds(b, 1)].rearrange("b p (k n) -> p (b k) n", k=KC))

            def x_group(g, u, fresh=False):
                if not fresh:
                    sp.wait_ge(s["x_lo"], g * 2 + (u - 1))
                    sp.wait_ge(s["tables"], 1)
                for j in range(8):
                    load_x(xf[:, u, :, j * S:(j + 1) * S], g * 16 + (8 * u + j)).then_inc(s[f"x_in{u}"], 16)

            def stores(p):
                def store(i, half, n):
                    if p.dynamic:
                        c = i if p.two_experts else i * 2 + half
                        first = sp.value_load(tbl[0:1, ds(c + T_POS, 1)], min_val=0, max_val=B) * S
                    else:
                        first = (i * 2 + half) * 512
                    sp.wait_ge(p.feat_done, n + 1)
                    sp.dma_start(p.out_d[:, :, ds(first, p.n)], outb[:, :, 0:p.n]).then_inc(p.st, 16)
                if p is cs:
                    x_group(0, 0, True)
                    x_group(0, 1, True)
                    x_group(1, 0)
                    x_group(1, 1)
                    store(0, 0, 0)
                    with sp.Fori(1, p.iters - 1) as i:
                        x_group(i + 1, 0)
                        store(i - 1, 1, i * 2 - 1)
                        x_group(i + 1, 1)
                        store(i, 0, i * 2)
                    store(p.iters - 2, 1, p.iters * 2 - 3)
                    store(p.iters - 1, 0, p.iters * 2 - 2)
                    store(p.iters - 1, 1, p.iters * 2 - 1)
                elif p.two_experts:
                    with sp.Fori(0, p.iters) as i:
                        store(i, 0, i)
                else:
                    with sp.Fori(0, p.iters) as i:
                        store(i, 0, i * 2)
                        store(i, 1, i * 2 + 1)
                sp.wait_ge(p.st, 16 * p.nst)

            stores(cs)
            stores(ce)
            sp.wait_ge(s["x_lo"], 8)
            sp.dma_start(misc[:, 4608:5632], a["c_g0"]).then_inc(s["gw_in"], 16)
            sp.dma_start(misc[:, 1024:1028], a["c_g1"]).then_inc(s["gw_in"], 16)

            def exsh(c):
                sp.dma_start(ex, cexp_d[:, :, ds(c * CH, CH)]).then_inc(s["exsh_in"], 16)
                sp.dma_start(sh, cshare_d[:, :, ds(c * CH, CH)]).then_inc(s["exsh_in"], 16)

            def xin_load(c):
                for j in range(GB):
                    load_x(xin[:, :, j * S:(j + 1) * S], c * GB + j).then_inc(s["xin_in"], 16)

            def x1_store(c):
                sp.wait_ge(s["x1_lo"], c + 1)
                sp.dma_start(x1_d[:, :, ds(c * CH, CH)], x1).then_inc(s["x1_out"], 16)

            exsh(0)
            xin_load(0)
            for c in range(1, 4):
                sp.wait_ge(s["y_lo"], c)
                exsh(c)
            with sp.Fori(2, NA - 2) as c:
                x1_store(c - 2)
                xin_load(c - 1)
                sp.wait_ge(s["y_lo"], c + 2)
                exsh(c + 2)
            for c in range(NA - 2, NA + 2):
                x1_store(c - 2)
                if c - 1 < NA:
                    xin_load(c - 1)

            for p in es + [ee]:
                stores(p)
            sp.wait_ge(s["gates"], 1)
            sp.dma_start(misc[:, 4608:6656], a["e_g1"]).then_inc(s["gw_in"], 16)
            sp.dma_start(misc[:, 1024:1032], a["e_g2"]).then_inc(s["gw_in"], 16)
            sp.dma_start(misc[:, 2560:2624], a["r_w3"]).then_inc(s["w3_in"], 16)

            def z_load(k):
                for j in range(4):
                    sp.dma_start(zsrc[:, j, :, :], src_d[j][:, :, ds(k * CH, CH)]).then_inc(s["z_in"], 16)
            z_load(0)
            with sp.Fori(1, NT // CH) as k:
                sp.wait_ge(s["z_lo"], k)
                z_load(k)

            sp.wait_ge(s["ct"], NP)
            sp.wait_ge(s["xe_hi"], 2 * NP)
            sp.wait_ge(s["xe_lo"], 2 * NP)
            sp.dma_start(misc[:, 4608:6656], a["eb2"].partition_broadcast(128)).then_inc(s["eb2_in"], 16)
            with sp.Fori(0, NE) as e:
                for t in range(5):
                    sp.wait_ge(s["eo_lo"], e * 5 + (t + 1))
                    sp.dma_start(eout_d[ds(e * PER_E + t * 128, 128), :],
                                 eo[:, t % 4, :, :].rearrange("p h n -> p (h n)")).then_inc(s[f"eo_st{t % 4}"], 16)
            with sp.Fori(0, NP // 2) as half_t:
                t = half_t * 2
                for u in range(2):
                    sp.wait_ge(s["fin"], t + (u + 1))
                    sp.wait_ge(s["tables"], 1)
                    for b2 in range(2):
                        b = sp.value_load(tbl[0:1, ds(t * 2 + (2 * u + b2 + T_PERM), 1)], min_val=0, max_val=B - 1)
                        sp.dma_start(a["out"][ds(b, 1)].rearrange("b p (k n) -> p (b k) n", k=KC),
                                     yo[:, u, b2, :, :]).then_inc(s[f"fin_st{u}"], 16)
            for u in range(2):
                sp.wait_ge(s[f"fin_st{u}"], 8 * B)

        @block.tensor
        def _(pe):
            mm = nc.tensor.matmul
            pe.wait_ge(s["type_oh"], 1)
            mm(ps[:, 0, 0:TYPES], ones[0:B, :], type_oh, start=True, stop=True)
            mm(ps[0:B, 1, 0:TYPES], upper[0:B, 0:B], type_oh, start=True, stop=True).then_inc(s["order_mm"], 1)
            pe.wait_ge(s["batch_oh"], 1)
            mm(ps[0:1, 2, 0:B], pidx[0:B, 0:1], batch_oh, start=True, stop=True).then_inc(s["perm_mm"], 1)

            def ffn(p):
                pe.wait_ge(s["w_ready"], p.need_w)
                if p is cs:
                    pe.wait_ge(s["tables"], 1)
                if p is ce:
                    pe.wait_ge(s["consts"], 1)
                if p is es[0]:
                    pe.wait_ge(s["pt_lo"], 4 * NA)
                prev = before(p)
                if prev is not None:
                    pe.wait_ge(prev.ev, prev.nev)

                def at_chunk(i, half):
                    if not p.dynamic:
                        return 0, (i * 2 + half) * 512
                    c = i if p.two_experts else i * 2 + half
                    first = pe.value_load(tbl[0:1, ds(c + T_START, 1)], min_val=0, max_val=NT)
                    off = pe.value_load(tbl[0:1, ds(c + (T_OFFE if p.two_experts else T_OFFC), 1)],
                                        min_val=0, max_val=6 * SLOT)
                    return off, first

                def weight(off, half, matrix, part, col):
                    if not p.dynamic:
                        return w16(p.slots[matrix], part, col)
                    base = (p.slots + matrix + (2 * half if p.two_experts else 0)) * SLOT + part * MAT + col
                    return arena[:, ds(off + base, 128)]

                def first(i, st, place):
                    half, f = divmod(st, FC)
                    off, start = place
                    if p is cs and f == 0:
                        pe.wait_ge(s["x_lo"], i * 2 + (half + 1))
                    if p is es[0] and f == 0:
                        pe.wait_ge(s["x1_lo"], i * 4 + (2 * half + 2))
                    for g in range(2 if p.gated else 1):
                        bank, col = p.bank(st, g)
                        for k in range(KC):
                            for n, (wp, xp) in enumerate(SPLIT):
                                last = mm(ps[:, bank, col:col + p.n], weight(off, half, g, wp, k * F + f * 128),
                                          xh[:, xp, k, ds(start, p.n)],
                                          start=(k == 0 and n == 0), stop=(k == KC - 1 and n == 2))
                    last.then_inc(p.l1, 1)

                def second(i, st, place):
                    half, f = divmod(st, FC)
                    if f == 0 and not (isinstance(i, int) and i == 0):
                        pe.wait_ge(p.ev, i * 2 + (half - 1))
                    if p is es[0] and isinstance(i, int) and i == 0 and st == 0:
                        pe.wait_ge(s["x1"], NA)
                    pe.wait_ge(p.h, i * 16 + (st + 1))
                    for m in range(2):
                        for n, (wp, hp) in enumerate(SPLIT):
                            last = mm(ps[:, 4 + 2 * half + m, 0:p.n],
                                      weight(place[0], half, 2 if p.gated else 1, wp, f * D + m * 128),
                                      hid[:, st % 4, hp, 0:p.n], start=(f == 0 and n == 0),
                                      stop=(f == FC - 1 and n == 2))
                    if f == FC - 1:
                        last.then_inc(p.l2, 1)

                def body(i, lastone):
                    here = at_chunk(i, 0)
                    place = (here, here if p.two_experts else at_chunk(i, 1))
                    ahead = None if lastone else at_chunk(i + 1, 0)
                    for st in range(16):
                        second(i, st, place[st // FC])
                        nxt = st + p.lead
                        if nxt < 16:
                            first(i, nxt, place[nxt // FC])
                        elif not lastone:
                            first(i + 1, nxt - 16, ahead)

                place0 = at_chunk(0, 0)
                for st in range(p.lead):
                    first(0, st, place0)
                body(0, False)
                with pe.Fori(1, p.iters - 1) as i:
                    body(i, False)
                body(p.iters - 1, True)

            def gate(kc_in, n_out, turn, p_last):
                pe.wait_ge(s["gw_in"], 32 * turn)
                pe.wait_ge(p_last.feat_done, p_last.nst)
                pe.wait_ge(p_last.ev, p_last.nev)
                for m in range(2):
                    for k in range(kc_in):
                        last = mm(ps[:, m, 0:B], gate_w1[:, k, m * 128:(m + 1) * 128], gate_in[:, k // KC, k % KC, 0:B],
                                  start=(k == 0), stop=(k == kc_in - 1))
                last.then_inc(s["ghid_mm"], 1)
                pe.wait_ge(s["grep"], turn)
                pe.wait_ge(s["ghid"], turn)
                for j in range(n_out):
                    for k in range(2):
                        last = mm(ps[:, 2, j * B:(j + 1) * B], gate_rep[:, j, k, :], gate_hid[:, k, :],
                                  start=(k == 0), stop=(k == 1))
                last.then_inc(s["glog_mm"], 1)

            ffn(cs)
            ffn(ce)
            gate(4, 2, 1, ce)

            def wide_products(dst, w, m, data):
                for k in range(KC):
                    for j, (wp, xp) in enumerate(SPLIT):
                        last = mm(dst, w16(ATTN_W, wp, (w * KC + k) * D + m * 128), data(xp, k),
                                  start=(k == 0 and j == 0), stop=(k == KC - 1 and j == 2))
                return last

            def attn(c, new, old):
                if new:
                    pe.wait_ge(s["y_lo"], c + 1)
                    for w in range(2):
                        if w == 1 and (not isinstance(c, int) or c >= 2):
                            pe.wait_ge(s["x1"], c - 1)
                        for m in range(2):
                            last = wide_products(ps[:, 4 + w, m * CH:(m + 1) * CH], w, m,
                                                 lambda xp, k: yd[:, xp, k, :, 0, :])
                        last.then_inc(s["qk_mm"], 1)
                    if old:
                        pe.wait_ge(s["v_lo"], c)
                    for b in range(GB):
                        for k in range(KC):
                            for j, (yp, wp) in enumerate(SPLIT):
                                last = mm(ps[:, 6 + b // 2, (b % 2) * D:(b % 2 + 1) * D],
                                          yd[:, yp, k, b, :, :].rearrange("p r n -> p (r n)"),
                                          w16(ATTN_W, wp, (2 * KC + k) * D, D),
                                          start=(k == 0 and j == 0), stop=(k == KC - 1 and j == 2))
                    last.then_inc(s["v_mm"], 1)
                if old:
                    for r in range(2):
                        pe.wait_ge(s["p_ready"], c * 2 + (r - 1))
                        for hb in range(2):
                            for q in range(4):
                                hp = hb * 4 + q
                                last = nc.tensor.transpose(ps[:, 2 * r + hb, q * 128:(q + 1) * 128],
                                                           prob[:, r, hp * 128:(hp + 1) * 128], ident[:, :])
                            last.then_inc(s["t_mm"], 1)
                    if new:
                        pe.wait_ge(s["qk_lo"], c * 2 + 1)
                    else:
                        pe.wait_ge(s["v_lo"], c)
                    for b in range(GB):
                        r, b2 = divmod(b, 2)
                        if b2 == 0:
                            pe.wait_ge(s["pt_lo"], c * 4 + (2 * r - 2))
                        for hp in range(8):
                            o, n0 = 32 * (hp % 4), (hp // 4) * CH + b * S
                            for j, (vp, pp) in enumerate(SPLIT):
                                col = hp * 128 + b2 * S
                                last = mm(ps[o:o + 32, 4, n0:n0 + S], vbd[:, vp, b, hp * 32:(hp + 1) * 32],
                                          pt[:, r, pp, col:col + S], start=(j == 0), stop=(j == 2))
                    last.then_inc(s["pv_mm"], 1)
                if new:
                    pe.wait_ge(s["kbd"], c + 1)
                    pe.wait_ge(s["kbd_act"], c + 1)
                    for r in range(2):
                        for m in range(2):
                            for b2 in range(2):
                                b = 2 * r + b2
                                for j, (kp, qp) in enumerate(SPLIT):
                                    mm(ps[b2 * 64:b2 * 64 + 64, 2 * r + m, :], qh[:, qp, m, b * S:(b + 1) * S],
                                       kbd[:, kp, m, b, :, :].rearrange("p h n -> p (h n)"),
                                       start=(j == 0), stop=False, skip_group_check=True)
                            last = mm(ps[:, 2 * r + m, :], identb[:, :], causal[:, :, :].rearrange("p h n -> p (h n)"),
                                      start=False, stop=True, skip_group_check=True)
                        last.then_inc(s["s_mm"], 1)
                if old:
                    pe.wait_ge(s["o_lo"], c)
                    if new:
                        pe.wait_ge(s["qk_lo"], c * 2 + 2)
                    else:
                        pe.wait_ge(s["x1"], c - 1)
                    for m in range(2):
                        last = wide_products(ps[:, 5, m * CH:(m + 1) * CH], 3, m, lambda xp, k: oh_[:, xp, k, :])
                    last.then_inc(s["wo_mm"], 1)

            pe.wait_ge(s["w_ready"], 15)
            attn(0, True, False)
            attn(1, True, True)
            with pe.Fori(2, NA) as c:
                attn(c, True, True)
            attn(NA, False, True)

            for p in es:
                ffn(p)
            ffn(ee)
            gate(8, 4, 2, ee)

            def router_in(c, f):
                if f >= 4:
                    pe.wait_ge(s["r_lo"], c * 16 + (f - 3))
                for k in range(KC):
                    for n, (wp, xp) in enumerate(SPLIT):
                        last = mm(ps[:, f % 4, :], w16(R_W1, wp, k * F + f * 128), xh[:, xp, k, ds(c * 512, 512)],
                                  start=(k == 0 and n == 0), stop=(k == KC - 1 and n == 2))
                last.then_inc(s["r_mm"], 1)

            def router_mid(c, fo):
                if fo >= 2:
                    pe.wait_ge(s["r_lo"], c * 16 + (8 + fo - 1))
                for k in range(FC):
                    if fo == 0:
                        pe.wait_ge(s["r_lo"], c * 16 + (k + 1))
                    for n, (wp, xp) in enumerate(SPLIT):
                        last = mm(ps[:, 4 + fo % 2, :], w16(R_W2[k // 2], wp, (k % 2) * F + fo * 128), h1[:, k, xp, :],
                                  start=(k == 0 and n == 0), stop=(k == FC - 1 and n == 2))
                last.then_inc(s["r_mm"], 1)

            def router_out(c):
                pe.wait_ge(s["r_lo"], c * 16 + 16)
                if not isinstance(c, int) or c > 0:
                    pe.wait_ge(s["logit"], c)
                for t in range(4):
                    for fo in range(FC):
                        for n, (wp, xp) in enumerate(SPLIT):
                            last = mm(ps[:, 6, t * NE:(t + 1) * NE], h2[:, fo, xp, t * 128:(t + 1) * 128],
                                      w3[:, wp, fo, :], start=(fo == 0 and n == 0), stop=(fo == FC - 1 and n == 2))
                last.then_inc(s["l_mm"], 1)

            def router(c, previous):
                pe.wait_ge(s["z_lo"], c * 2 + 2)
                for f in range(FC):
                    router_in(c, f)
                if previous:
                    router_out(c - 1)
                for fo in range(FC):
                    router_mid(c, fo)

            pe.wait_ge(s["w_ready"], 32)
            pe.wait_ge(s["w3"], 1)
            pe.wait_ge(s["gates"], 2)
            router(0, False)
            with pe.Fori(1, 8) as c:
                router(c, True)
            router_out(7)

            pe.wait_ge(s["oh"], 1)
            mm(ps[:, 0, 0:NP * NE], upperb[:, :], oh16.rearrange("p t e -> p (t e)"), start=True,
               stop=True).then_inc(s["pos_mm"], 1)

            pe.wait_ge(s["slot_oh"], 1)

            def dispatch(t, u, fresh):
                if not fresh:
                    pe.wait_ge(s["zt"], t + (u - 1))
                for h in range(2):
                    for k in range(KC):
                        c0 = (h * KC + k) * 128
                        last = nc.tensor.transpose(zt_ps[u][:, c0:c0 + 128], xh[:, h, k, ds((t + u) * 128, 128)],
                                                   ident16[:, :])
                last.then_inc(s["zt_mm"], 1)
                if not fresh:
                    pe.wait_ge(s["ct"], t + (u - 1))
                for h in range(2):
                    last = nc.tensor.transpose(ct_ps[u][:, h * 128:(h + 1) * 128],
                                               dsc[:, h, ds(t + u, 1), :].rearrange("p t s -> p (t s)"), ident16[:, :])
                last.then_inc(s["ct_mm"], 1)
                if not fresh:
                    pe.wait_ge(s["xe_hi"], t * 2 + (2 * u - 2))
                    pe.wait_ge(s["xe_lo"], t * 2 + (2 * u - 2))
                pe.wait_ge(s["zt"], t + (u + 1))
                for h in range(2):
                    for k in range(KC):
                        last = mm(ps[:, 2 + 2 * u + h, k * 2 * SLOTS:(k + 1) * 2 * SLOTS], ztok[:, u, h, k, :],
                                  d01[:, ds(t + u, 1), :, :].rearrange("p t b s -> p (t b s)"), start=True, stop=True)
                last.then_inc(s["dp_mm"], 1)
            dispatch(0, 0, True)
            dispatch(0, 1, True)
            with pe.Fori(1, NP // 2) as half_t:
                t = half_t * 2
                dispatch(t, 0, False)
                dispatch(t, 1, False)

            pe.wait_ge(s["xe_hi"], 2 * NP)
            pe.wait_ge(s["xe_lo"], 2 * NP)
            pe.wait_ge(s["ct"], NP)

            def expert_in(e, par, st):
                half, f = divmod(st, FC)
                n, c0 = len(TILES[half]) * 128, TILES[half][0] * 128
                if st == 0:
                    pe.wait_ge(s["w_ready"], e * 2 + 34)
                for k in range(KC):
                    for j, (wp, xp) in enumerate(SPLIT):
                        last = mm(ps[:, st % 2, 0:n], w16(MOE_W[par][0], wp, k * F + f * 128),
                                  xe[:, xp, k, ds(e * PER_E + c0, n)],
                                  start=(k == 0 and j == 0), stop=(k == KC - 1 and j == 2))
                last.then_inc(s["m_mm"], 1)

            def expert_out(e, par, st):
                half, f = divmod(st, FC)
                if f == 0 and not (isinstance(e, int) and e == 0):
                    pe.wait_ge(s["ev"], e * 5 + (-2 if half == 0 else 0))
                pe.wait_ge(s["m_lo"], e * 16 + (st + 1))
                for i_t, t in enumerate(TILES[half]):
                    for j, (hp, wp) in enumerate(SPLIT):
                        last = mm(ps[:, 3 + t, 0:D], hid[:, st % 4, hp, i_t * 128:(i_t + 1) * 128],
                                  w16(MOE_W[par][1], wp, f * D, D), start=(f == 0 and j == 0),
                                  stop=(f == FC - 1 and j == 2))
                if f == FC - 1:
                    last.then_inc(s["m_out"], 1)

            def expert(e, par, lastone=False):
                for st in range(16):
                    expert_out(e, par, st)
                    if st + 2 < 16:
                        expert_in(e, par, st + 2)
                    elif not lastone:
                        expert_in(e + 1, 1 - par, st - 14)
            expert_in(0, 0, 0)
            expert_in(0, 0, 1)
            expert(0, 0)
            expert(1, 1)
            with pe.Fori(1, NE // 2 - 1) as half_e:
                e = half_e * 2
                expert(e, 0)
                expert(e + 1, 1)
            expert(NE - 2, 0)
            expert(NE - 1, 1, True)

            pe.wait_ge(s["ev"], 5 * NE)

            def combine(t, u, fresh):
                pe.wait_ge(s[f"fin_in{u}"], t * 24 + 48)
                if not fresh:
                    pe.wait_ge(s["fin"], t + (u - 1))
                for b2 in range(2):
                    for m in range(2):
                        for j, (ep, cp) in enumerate(SPLIT):
                            last = mm(ps[:, u, (b2 * KC + m) * S:(b2 * KC + m + 1) * S],
                                      ebf[0:SLOTS, u, b2, ep, m * 128:(m + 1) * 128],
                                      ct[0:SLOTS, cp, ds(t + u, 1), b2 * S:(b2 + 1) * S].rearrange("p t n -> p (t n)"),
                                      start=(j == 0), stop=(j == 2))
                last.then_inc(s["fin_mm"], 1)
            combine(0, 0, True)
            combine(0, 1, True)
            with pe.Fori(1, NP // 2) as half_t:
                t = half_t * 2
                combine(t, 0, False)
                combine(t, 1, False)

        @block.scalar
        def _(act):
            fn = nc.scalar.activation
            act.wait_ge(s["ssub"], 1)
            fn(gate_vec, gate_vec, ACT.Exp, scale=10.0).then_inc(s["pexp"], 1)

            def x_group(g, u):
                act.wait_ge(s[f"x_in{u}"], (g - u) * 64 + 128)
                act.wait_ge(s["tables"], 1)
                fn(xh[:, 0, :, ds(g * 512, 512)], xf[:, u, :, :], ACT.Copy, scale=SX).then_inc(s["x_hi"], 1)
            x_group(0, 0)
            x_group(1, 1)

            def ffn(p):
                def hidden(i, st):
                    act.wait_ge(p.l1, i * 16 + (st + 1))
                    bank, col = p.bank(st, 0)
                    if p.gated:
                        fn(p.gbuf(st), ps[:, bank, col:col + p.n], ACT.Gelu_apprx_tanh, scale=1 / SH).then_inc(p.g, 1)
                        act.wait_ge(p.mul, i * 16 + (st + 1))
                        fn(hid[:, st % 4, 0, 0:p.n], p.fbuf(st), ACT.Copy).then_inc(p.hi, 1)
                    else:
                        fn(hid[:, st % 4, 0, 0:p.n], ps[:, bank, col:col + p.n], ACT.Relu).then_inc(p.hi, 1)

                def evacuate(i, half):
                    act.wait_ge(p.l2, i * 2 + (half + 1))
                    if half == 0 and isinstance(i, int) and i == 0 and before(p) is not None:
                        act.wait_ge(before(p).st, 16 * before(p).nst)
                    if p.two_experts:
                        if half == 0:
                            if not (isinstance(i, int) and i == 0):
                                act.wait_ge(p.st, i * 16)
                            act.wait_ge(s["consts"], 1)
                            fn(outb[:, :, 0:p.n], ps[:, 4:6, 0:p.n], ACT.Copy,
                               scale=wab[:, 0, ds(i, 1)]).then_inc(p.ev, 1)
                        return
                    if not (isinstance(i, int) and i == 0 and half == 0):
                        act.wait_ge(p.st, i * 32 + 16 * half)
                    fn(outb[:, :, 0:p.n], ps[:, 4 + 2 * half:6 + 2 * half, 0:p.n], ACT.Copy,
                       scale=1 / SO).then_inc(p.ev, 1)

                def body(i, first, lastone):
                    for st in range(16):
                        hidden(i, st)
                        if st == 1 and not first:
                            evacuate(i - 1, 1)
                        if st == 9:
                            evacuate(i, 0)
                        if p is cs and not lastone and st in (3, 11):
                            x_group(i * 2 + (2 if st == 3 else 3), 0 if st == 3 else 1)
                body(0, True, False)
                with act.Fori(1, p.iters - 1) as i:
                    body(i, False, False)
                body(p.iters - 1, False, True)
                evacuate(p.iters - 1, 1)

            def gate(turn):
                act.wait_ge(s["gsub"], turn)
                fn(gates[:, :, 0:2 * turn], gates[:, :, 0:2 * turn], ACT.Exp).then_inc(s["gexp"], 1)

            ffn(cs)
            ffn(ce)
            gate(1)

            def y_parts(c):
                act.wait_ge(s["y_sum"], c + 1)
                if not isinstance(c, int) or c > 0:
                    act.wait_ge(s["v_mm"], c)
                fn(yd[:, 0, :, :, :, :].rearrange("p k b r n -> p (k b) r n"), y_twice, ACT.Copy,
                   scale=SY).then_inc(s["y_hi"], 1)

            def attn(c, new, old, fin, more):
                if old:
                    for r in range(2):
                        act.wait_ge(s["sub"], c * 2 + (r - 1))
                        fn(prob[:, r, :], prob[:, r, :], ACT.Exp, scale=0.25 / (SQ * SQ)).then_inc(s["exp"], 1)
                if fin:
                    act.wait_ge(s["x1"], c - 1)
                    act.wait_ge(ce.l2, 2 * ce.iters)
                    fn(xh[:, 0, :, ds((c - 2) * CH, CH)], x1, ACT.Copy, scale=SX).then_inc(s["x1_hi"], 1)
                if new:
                    for w, dst in enumerate((qh, kh)):
                        act.wait_ge(s["qk_mm"], c * 2 + (w + 1))
                        for m in range(KC):
                            last = fn(dst[:, 0, m, :], ps[:, 4 + w, m * CH:(m + 1) * CH], ACT.Identity,
                                      bias=ab[:, w, m:m + 1])
                        last.then_inc(s["qk_hi"], 1)
                    act.wait_ge(s["qk_lo"], c * 2 + 2)
                    for h in range(KBD_DVE, 8):
                        last = fn(kbd_head(h), kh_batches, ACT.Copy, scale=head_mask[:, h:h + 1])
                    last.then_inc(s["kbd_act"], 1)
                if more:
                    y_parts(c + 1)
                if old:
                    for r in range(2):
                        for hb in range(2):
                            act.wait_ge(s["t_mm"], c * 4 + (2 * r + hb - 3))
                            fn(pt[:, r, 0, hb * 512:(hb + 1) * 512], ps[:, 2 * r + hb, :], ACT.Copy
                               ).then_inc(s["pt_hi"], 1)
                    act.wait_ge(s["pv_mm"], c)
                    for m in range(KC):
                        last = fn(oh_[:, 0, m, :], ps[:, 4, m * CH:(m + 1) * CH], ACT.Identity, bias=ab[:, 2, m:m + 1])
                    last.then_inc(s["o_hi"], 1)
                if new:
                    act.wait_ge(s["v_mm"], c + 1)
                    for r in range(2):
                        for j in range(2):
                            last = fn(vb(0, r, j), vp(r, j), ACT.Copy, scale=half_mask[:, j:j + 1])
                    last.then_inc(s["v_hi"], 1)
                if old:
                    act.wait_ge(s["xin_in"], c * 64)
                    for k in range(KC):
                        last = fn(xin[:, k, :], xin[:, k, :], ACT.Identity, bias=ab[:, 3, k:k + 1])
                    last.then_inc(s["xb"], 1)

            y_parts(0)
            attn(0, True, False, False, True)
            attn(1, True, True, False, True)
            with act.Fori(2, NA - 1) as c:
                attn(c, True, True, True, True)
            attn(NA - 1, True, True, True, False)
            attn(NA, False, True, True, False)
            attn(NA + 1, False, False, True, False)

            for p in es:
                ffn(p)
            ffn(ee)
            gate(2)

            def z_parts(k):
                act.wait_ge(s["z_sum"], k + 1)
                act.wait_ge(ee.l2, 2 * ee.iters)
                fn(xh[:, 0, :, ds(k * CH, CH)], zsrc[:, 0, :, :], ACT.Copy, scale=SZ).then_inc(s["z_hi"], 1)

            def rhidden(c, st, fresh):
                act.wait_ge(s["r_mm"], c * 16 + (st + 1))
                if st < FC:
                    src, dst, b_, scale = ps[:, st % 4, :], h1[:, st, 0, :], rb1[:, st:st + 1], 1.0
                else:
                    fo = st - FC
                    src, dst, b_, scale = ps[:, 4 + fo % 2, :], h2[:, fo, 0, :], rb2[:, fo:fo + 1], 1 / SW
                if not (fresh and st < 2):
                    act.wait_ge(s["r_lo"], c * 16 + (st - 1))
                fn(gt[:, (st % 2) * 512:(st % 2 + 1) * 512], src, ACT.Relu, bias=b_, scale=scale)
                fn(dst, src, ACT.Relu, bias=b_, scale=scale).then_inc(s["r_hi"], 1)

            def router(c, fresh, more):
                for st in range(16):
                    rhidden(c, st, fresh)
                    if more and st in (8, 11):
                        z_parts(c * 2 + (2 if st == 8 else 3))
            z_parts(0)
            z_parts(1)
            router(0, True, True)
            with act.Fori(1, 7) as c:
                router(c, False, True)
            router(7, False, False)

            act.wait_ge(s["ssub"], 2)
            fn(score, score, ACT.Exp).then_inc(s["sexp"], 1)

            def dispatch(t, u):
                act.wait_ge(s["ct_mm"], t + (u + 1))
                act.wait_ge(s["slot_oh"], 1)
                fn(ct[0:SLOTS, :, ds(t + u, 1), :].rearrange("p h t n -> p (h t) n"),
                   ct_ps[u].rearrange("p (h n) -> p h n", h=2), ACT.Copy).then_inc(s["ct"], 1)
                act.wait_ge(s["dp_mm"], t + (u + 1))
                act.wait_ge(s["slot_oh"], 1)
                for k in range(KC):
                    fn(xe_pair(0, k, t, u), dp(u, 0, k), ACT.Copy).then_inc(s["xe_hi"], 1)
            with act.Fori(0, NP // 2) as half_t:
                t = half_t * 2
                dispatch(t, 0)
                dispatch(t, 1)

            def ehidden(e, st):
                half, f = divmod(st, FC)
                n = len(TILES[half]) * 128
                act.wait_ge(s["m_mm"], e * 16 + (st + 1))
                b_ = eb1_now[:, f:f + 1]
                fn(gt[:, (st % 2) * 512:(st % 2) * 512 + n], ps[:, st % 2, 0:n], ACT.Relu, bias=b_)
                fn(hid[:, st % 4, 0, 0:n], ps[:, st % 2, 0:n], ACT.Relu, bias=b_).then_inc(s["m_hi"], 1)

            def eout(e, half):
                for t in TILES[half]:
                    act.wait_ge(s["ev"], e * 5 + (t + 1))
                    if t == 4:
                        act.wait_ge(s["eo_st0"], e * 32 + 16)
                    elif not (isinstance(e, int) and e == 0):
                        act.wait_ge(s[f"eo_st{t}"], e * (32 if t == 0 else 16))
                    fn(eo[:, t % 4, 0, :], ev[:, t % 2, :], ACT.Copy).then_inc(s["eo_hi"], 1)

            def expert(e, fresh=False):
                if not fresh:
                    act.wait_ge(s["m_hi"], e * 16)
                act.wait_ge(s["consts"], 1)
                fn(eb1_now, eb1[:, ds(e * FC, FC)], ACT.Copy).then_inc(s["eb1"], 1)
                act.wait_ge(s["eb1"], e + 1)
                for st in range(16):
                    ehidden(e, st)
                    if st == 1 and not fresh:
                        eout(e - 1, 1)
                    if st == 9:
                        eout(e, 0)
            expert(0, True)
            with act.Fori(1, NE) as e:
                expert(e)
            eout(NE - 1, 1)

            for t in range(4):
                act.wait_ge(s[f"eo_st{t}"], 16 * NE * (2 if t == 0 else 1))
            by_batch = eout_d.rearrange("(e b n) c -> b e n c", e=NE, b=B)

            def fin_load(t, u):
                for b2 in range(2):
                    act.dma_start(ebf[0:SLOTS, u, b2, :, :].rearrange("p h n -> p (h n)"),
                                  by_batch[ds(t * 2 + (2 * u + b2), 1)].rearrange("b e n c -> (b e) n c")
                                  ).then_inc(s[f"fin_in{u}"], 16)
                act.dma_start(x1f[:, u, :, :], x1_d[:, :, ds((t + u) * 128, 128)]).then_inc(s[f"fin_in{u}"], 16)
            fin_load(0, 0)
            fin_load(0, 1)
            with act.Fori(1, NP // 2) as half_t:
                t = half_t * 2
                for u in range(2):
                    act.wait_ge(s["fin"], t + (u - 1))
                    fin_load(t, u)

        @block.vector
        def _(dve):
            v = nc.vector
            links = [0]

            def link(ins):
                ins.then_inc(s["dve"], 1)
                links[0] += 1
                dve.wait_ge(s["dve"], links[0])

            dve.wait_ge(s["iotas"], 2)
            v.memset(ones, 1.0)
            link(v.tensor_scalar(upper[:, :], row[:, :], pidx[:, 0:1], None, ALU.is_gt))
            dve.wait_ge(s["small_in"], 32)
            link(v.tensor_copy(itok_f, itok_i))
            v.tensor_scalar(type_oh, row[0:B, 0:TYPES], itok_f, None, ALU.is_equal).then_inc(s["type_oh"], 1)
            gv = gate_vec.rearrange("p (t e) -> p t e", t=TYPES)
            link(v.reduce_max(gsum, gv, AX.X))
            v.tensor_tensor(gv, gv, gsum.unsqueeze(2).to_broadcast([128, TYPES, E2]), ALU.subtract).then_inc(s["ssub"], 1)
            dve.wait_ge(s["order_mm"], 1)
            v.memset(starts[:, 0:1], 0.0)
            link(v.tensor_copy(cnt, ps[:, 0, 0:TYPES]))
            v.tensor_copy(starts[:, 1:2], cnt[:, 0:1])
            link(v.tensor_tensor(starts[:, 2:3], cnt[:, 0:1], cnt[:, 1:2], ALU.add))
            link(v.tensor_tensor(tmp3[0:B, :], ps[0:B, 1, 0:TYPES], starts[0:B, :], ALU.add))
            link(v.tensor_tensor(tmp3[0:B, :], tmp3[0:B, :], type_oh, ALU.mult))
            link(v.reduce_sum(rank, tmp3[0:B, :], AX.X))
            v.tensor_scalar(batch_oh, row[0:B, 0:B], rank, None, ALU.is_equal).then_inc(s["batch_oh"], 1)
            lt = scr[:, 0:3 * 16].rearrange("p (t j) -> p t j", t=TYPES)
            link(v.tensor_scalar(scr[:, 64:80], row[:, 0:16], float(GB), None, ALU.mult))
            link(v.tensor_tensor(lt, scr[:, 64:80].unsqueeze(1).to_broadcast([128, TYPES, 16]),
                                 cnt.unsqueeze(2).to_broadcast([128, TYPES, 16]), ALU.is_lt))
            link(v.reduce_sum(nchunks, lt, AX.X))
            link(v.tensor_tensor(nchunks[:, 1:2], nchunks[:, 0:1], nchunks[:, 1:2], ALU.add))
            p0, p1, start, typ, t_ = (scr[:, 96 + 20 * j:116 + 20 * j] for j in range(5))
            v.tensor_scalar(p0, row[:, 0:20], nchunks[:, 0:1], None, ALU.is_ge)
            link(v.tensor_scalar(p1, row[:, 0:20], nchunks[:, 1:2], None, ALU.is_ge))
            link(v.tensor_tensor(typ, p0, p1, ALU.add))
            link(v.tensor_scalar(scr[:, 200:202], nchunks[:, 0:2], -float(GB), None, ALU.mult))
            link(v.tensor_tensor(scr[:, 200:202], scr[:, 200:202], starts[:, 1:3], ALU.add))
            link(v.tensor_tensor(scr[:, 201:202], scr[:, 201:202], scr[:, 200:201], ALU.subtract))
            link(v.tensor_scalar(start, row[:, 0:20], float(GB), None, ALU.mult))
            link(v.tensor_scalar(t_, p0, scr[:, 200:201], None, ALU.mult))
            link(v.tensor_tensor(start, start, t_, ALU.add))
            link(v.tensor_scalar(t_, p1, scr[:, 201:202], None, ALU.mult))
            link(v.tensor_tensor(start, start, t_, ALU.add))
            link(v.tensor_scalar(start, start, float(B), None, ALU.min))
            v.tensor_copy(tbl[:, T_POS:T_POS + 20], start)
            v.tensor_scalar(tbl[:, T_START:T_START + 20], start, float(S), None, ALU.mult)
            v.tensor_scalar(tbl[:, T_OFFC:T_OFFC + 20], typ, float(3 * SLOT), None, ALU.mult)
            v.tensor_scalar(tbl[:, T_OFFE:T_OFFE + 20], typ, float(2 * SLOT), None, ALU.mult)
            dve.wait_ge(s["perm_mm"], 1)
            v.tensor_copy(tbl[0:1, T_PERM:T_PERM + B], ps[0:1, 2, 0:B]).then_inc(s["tables"], 1)

            def x_group(g, u):
                dve.wait_ge(s["x_hi"], g + 1)
                v.scalar_tensor_tensor(xh[:, 1, :, ds(g * 512, 512)], xf[:, u, :, :], SX, xh[:, 0, :, ds(g * 512, 512)],
                                       ALU.mult, ALU.subtract).then_inc(s["x_lo"], 1)
            x_group(0, 0)
            x_group(1, 1)

            dve.wait_ge(s["pexp"], 1)
            link(v.reduce_sum(gsum, gv, AX.X))
            link(v.reciprocal(gsum, gsum))
            link(v.tensor_scalar(gsum, gsum, 1 / SO, None, ALU.mult))
            link(v.tensor_tensor(gv, gv, gsum.unsqueeze(2).to_broadcast([128, TYPES, E2]), ALU.mult))
            for e in range(2):
                link(v.tensor_scalar(t_, p0, -1.0, 1.0, ALU.mult, ALU.add))
                link(v.tensor_scalar(wab[:, e, :], t_, gv[:, 0, e:e + 1], None, ALU.mult))
                link(v.tensor_tensor(t_, p0, p1, ALU.subtract))
                link(v.scalar_tensor_tensor(wab[:, e, :], t_, gv[:, 1, 1 + e:2 + e], wab[:, e, :], ALU.mult, ALU.add))
                link(v.scalar_tensor_tensor(wab[:, e, :], p1, gv[:, 2, 2 + e:3 + e], wab[:, e, :], ALU.mult, ALU.add))

            v.memset(xh[:, :, :, NT:NTP], 0.0)
            link(v.tensor_scalar(ident[:, :], row[:, :], pidx[:, 0:1], None, ALU.is_equal))
            v.tensor_copy(ident16[:, :], ident[:, :])
            v.tensor_copy(identb[:, :], ident[:, :])
            link(v.tensor_copy(upperb[:, :], upper[:, :]))
            v.memset(upperb[0:64, 64:128], 0.0)
            link(v.tensor_scalar(half_mask[:, 1:2], pidx[:, 0:1], 64.0, None, ALU.is_ge))
            v.tensor_scalar(half_mask[:, 0:1], half_mask[:, 1:2], -1.0, 1.0, ALU.mult, ALU.add)
            link(v.scalar_tensor_tensor(gsum[:, 0:1], half_mask[:, 1:2], -64.0, pidx[:, 0:1], ALU.mult, ALU.add))
            link(v.tensor_scalar(scr[:, 0:64], row[:, 0:64], gsum[:, 0:1], MASKED, ALU.is_gt, ALU.mult))
            v.tensor_copy(causal[:, :, :], scr[:, 0:64].unsqueeze(1).to_broadcast([128, 8, S]))
            link(v.tensor_scalar(t_[:, 0:8], row[:, 0:8], float(HD), pidx[:, 0:1], ALU.mult, ALU.subtract))
            v.tensor_scalar(typ[:, 0:8], t_[:, 0:8], -float(HD), None, ALU.is_gt)
            link(v.tensor_scalar(t_[:, 0:8], t_[:, 0:8], 0.0, None, ALU.is_le))
            v.tensor_tensor(head_mask[:, :], t_[:, 0:8], typ[:, 0:8], ALU.mult)
            dve.wait_ge(s["bias_in"], 32)
            v.tensor_scalar(bias[:, 0:6], bias[:, 0:6], SQ, None, ALU.mult)
            v.tensor_scalar(bias[:, 8:88], bias[:, 8:88], SR, None, ALU.mult).then_inc(s["consts"], 1)

            def ffn(p):
                def hidden(i, st):
                    bank, col = p.bank(st, 1 if p.gated else 0)
                    src, n = ps[:, bank, col:col + p.n], i * 16 + (st + 1)
                    if p.gated:
                        dve.wait_ge(p.g, n)
                        v.tensor_tensor(p.fbuf(st), src, p.gbuf(st), ALU.mult).then_inc(p.mul, 1)
                        dve.wait_ge(p.hi, n)
                        v.tensor_tensor(hid[:, st % 4, 1, 0:p.n], p.fbuf(st), hid[:, st % 4, 0, 0:p.n],
                                        ALU.subtract).then_inc(p.h, 1)
                    else:
                        dve.wait_ge(p.hi, n)
                        v.scalar_tensor_tensor(hid[:, st % 4, 1, 0:p.n], src, 0.0, hid[:, st % 4, 0, 0:p.n],
                                               ALU.max, ALU.subtract).then_inc(p.h, 1)

                def evacuate(i, half):
                    if p.two_experts:
                        if half == 0:
                            return
                        dve.wait_ge(p.l2, i * 2 + 2)
                        dve.wait_ge(p.ev, i * 2 + 1)
                        v.scalar_tensor_tensor(outb[:, :, 0:p.n], ps[:, 6:8, 0:p.n], wab[:, 1, ds(i, 1)],
                                               outb[:, :, 0:p.n], ALU.mult, ALU.add).then_inc(p.ev, 1)
                        dve.wait_ge(p.ev, i * 2 + 2)
                    else:
                        dve.wait_ge(p.ev, i * 2 + (half + 1))
                    nb = p.n // S
                    if p.dynamic:
                        c = i if p.two_experts else i * 2 + half
                        b0 = dve.value_load(tbl[0:1, ds(c + T_POS, 1)], min_val=0, max_val=B)
                    else:
                        b0 = (i * 2 + half) * nb
                    v.tensor_copy(gate_in[:, p.feat, :, ds(b0, nb)], outb[:, :, 0:p.n:S]).then_inc(p.feat_done, 1)

                def body(i, first, lastone):
                    for st in range(16):
                        hidden(i, st)
                        if st == 1 and not first:
                            evacuate(i - 1, 1)
                        if st == 9:
                            evacuate(i, 0)
                        if p is cs and not lastone and st in (3, 11):
                            x_group(i * 2 + (2 if st == 3 else 3), 0 if st == 3 else 1)
                body(0, True, False)
                with dve.Fori(1, p.iters - 1) as i:
                    body(i, False, False)
                body(p.iters - 1, False, True)
                evacuate(p.iters - 1, 1)

            def gate(n_out, turn):
                dve.wait_ge(s["gw_in"], 32 * turn)
                for j in range(n_out):
                    last = v.tensor_copy(gate_rep[:, j, :, :], (gate_w2 if turn == 2 else gate_w2c)[:, :, j:j + 1]
                                         .to_broadcast([128, 2, 128]))
                last.then_inc(s["grep"], 1)
                dve.wait_ge(s["ghid_mm"], turn)
                v.tensor_scalar(gate_hid, ps[:, 0:2, 0:B], 0.0, None, ALU.max).then_inc(s["ghid"], 1)
                dve.wait_ge(s["glog_mm"], turn)
                logits = ps[:, 2, 0:n_out * B].rearrange("p (j b) -> p b j", j=n_out)
                g = gates[:, :, 0:n_out]
                over_j = gate_mx.unsqueeze(2).to_broadcast([128, B, n_out])
                link(v.reduce_max(gate_mx, logits, AX.X))
                v.tensor_tensor(g, logits, over_j, ALU.subtract).then_inc(s["gsub"], 1)
                dve.wait_ge(s["gexp"], turn)
                link(v.reduce_sum(gate_mx, g, AX.X))
                link(v.reciprocal(gate_mx, gate_mx))
                link(v.tensor_tensor(g, g, over_j, ALU.mult))
                dve.sem_inc(s["gates"], 1)

            ffn(cs)
            ffn(ce)
            gate(2, 1)

            def y_low(c):
                dve.wait_ge(s["y_hi"], c + 1)
                two = yd[:, :, :, :, :, :].rearrange("p h k b r n -> p h (k b) r n")
                for twice in range(2):
                    last = v.scalar_tensor_tensor(two[:, 1, :, twice, :], ex.rearrange("p k (b n) -> p (k b) n", b=GB), SY,
                                                  two[:, 0, :, twice, :], ALU.mult, ALU.subtract)
                last.then_inc(s["y_lo"], 1)

            def softmax_shift(c, r):
                dve.wait_ge(s["s_mm"], c * 2 + (r - 1))
                sc = ps[:, 2 * r:2 * r + 2, :].rearrange("p a (h n) -> p (a h) n", n=S)
                v.reduce_max(mx[:, r, :], sc, AX.X).then_inc(s["mx"], 1)
                dve.wait_ge(s["mx"], c * 2 + (r - 1))
                v.tensor_tensor(heads(prob[:, r, :]), sc, mx[:, r, :].unsqueeze(2).to_broadcast([128, H, S]),
                                ALU.subtract).then_inc(s["sub"], 1)

            def softmax_sum(c, r):
                dve.wait_ge(s["exp"], c * 2 + (r - 1))
                v.reduce_sum(sm[:, r, :], heads(prob[:, r, :]), AX.X).then_inc(s["norm"], 1)
                dve.wait_ge(s["norm"], c * 4 + (2 * r - 3))
                v.reciprocal(rs[:, r, :], sm[:, r, :]).then_inc(s["norm"], 1)

            def qk_low(c, w, dst):
                dve.wait_ge(s["qk_hi"], c * 2 + (w + 1))
                for m in range(KC):
                    last = v.scalar_tensor_tensor(dst[:, 1, m, :], ps[:, 4 + w, m * CH:(m + 1) * CH],
                                                  ab[:, w, m:m + 1], dst[:, 0, m, :], ALU.add, ALU.subtract)
                last.then_inc(s["qk_lo"], 1)

            def attn(c, new, old, fin, more):
                if old:
                    softmax_shift(c, 0)
                    softmax_shift(c, 1)
                if fin:
                    dve.wait_ge(s["wo_mm"], c - 1)
                    dve.wait_ge(s["xb"], c - 1)
                    if not isinstance(c, int) or c >= 3:
                        dve.wait_ge(s["x1_lo"], c - 2)
                        dve.wait_ge(s["x1_out"], c * 16 - 32)
                    v.scalar_tensor_tensor(x1.rearrange("p k n -> p (k n)"), ps[:, 5, :], 1 / (SQ * SA),
                                           xin.rearrange("p k n -> p (k n)"), ALU.mult, ALU.add).then_inc(s["x1"], 1)
                if old:
                    softmax_sum(c, 0)
                if fin:
                    dve.wait_ge(s["x1_hi"], c - 1)
                    cols = ds((c - 2) * CH, CH)
                    v.scalar_tensor_tensor(xh[:, 1, :, cols], x1, SX, xh[:, 0, :, cols],
                                           ALU.mult, ALU.subtract).then_inc(s["x1_lo"], 1)
                if new:
                    qk_low(c, 0, qh)
                if old:
                    softmax_sum(c, 1)
                if new:
                    qk_low(c, 1, kh)
                    dve.wait_ge(s["qk_lo"], c * 2 + 2)
                    for h in range(KBD_DVE):
                        last = v.tensor_scalar(kbd_head(h), kh_batches, head_mask[:, h:h + 1], None, ALU.mult)
                    last.then_inc(s["kbd"], 1)
                if more:
                    y_low(c + 1)
                if old:
                    for r in range(2):
                        for hb in range(2):
                            dve.wait_ge(s["pt_hi"], c * 4 + (2 * r + hb - 3))
                            cols = slice(hb * 512, (hb + 1) * 512)
                            v.tensor_tensor(pt[:, r, 1, cols], ps[:, 2 * r + hb, :], pt[:, r, 0, cols],
                                            ALU.subtract).then_inc(s["pt_lo"], 1)
                    dve.wait_ge(s["o_hi"], c)
                    for m in range(KC):
                        last = v.scalar_tensor_tensor(oh_[:, 1, m, :], ps[:, 4, m * CH:(m + 1) * CH], ab[:, 2, m:m + 1],
                                                      oh_[:, 0, m, :], ALU.add, ALU.subtract)
                    last.then_inc(s["o_lo"], 1)
                if new:
                    dve.wait_ge(s["v_hi"], c + 1)
                    for r in range(2):
                        for j in range(2):
                            last = v.scalar_tensor_tensor(vb(1, r, j), vp(r, j), half_mask[:, j:j + 1], vb(0, r, j),
                                                          ALU.mult, ALU.subtract)
                    last.then_inc(s["v_lo"], 1)

            y_low(0)
            attn(0, True, False, False, True)
            attn(1, True, True, False, True)
            with dve.Fori(2, NA - 1) as c:
                attn(c, True, True, True, True)
            attn(NA - 1, True, True, True, False)
            attn(NA, False, True, True, False)
            attn(NA + 1, False, False, True, False)

            for p in es:
                ffn(p)
            ffn(ee)
            gate(4, 2)

            dve.wait_ge(s["w3_in"], 16)
            raw = misc[:, 2560:2624].rearrange("p (f e) -> p f e", f=FC)
            link(v.tensor_scalar(w3[:, 0, :, :], raw, SW, None, ALU.mult))
            v.scalar_tensor_tensor(w3[:, 1, :, :], raw, SW, w3[:, 0, :, :], ALU.mult, ALU.subtract).then_inc(s["w3"], 1)

            def z_make(k):
                dve.wait_ge(s["z_in"], k * 64 + 64)
                for j in range(4):
                    last = weighted(v, zsrc[:, j, :, :], k * GB, GB, j)
                last.then_inc(s["zchain"], 1)
                dve.wait_ge(s["zchain"], k * 2 + 1)
                v.tensor_tensor(zsrc[:, 0:2, :, :].rearrange("p j k n -> p j (k n)"),
                                zsrc[:, 0:2, :, :].rearrange("p j k n -> p j (k n)"),
                                zsrc[:, 2:4, :, :].rearrange("p j k n -> p j (k n)"), ALU.add).then_inc(s["zchain"], 1)
                dve.wait_ge(s["zchain"], k * 2 + 2)
                v.tensor_tensor(zsrc[:, 0, :, :], zsrc[:, 0, :, :], zsrc[:, 1, :, :], ALU.add).then_inc(s["z_sum"], 1)
                dve.wait_ge(s["z_hi"], k + 1)
                cols = ds(k * CH, CH)
                v.scalar_tensor_tensor(xh[:, 1, :, cols], zsrc[:, 0, :, :], SZ, xh[:, 0, :, cols],
                                       ALU.mult, ALU.subtract).then_inc(s["z_lo"], 1)

            def logits(c):
                dve.wait_ge(s["l_mm"], c + 1)
                v.scalar_tensor_tensor(logit[:, ds(c * 4, 4), :], ps[:, 6, 0:4 * NE].rearrange("p (t e) -> p t e", t=4),
                                       1 / (SR * SW), rb3.unsqueeze(1).to_broadcast([128, 4, NE]),
                                       ALU.mult, ALU.add).then_inc(s["logit"], 1)

            def router(c, previous, more):
                for st in range(16):
                    dve.wait_ge(s["r_hi"], c * 16 + (st + 1))
                    dst = h1[:, st, :, :] if st < FC else h2[:, st - FC, :, :]
                    v.tensor_tensor(dst[:, 1, :], gt[:, (st % 2) * 512:(st % 2 + 1) * 512], dst[:, 0, :],
                                    ALU.subtract).then_inc(s["r_lo"], 1)
                    if previous and st == 7:
                        logits(c - 1)
                    if more and st in (8, 11):
                        z_make(c * 2 + (2 if st == 8 else 3))
            z_make(0)
            z_make(1)
            router(0, False, True)
            with dve.Fori(1, 7) as c:
                router(c, True, True)
            router(7, True, False)
            logits(7)

            def over_e(x):
                return x.unsqueeze(2).to_broadcast([128, NP, NE])
            m1 = top8[:, :, 0:1].rearrange("p t e -> p (t e)")
            dve.wait_ge(s["logit"], 8)
            link(v.reduce_max(m1, logit, AX.X))
            v.tensor_tensor(score, logit, over_e(m1), ALU.subtract).then_inc(s["ssub"], 1)
            dve.wait_ge(s["sexp"], 1)
            link(v.reduce_sum(m1, score, AX.X))
            link(v.reciprocal(m1, m1))
            link(v.tensor_tensor(score, score, over_e(m1), ALU.mult))
            for t in range(NP):
                last = v.max(top8[:, t, :], score[:, t, :])
            link(last)
            for t in range(NP):
                last = v.max_index(index8[:, t, :], top8[:, t, :], score[:, t, :])
            link(last)
            experts = row[:, 0:NE].unsqueeze(1).to_broadcast([128, NP, NE])
            link(v.tensor_copy(pos, index8))
            for n, o in enumerate((oh0, oh1)):
                last = v.tensor_tensor(o, experts, over_e(pos[:, :, n:n + 1].rearrange("p t e -> p (t e)")), ALU.is_equal)
            link(last)
            link(v.tensor_tensor(oh0, oh0, oh1, ALU.add))
            v.tensor_copy(oh16, oh0).then_inc(s["oh"], 1)
            dve.wait_ge(s["pos_mm"], 1)
            flat = lambda x: x.rearrange("p t e -> p (t e)")
            link(v.tensor_copy(flat(pos), ps[:, 0, 0:NP * NE]))
            te = lambda x: flat(x).unsqueeze(2).to_broadcast([128, NP * NE, CAP])
            dt = dtmp.rearrange("p t (e n) -> p (t e) n", n=CAP)
            link(v.tensor_tensor(dt, te(pos), row[:, 0:CAP].unsqueeze(1).to_broadcast([128, NP * NE, CAP]), ALU.is_equal))
            link(v.tensor_tensor(dt, dt, te(oh0), ALU.mult))
            for b2 in range(2):
                v.tensor_scalar(d01[:, :, b2, :], dtmp, half_mask[:, b2:b2 + 1], None, ALU.mult)
            link(v.tensor_tensor(dt, dt, te(score), ALU.mult))
            link(v.tensor_scalar(dsc[:, 0, :, :], dtmp, SCW, None, ALU.mult))
            v.scalar_tensor_tensor(dsc[:, 1, :, :], dtmp, SCW, dsc[:, 0, :, :], ALU.mult, ALU.subtract
                                   ).then_inc(s["slot_oh"], 1)

            def dispatch(t, u):
                dve.wait_ge(s["zt_mm"], t + (u + 1))
                v.tensor_copy(ztok[:, u, :, :, :].rearrange("p h k n -> p (h k n)"), zt_ps[u]).then_inc(s["zt"], 1)
                dve.wait_ge(s["dp_mm"], t + (u + 1))
                for k in range(KC):
                    v.tensor_copy(xe_pair(1, k, t, u), dp(u, 1, k)).then_inc(s["xe_lo"], 1)
            with dve.Fori(0, NP // 2) as half_t:
                t = half_t * 2
                dispatch(t, 0)
                dispatch(t, 1)

            dve.wait_ge(s["eb2_in"], 16)
            v.tensor_scalar(misc[:, 4608:6656], misc[:, 4608:6656], SEO, None, ALU.mult).then_inc(s["eb2"], 1)
            dve.wait_ge(s["eb2"], 1)

            def eout(e, half):
                for t in TILES[half]:
                    dve.wait_ge(s["m_out"], e * 2 + (half + 1))
                    if t >= 2:
                        dve.wait_ge(s["eo_lo"], e * 5 + (t - 1))
                    elif t == 0 and not (isinstance(e, int) and e == 0):
                        dve.wait_ge(s["eo_lo"], e * 5)
                    v.scalar_tensor_tensor(ev[:, t % 2, :], ps[:, 3 + t, 0:D], SEO / (SR * SW), misc[:, ds(e * D + 4608, D)],
                                           ALU.mult, ALU.add).then_inc(s["ev"], 1)
                    dve.wait_ge(s["eo_hi"], e * 5 + (t + 1))
                    v.tensor_tensor(eo[:, t % 4, 1, :], ev[:, t % 2, :], eo[:, t % 4, 0, :], ALU.subtract).then_inc(s["eo_lo"], 1)

            def expert(e, fresh=False):
                for st in range(16):
                    n = len(TILES[st // FC]) * 128
                    dve.wait_ge(s["m_hi"], e * 16 + (st + 1))
                    v.tensor_tensor(hid[:, st % 4, 1, 0:n], gt[:, (st % 2) * 512:(st % 2) * 512 + n],
                                    hid[:, st % 4, 0, 0:n], ALU.subtract).then_inc(s["m_lo"], 1)
                    if st == 1 and not fresh:
                        eout(e - 1, 1)
                    if st == 9:
                        eout(e, 0)
            expert(0, True)
            with dve.Fori(1, NE) as e:
                expert(e)
            eout(NE - 1, 1)

            def output(t, u, fresh):
                dve.wait_ge(s["fin_mm"], t + (u + 1))
                dve.wait_ge(s[f"fin_in{u}"], t * 24 + 48)
                if not fresh:
                    dve.wait_ge(s[f"fin_st{u}"], t * 16)
                for b2 in range(2):
                    last = v.scalar_tensor_tensor(yo[:, u, b2, :, :],
                                                  ps[:, u, b2 * 128:(b2 + 1) * 128].rearrange("p (k n) -> p k n", k=KC),
                                                  1 / (SEO * SCW), x1f[:, u, :, b2 * S:(b2 + 1) * S], ALU.mult, ALU.add)
                last.then_inc(s["fin"], 1)
            output(0, 0, True)
            output(0, 1, True)
            with dve.Fori(1, NP // 2) as half_t:
                t = half_t * 2
                output(t, 0, False)
                output(t, 1, False)


_NAMES = ("itok", "gv", "bias", "rb3", "x", "c_swi0", "c_swi1", "c_swo", "c_wi0", "c_wi1", "c_wo", "c_g0", "c_g1",
          "a_w", "e_wi", "e_wo", "e_swi", "e_swo", "e_g1", "e_g2", "r_w1", "r_w2", "r_w3", "m_w1", "m_w2", "eb2")


def kernel(**inputs):
    import concourse.bacc as bacc
    from concourse.bass_utils import run_bass_kernel_spmd

    g = {k.replace("L0_", ""): np.asarray(v) for k, v in inputs.items()}

    def rows(w):
        *lead, r, n = w.shape
        return np.ascontiguousarray(np.moveaxis(w.reshape(*lead, r // 128, 128, n), -2, -3)).reshape(*lead, 128, -1)

    def cols(b):
        return np.moveaxis(b.reshape(-1, b.shape[-1] // 128, 128), -1, 0).reshape(128, -1)

    arrays = {
        "itok": g["itok_B_0_2"].astype(np.int32).reshape(B, 1),
        "gv": g["cond2_gate_vecs"].reshape(-1),
        "bias": np.concatenate([cols(g[n]) for n in ("attn_bq", "attn_bk", "attn_bv", "attn_bo", "ffn_rb1", "ffn_rb2",
                                                     "ffn_eb1")], axis=1),
        "rb3": g["ffn_rb3"],
        "x": g["x"].reshape(B, S, KC, 128).transpose(0, 3, 2, 1).reshape(B, 128, KC * S),
        "c_swi0": rows(g["cond_sWi0"]), "c_swi1": rows(g["cond_sWi1"]), "c_swo": rows(g["cond_sWo"]),
        "c_wi0": rows(g["cond_Wi0"]), "c_wi1": rows(g["cond_Wi1"]), "c_wo": rows(g["cond_Wo"]),
        "c_g0": rows(g["cond_g0"]), "c_g1": rows(g["cond_g1"]),
        "a_w": np.concatenate([rows(g[f"attn_W{c}"].T) for c in "qkvo"], axis=1),
        "e_wi": rows(g["cond2_expert_wi"]), "e_wo": rows(g["cond2_expert_wo"]),
        "e_swi": rows(g["cond2_share_wi"]), "e_swo": rows(g["cond2_share_wo"]),
        "e_g1": rows(g["cond2_gate_w1"]), "e_g2": rows(g["cond2_gate_w2"]),
        "r_w1": rows(g["ffn_rW1"]), "r_w2": rows(g["ffn_rW2"].reshape(4, 2 * 128, F)), "r_w3": rows(g["ffn_rW3"]),
        "m_w1": rows(g["ffn_eW1"]), "m_w2": rows(g["ffn_eW2"]),
        "eb2": g["ffn_eb2"].reshape(-1),
    }
    nc = bacc.Bacc("TRN2", target_bir_lowering=False, num_devices=1)
    feeds, a = {}, {}
    for n in _NAMES:
        arr = np.ascontiguousarray(arrays[n])
        feeds[f"in_{n}"] = arr
        a[n] = nc.dram_tensor(f"in_{n}", arr.shape, mybir.dt.from_np(arr.dtype), kind="ExternalInput").ap()
    a["out"] = nc.dram_tensor("out_x", (B, 128, KC * S), F32, kind="ExternalOutput").ap()
    build(nc, a)
    got = np.asarray(run_bass_kernel_spmd(nc, [feeds], core_ids=[0]).results[0]["out_x"])
    return np.ascontiguousarray(got.reshape(B, 128, KC, S).transpose(0, 3, 2, 1)).reshape(B, S, D)
```

```python
import numpy as np
import concourse.bass as bass
from concourse import mybir
from contextlib import ExitStack

F32, F16, BF16, I32, U32 = (mybir.dt.float32, mybir.dt.float16, mybir.dt.bfloat16,
                            mybir.dt.int32, mybir.dt.uint32)
ALU = mybir.AluOpType
ACT = mybir.ActivationFunctionType
AX = mybir.AxisListType
ds = bass.ds

B, S, D, F = 64, 64, 256, 1024
NT = B * S
KC, FC = D // 128, F // 128
H, HD = 16, 16
TYPES, E2 = 3, 4
NE, CAP = 8, int(S / 8 * 1.25)
GB = 4
CH = GB * S
NCH = (B + TYPES * (GB - 1)) // GB
NTP = NT + CH
MAT = 2048
SLOT = 2 * MAT
NSLOT = 15
SLOTS = NE * CAP
NA = B // GB
NP = B // 2
FIRST_MOE = 31
TILES = ((0, 1, 2), (3, 4))
PER_E = B * CAP

SX, SW = 4.0, 64.0
SH = SX * SW
SO = SH * SW
SY, SA = 16.0, 16.0
SQ = SY * SA
SZ = 8.0
SR = SZ * SW
SEO, SCW = 64.0, 16.0
MASKED = -1e30
KBD_DVE = 6

C_SHARE = (0, 1, 2)
C_EXP = 3
E_SHARE = ((12, 13), (1, 2), (11, 14))
E_EXP = 3
ATTN_W = 0
R_W1, R_W2 = 0, (12, 13, 1, 2)
MOE_W = ((11, 14), (10, 0))
ATTN_WORK = 3
HID_SLOT = 14
H1_SLOT, H2_SLOT, ZSRC_SLOT = 3, 5, 7
XE_SLOT, CT_SLOT, SEL_SLOT = 3, 8, 10


def build(nc, a):
    ctx = ExitStack()
    with ctx:
        def sb(name, shape, dt):
            return ctx.enter_context(nc.sbuf_tensor(name, shape, dt))

        def sem(name):
            return ctx.enter_context(nc.semaphore(name))

        def scratch(name, shape, dt):
            return nc.dram_tensor(name, shape, dt, kind="Internal").ap()

        arena = sb("arena", [128, NSLOT * SLOT], F16)
        xh = sb("xh", [128, 2, KC, NTP], F16)
        wstage = sb("wstage", [128, 2, MAT], F32)
        misc = sb("misc", [128, 6656], F32)
        row = sb("row", [128, 128], F32)
        pidx = sb("pidx", [128, 1], F32)
        ident = sb("ident", [128, 128], F32)
        ident16 = sb("ident16", [128, 128], F16)
        identb = sb("identb", [128, 128], BF16)
        upper = sb("upper", [128, 128], F32)
        upperb = sb("upperb", [128, 128], BF16)
        causal = sb("causal", [128, 8, S], BF16)
        head_mask = sb("head_mask", [128, 8], F32)
        half_mask = sb("half_mask", [128, 2], F32)
        tbl = sb("tbl", [128, 148], I32)
        wab = sb("wab", [128, 2, 20], F32)
        small = sb("small", [128, 232], F32)
        gate_in = sb("gate_in", [128, 4, KC, B + GB], F32)
        gates = sb("gates", [128, B, 4], F32)
        bias = sb("bias", [128, 8 + 16 + 64], F32)

        outb = misc[:, 0:1024].rearrange("p (m n) -> p m n", m=2)
        gt = misc[:, 1024:2048]
        hid = misc[:, 2560:4608].bitcast(F16).rearrange("p (s h n) -> p s h n", s=4, h=2)
        xf = misc[:, 4608:6656].rearrange("p (u k n) -> p u k n", u=2, k=KC)

        ps = ctx.enter_context(nc.psum_tensor("ps", [128, 8, 512], F32))

        def region(slot, nbytes, dt, at=0):
            lo = slot * SLOT + at // 2
            v = arena[:, lo:lo + nbytes // 2]
            return v if dt == F16 else v.bitcast(dt)

        hidden_f32 = region(HID_SLOT, 4096, F32)
        first_stage = [region(11 + i, 8192, F32) for i in range(3)]
        at = [0]

        def attn_buf(nbytes, dt):
            v = region(ATTN_WORK, nbytes, dt, at[0])
            at[0] += nbytes
            assert at[0] <= 8 * SLOT * 2
            return v
        ex = attn_buf(2048, F32).rearrange("p (k n) -> p k n", k=KC)
        sh = attn_buf(2048, F32).rearrange("p (k n) -> p k n", k=KC)
        xin = attn_buf(2048, F32).rearrange("p (k n) -> p k n", k=KC)
        x1 = attn_buf(2048, F32).rearrange("p (k n) -> p k n", k=KC)
        yd = attn_buf(4096, F16).rearrange("p (h k b r n) -> p h k b r n", h=2, k=KC, b=GB, r=2)
        qh = attn_buf(2048, F16).rearrange("p (h k n) -> p h k n", h=2, k=KC)
        kh = attn_buf(2048, F16).rearrange("p (h k n) -> p h k n", h=2, k=KC)
        kbd = attn_buf(16384, F16).rearrange("p (h m b e n) -> p h m b e n", h=2, m=KC, b=GB, e=8)
        vbd = attn_buf(4096, F16).rearrange("p (h b c) -> p h b c", h=2, b=GB)
        prob = attn_buf(8192, F32).rearrange("p (r n) -> p r n", r=2)
        pt = attn_buf(8192, F16).rearrange("p (r h n) -> p r h n", r=2, h=2)
        oh_ = attn_buf(2048, F16).rearrange("p (h k n) -> p h k n", h=2, k=KC)

        def vp(r, j):
            return ps[:, 6 + r, :].rearrange("p (g c) -> p g c", c=2 * HD)[:, :, j * HD:(j + 1) * HD]

        def vb(part, r, j):
            return vbd[:, part, 2 * r:2 * r + 2, :].rearrange("p b (g c) -> p (b g) c", c=2 * HD)[
                :, :, j * HD:(j + 1) * HD]
        mx = small[:, 0:32].rearrange("p (r n) -> p r n", r=2)
        sm = small[:, 32:64].rearrange("p (r n) -> p r n", r=2)
        rs = small[:, 64:96].rearrange("p (r n) -> p r n", r=2)

        h1 = region(H1_SLOT, 16384, F16).rearrange("p (f h n) -> p f h n", f=FC, h=2)
        h2 = region(H2_SLOT, 16384, F16).rearrange("p (f h n) -> p f h n", f=FC, h=2)
        zsrc = region(ZSRC_SLOT, 8192, F32).rearrange("p (j k n) -> p j k n", j=4, k=KC)
        w3 = small[:, 128:192].bitcast(F16).rearrange("p (h f e) -> p h f e", h=2, f=FC)
        def sel(i):
            return region(SEL_SLOT, 1024, F32, 1024 * i).rearrange("p (t e) -> p t e", t=NP)
        logit, score, top8, oh0, oh1, pos = (sel(i) for i in range(6))
        index8 = region(SEL_SLOT, 1024, U32, 1024 * 6).rearrange("p (t e) -> p t e", t=NP)
        oh16 = region(SEL_SLOT, 512, BF16, 1024 * 7).rearrange("p (t e) -> p t e", t=NP)
        d01 = misc[:, 0:2560].bitcast(F16).rearrange("p (t b s) -> p t b s", t=NP, b=2)
        dsc = misc[:, 2560:5120].bitcast(F16).rearrange("p (h t s) -> p h t s", h=2, t=NP)
        ztok = misc[:, 5120:5632].bitcast(F16).rearrange("p (u h k n) -> p u h k n", u=2, h=2, k=KC)
        dtmp = region(XE_SLOT, 10240, F32).rearrange("p (t s) -> p t s", t=NP)
        xe = region(XE_SLOT, 40960, F16).rearrange("p (h k n) -> p h k n", h=2, k=KC)
        ct = region(CT_SLOT, 16384, F16).rearrange("p (h t n) -> p h t n", h=2, t=NP)
        eo = misc[:, 0:1024].bitcast(F16).rearrange("p (u h n) -> p u h n", u=4, h=2)
        ev = misc[:, 2048:2048 + 2 * D].rearrange("p (u n) -> p u n", u=2)
        zt_ps = [ps[:, u, 0:256].bitcast(F16) for u in range(2)]
        ct_ps = [ps[0:SLOTS, 6 + u, 0:128].bitcast(F16) for u in range(2)]

        def xe_pair(part, k, t, u):
            v = xe[:, part, k, :].rearrange("p (e n b) -> p e b n", e=NE, n=CAP)
            return v[:, :, ds((t + u) * 2, 2), :]

        def dp(u, part, k):
            return ps[:, 2 + 2 * u + part, k * 2 * SLOTS:(k + 1) * 2 * SLOTS].rearrange(
                "p (b e n) -> p e b n", b=2, e=NE)
        ebf = region(0, B * 2 * D * 2, F16)
        x1f = xh[:, :, :, :].rearrange("p h k n -> p (h k n)").bitcast(F32)[:, 0:KC * NT].rearrange(
            "p (k n) -> p k n", k=KC)
        yo = misc[:, 3072:4096].rearrange("p (u b k n) -> p u b k n", u=4, b=2, k=KC)
        egt = region(1, 4 * 384 * 4, F32).rearrange("p (u n) -> p u n", u=4)

        ab = bias[:, 0:8].rearrange("p (w k) -> p w k", w=4)
        rb1, rb2 = bias[:, 8:16], bias[:, 16:24]
        eb1 = bias[:, 24:88]
        rb3 = small[:, 96:104]
        eb1_now = small[:, 104:112]
        itok_i, itok_f, rank = small[0:B, 192:193].bitcast(I32), small[0:B, 193:194], small[0:B, 194:195]
        gate_vec, type_oh, cnt = small[:, 196:208], small[0:B, 208:211], small[:, 212:215]
        starts, nchunks = small[:, 216:219], small[:, 220:223]
        gsum, tmp3 = small[:, 224:227], small[:, 228:231]
        scr = misc[:, 256:512]
        ones = misc[:, 0:128]
        batch_oh = misc[0:B, 128:192]
        gate_w1 = misc[:, 4608:6656].rearrange("p (k n) -> p k n", k=4 * KC)
        gate_w2 = misc[:, 1024:1032].rearrange("p (k j) -> p k j", k=2)
        gate_w2c = misc[:, 1024:1028].rearrange("p (k j) -> p k j", k=2)
        gate_hid = misc[:, 2048:2176].rearrange("p (k n) -> p k n", k=2)
        gate_rep = misc[:, 2560:3584].rearrange("p (j k n) -> p j k n", j=4, k=2)
        gate_mx = misc[:, 2304:2368]
        T_START, T_OFFC, T_OFFE, T_POS, T_PERM = 0, 20, 40, 64, 84

        cshare_d = scratch("cshare_d", [128, KC, NTP], F32)
        cexp_d = scratch("cexp_d", [128, KC, NTP], F32)
        x1_d = scratch("x1_d", [128, KC, NT], F32)
        src_d = [scratch(f"src{j}_d", [128, KC, NTP], F32) for j in range(4)]
        eout_d = scratch("eout_d", [B, NE, CAP, 2 * D], F16)

        s = {n: sem(n) for n in (
            "iotas", "dve", "small_in", "bias_in", "order_oh", "order_mm", "soft_sub", "soft_exp",
            "tables", "perm", "consts",
            "w_first_in0", "w_first_in1", "w_first_in2", "w_first_hi", "w_first_lo", "w_in", "wchain", "mw_hi", "mw_lo", "w_ready", "x_in0", "x_in1", "x_hi", "x_lo",
            "gw_in", "gate_mm", "gate_rdy", "gates",
            "exsh_in", "y_mul", "y_sum", "y_hi", "y_lo", "qk_mm", "qk_hi", "qk_lo", "kbd", "kbd_act", "s_mm",
            "mx", "sub", "exp", "norm", "p_ready", "t_mm", "pt_hi", "pt_lo", "pv_mm", "o_hi", "o_lo",
            "v_mm", "v_hi", "v_lo", "wo_mm", "xin_in", "xb", "x1", "x1_hi", "x1_lo", "x1_out",
            "z_in", "zchain", "z_sum", "z_hi", "z_lo", "r_mm", "r_hi", "r_lo", "l_mm", "logit",
            "w3_in", "w3",
            "oh", "pos_mm", "slot_oh", "d01", "zt_mm", "zt", "dp_mm", "xe_hi", "xe_lo", "ct_mm", "ct",
            "eb1", "eb2_in", "eb2", "m_mm", "m_hi", "m_lo", "m_out", "ev", "eo_hi", "eo_lo", "eo_st0", "eo_st1", "eo_st2", "eo_st3",
            "fin_in0", "fin_in1", "fin_in2", "fin_in3", "fin_mm", "fin", "fin_st0", "fin_st1", "fin_st2", "fin_st3", "x1_in")}

        class FfnPass:
            def __init__(self, name, iters, n, gated, dynamic, two_experts, slots, need_w, out_d, feat):
                self.name, self.iters, self.n, self.gated = name, iters, n, gated
                self.dynamic, self.two_experts, self.slots, self.need_w = dynamic, two_experts, slots, need_w
                self.out_d, self.feat = out_d, feat
                self.lead = 2 if gated and n == 512 else 3
                self.l1, self.hi, self.h, self.l2, self.ev, self.feat_done, self.st = (
                    sem(f"{name}_{x}") for x in ("l1", "hi", "hidden", "l2", "evac", "feat", "store"))
                if gated:
                    self.g, self.mul = sem(f"{name}_gelu"), sem(f"{name}_mul")
                self.nev = 2 * iters
                self.nst = iters if two_experts else 2 * iters

            def bank(self, st, gate):
                if self.gated and self.n == 512:
                    return 2 * (st % 2) + gate, 0
                return st % 4, gate * self.n

            def fbuf(self, st):
                u = st % (1024 // self.n)
                return hidden_f32[:, u * self.n:(u + 1) * self.n]

            def gbuf(self, st):
                return gt[:, (st % 2) * 512:(st % 2) * 512 + 512] if self.n == 512 \
                    else gt[:, (st % 4) * 256:(st % 4) * 256 + 256]

        cs = FfnPass("cs", B // 16, 512, True, False, False, C_SHARE, 0, cshare_d, 1)
        ce = FfnPass("ce", NCH // 2, CH, True, True, False, C_EXP, 9, cexp_d, 0)
        es = [FfnPass(f"s{j}", B // 16, 512, False, False, False, E_SHARE[j], 11 + (0, 3, 5)[j], src_d[1 + j], 1 + j)
              for j in range(3)]
        ee = FfnPass("ee", NCH, CH, False, True, True, E_EXP, 24, src_d[0], 0)
        passes = [cs, ce] + es + [ee]

        def before(p):
            return {"ce": cs, "s1": es[0], "s2": es[1], "ee": es[2]}.get(p.name)

        def w16(slot, part, col, width=128):
            lo = slot * SLOT + part * MAT + col
            return arena[:, lo:lo + width]

        SPLIT = ((0, 0), (0, 1), (1, 0))

        y_twice = ex.rearrange("p k (b n) -> p (k b) n", b=GB).unsqueeze(2).to_broadcast([128, KC * GB, 2, S])

        def kbd_head(h):
            return kbd.rearrange("p h m b e n -> p (h m b) e n")[:, :, h, :]
        kh_batches = kh.rearrange("p h k (b n) -> p (h k b) n", b=GB)

        def heads(x):
            return x.rearrange("p (h n) -> p h n", h=H)

        def weighted(engine, buf, b0, nb, j):
            b4 = buf.rearrange("p k (b n) -> p k b n", b=nb)
            g = gates[:, ds(b0, nb), j:j + 1].rearrange("p b j -> p (b j)").unsqueeze(1).unsqueeze(3)
            return engine.tensor_tensor(b4, b4, g.to_broadcast([128, KC, nb, S]), ALU.mult)

        block = ctx.enter_context(nc.Block())

        @block.gpsimd
        def _(pool):
            nc.gpsimd.iota(row[:, :], [[1, 128]], base=0, channel_multiplier=0,
                           allow_small_or_imprecise_dtypes=True).then_inc(s["iotas"], 1)
            nc.gpsimd.iota(pidx[:, :], [[1, 1]], base=0, channel_multiplier=1,
                           allow_small_or_imprecise_dtypes=True).then_inc(s["iotas"], 1)

            loads = []
            for t in range(TYPES):
                loads += [(a[n][t], C_EXP + 3 * t + i, SW, (s["w_first_lo"], 3) if t == 2 and i == 2 else None) for i, n in enumerate(("c_wi0", "c_wi1", "c_wo"))]
            loads += [(a["e_swi"][0], 12, SW, None), (a["e_swo"][0], 13, SW, None)]
            loads += [(a["a_w"], ATTN_W, SA, (cs.l2, 2 * cs.iters))]
            loads += [(a["e_swi"][1], 1, SW, None), (a["e_swo"][1], 2, SW, None)]
            loads += [(a["e_swi"][2], 11, SW, (ce.l2, 2 * ce.iters)), (a["e_swo"][2], 14, SW, None)]
            for e in range(E2):
                loads += [(a["e_wi"][e], E_EXP + 2 * e, SW, (s["x1_out"], 16 * (B // GB)) if e == 0 else None),
                          (a["e_wo"][e], E_EXP + 2 * e + 1, SW, None)]
            loads += [(a["r_w1"], R_W1, SW, None)]
            loads += [(a["r_w2"][0], R_W2[0], SW, (es[0].l2, 2 * es[0].iters)), (a["r_w2"][1], R_W2[1], SW, None)]
            loads += [(a["r_w2"][2], R_W2[2], SW, (es[1].l2, 2 * es[1].iters)), (a["r_w2"][3], R_W2[3], SW, None)]
            loads += [(a["m_w1"][0], MOE_W[0][0], SW, (es[2].l2, 2 * es[2].iters)), (a["m_w2"][0], MOE_W[0][1], SW, None)]
            for e in range(1, NE):
                wait = (s["slot_oh"], 3) if e == 1 else (s["m_out"], 2 * (e - 1))
                loads += [(a["m_w1"][e], MOE_W[e % 2][0], SW, wait), (a["m_w2"][e], MOE_W[e % 2][1], SW, None)]

            def fetch(i):
                pool.dma_start(wstage[:, i % 2, :], loads[i][0]).then_inc(s["w_in"], 16)

            def cut_up(i):
                _, slot, scale, wait = loads[i]
                pool.wait_ge(s["w_in"], 16 * (i + 1))
                if i + 1 < len(loads):
                    if i >= 1:
                        if i > FIRST_MOE:
                            pool.wait_ge(s["mw_lo"], i - FIRST_MOE)
                        else:
                            pool.wait_ge(s["w_ready"], i)
                    fetch(i + 1)
                if wait is not None:
                    pool.wait_ge(*wait)
                st = wstage[:, i % 2, :]
                hi, lo = (arena[:, slot * SLOT + h * MAT:slot * SLOT + (h + 1) * MAT] for h in (0, 1))
                if i >= FIRST_MOE:
                    nc.gpsimd.tensor_scalar(hi, st, scale, None, ALU.mult).then_inc(s["mw_hi"], 1)
                    return
                nc.gpsimd.tensor_scalar(st, st, scale, None, ALU.mult).then_inc(s["wchain"], 1)
                pool.wait_ge(s["wchain"], 2 * i + 1)
                nc.gpsimd.tensor_copy(hi, st).then_inc(s["wchain"], 1)
                pool.wait_ge(s["wchain"], 2 * i + 2)
                nc.gpsimd.tensor_tensor(lo, st, hi, ALU.subtract).then_inc(s["w_ready"], 1)

            fetch(0)
            for i in range(14):
                cut_up(i)

            def y_make(c):
                pool.wait_ge(s["exsh_in"], c * 32 + 32)
                weighted(nc.gpsimd, ex, c * GB, GB, 0)
                weighted(nc.gpsimd, sh, c * GB, GB, 1).then_inc(s["y_mul"], 1)
                pool.wait_ge(s["y_mul"], c + 1)
                nc.gpsimd.tensor_tensor(ex, ex, sh, ALU.add).then_inc(s["y_sum"], 1)

            def normalise(c, r):
                pool.wait_ge(s["norm"], c * 4 + (2 * r - 2))
                p_ = heads(prob[:, r, :])
                nc.gpsimd.tensor_tensor(p_, p_, rs[:, r, :].unsqueeze(2).to_broadcast([128, H, S]),
                                        ALU.mult).then_inc(s["p_ready"], 1)

            pool.wait_ge(s["gates"], 1)
            y_make(0)
            y_make(1)
            with pool.Fori(1, NA - 1) as c:
                y_make(c + 1)
                normalise(c, 0)
                normalise(c, 1)
            for c in (NA - 1, NA):
                normalise(c, 0)
                normalise(c, 1)

            for i in range(14, len(loads)):
                cut_up(i)

        @block.sync
        def _(sp):
            sp.dma_start(itok_i, a["itok"]).then_inc(s["small_in"], 16)
            sp.dma_start(gate_vec, a["gv"].partition_broadcast(128)).then_inc(s["small_in"], 16)
            sp.dma_start(first_stage[0], a["c_swi0"]).then_inc(s["w_first_in0"], 16)
            sp.wait_ge(s["perm"], 1)

            def load_x(dst, position):
                b = sp.value_load(tbl[0:1, ds(position + T_PERM, 1)], min_val=0, max_val=B - 1)
                return sp.dma_start(dst, a["x"][ds(b, 1)].rearrange("b p (k n) -> p (b k) n", k=KC))

            def g_is_first(g, u):
                return isinstance(g, int) and g == 0 and u == 0

            def x_group(g, u, fresh=False):
                if not fresh:
                    sp.wait_ge(s["x_lo"], g * 2 + (u - 1))
                    sp.wait_ge(s["tables"], 1)
                for j in range(0, 8, 2 if g_is_first(g, u) else 1):
                    load_x(xf[:, u, :, j * S:(j + 1) * S], g * 16 + (8 * u + j)).then_inc(s[f"x_in{u}"], 16)

            def stores(p):
                def store(i, half, n):
                    if p.dynamic:
                        c = i if p.two_experts else i * 2 + half
                        first = sp.value_load(tbl[0:1, ds(c + T_POS, 1)], min_val=0, max_val=B) * S
                    else:
                        first = (i * 2 + half) * 512
                    sp.wait_ge(p.feat_done, n + 1)
                    sp.dma_start(p.out_d[:, :, ds(first, p.n)], outb[:, :, 0:p.n]).then_inc(p.st, 16)
                if p is cs:
                    x_group(0, 0, True)
                    x_group(0, 1, True)
                    sp.dma_start(bias[:, :], a["bias"]).then_inc(s["bias_in"], 16)
                    sp.dma_start(rb3, a["rb3"].partition_broadcast(128)).then_inc(s["bias_in"], 16)
                    x_group(1, 0)
                    x_group(1, 1)
                    store(0, 0, 0)
                    with sp.Fori(1, p.iters - 1) as i:
                        x_group(i + 1, 0)
                        store(i - 1, 1, i * 2 - 1)
                        x_group(i + 1, 1)
                        store(i, 0, i * 2)
                    store(p.iters - 2, 1, p.iters * 2 - 3)
                    store(p.iters - 1, 0, p.iters * 2 - 2)
                    store(p.iters - 1, 1, p.iters * 2 - 1)
                elif p.two_experts:
                    with sp.Fori(0, p.iters) as i:
                        store(i, 0, i)
                else:
                    with sp.Fori(0, p.iters) as i:
                        store(i, 0, i * 2)
                        store(i, 1, i * 2 + 1)
                sp.wait_ge(p.st, 16 * p.nst)

            stores(cs)
            stores(ce)
            sp.wait_ge(s["x_lo"], 8)
            sp.dma_start(misc[:, 4608:5632], a["c_g0"]).then_inc(s["gw_in"], 16)
            sp.dma_start(misc[:, 1024:1028], a["c_g1"]).then_inc(s["gw_in"], 16)

            def exsh(c):
                sp.dma_start(ex, cexp_d[:, :, ds(c * CH, CH)]).then_inc(s["exsh_in"], 16)
                sp.dma_start(sh, cshare_d[:, :, ds(c * CH, CH)]).then_inc(s["exsh_in"], 16)

            def xin_load(c):
                for j in range(GB):
                    load_x(xin[:, :, j * S:(j + 1) * S], c * GB + j).then_inc(s["xin_in"], 16)

            def x1_store(c):
                sp.wait_ge(s["x1_lo"], c + 1)
                sp.dma_start(x1_d[:, :, ds(c * CH, CH)], x1).then_inc(s["x1_out"], 16)

            exsh(0)
            xin_load(0)
            for c in range(1, 4):
                sp.wait_ge(s["y_lo"], c)
                exsh(c)
            with sp.Fori(2, NA - 2) as c:
                x1_store(c - 2)
                xin_load(c - 1)
                sp.wait_ge(s["y_lo"], c + 2)
                exsh(c + 2)
            for c in range(NA - 2, NA + 2):
                x1_store(c - 2)
                if c - 1 < NA:
                    xin_load(c - 1)

            sp.wait_ge(s["gates"], 1)
            sp.dma_start(misc[:, 4608:6656], a["e_g1"]).then_inc(s["gw_in"], 16)
            sp.dma_start(misc[:, 1024:1032], a["e_g2"]).then_inc(s["gw_in"], 16)
            sp.dma_start(misc[:, 2400:2464], a["r_w3"]).then_inc(s["w3_in"], 16)

            for p in es + [ee]:
                stores(p)

            def z_load(k):
                for j in range(4):
                    sp.dma_start(zsrc[:, j, :, :], src_d[j][:, :, ds(k * CH, CH)]).then_inc(s["z_in"], 16)
            z_load(0)
            with sp.Fori(1, NT // CH) as k:
                sp.wait_ge(s["z_lo"], k)
                z_load(k)

            sp.wait_ge(s["ct"], NP)
            sp.wait_ge(s["xe_hi"], 2 * NP)
            sp.wait_ge(s["xe_lo"], 2 * NP)
            sp.dma_start(misc[:, 4608:6656], a["eb2"].partition_broadcast(128)).then_inc(s["eb2_in"], 16)
            sp.wait_ge(s["zt_mm"], NP)
            sp.dma_start(x1f, x1_d).then_inc(s["x1_in"], 16)
            with sp.Fori(0, NE) as e:
                for t in range(5):
                    sp.wait_ge(s["eo_lo"], e * 5 + (t + 1))
                    for h in range(2):
                        sp.dma_start(eout_d[:, ds(e, 1), 2 * t + h, :].rearrange("b e c -> b (e c)"),
                                     eo[h * 64:(h + 1) * 64, t % 4, :, :].rearrange("p h n -> p (h n)")
                                     ).then_inc(s[f"eo_st{t % 4}"], 16)
            def out_store(q, u):
                b = sp.value_load(tbl[0:1, ds(q * 8 + (2 * u + T_PERM), 1)], min_val=0, max_val=B - 1)
                sp.wait_ge(s["fin"], q * 4 + (u + 1))
                sp.dma_start(a["out"][ds(b, 1)].rearrange("b p (k n) -> p (b k) n", k=KC),
                             yo[:, u, 0, :, :]).then_inc(s[f"fin_st{u}"], 16)
            with sp.Fori(0, NP // 4) as q:
                for u in range(4):
                    out_store(q, u)
            for u in range(4):
                sp.wait_ge(s[f"fin_st{u}"], 4 * B)

        @block.tensor
        def _(pe):
            mm = nc.tensor.matmul
            pe.wait_ge(s["order_oh"], 1)
            mm(ps[:, 0, 0:TYPES], ones[0:B, :], type_oh, start=True, stop=True)
            mm(ps[0:B, 1, 0:TYPES], upper[0:B, 0:B], type_oh, start=True, stop=True).then_inc(s["order_mm"], 1)
            pe.wait_ge(s["order_oh"], 2)
            mm(ps[0:1, 2, 0:B], pidx[0:B, 0:1], batch_oh, start=True, stop=True).then_inc(s["order_mm"], 1)

            def ffn(p):
                if p is cs:
                    pe.wait_ge(s["tables"], 1)
                else:
                    pe.wait_ge(s["w_ready"], p.need_w)
                if p is ce:
                    pe.wait_ge(s["consts"], 1)
                if p is es[0]:
                    pe.wait_ge(s["pt_lo"], 4 * NA)
                prev = before(p)
                if prev is not None:
                    pe.wait_ge(prev.ev, prev.nev)

                def at_chunk(i, half):
                    if not p.dynamic:
                        return 0, (i * 2 + half) * 512
                    c = i if p.two_experts else i * 2 + half
                    first = pe.value_load(tbl[0:1, ds(c + T_START, 1)], min_val=0, max_val=NT)
                    off = pe.value_load(tbl[0:1, ds(c + (T_OFFE if p.two_experts else T_OFFC), 1)],
                                        min_val=0, max_val=6 * SLOT)
                    return off, first

                def weight(off, half, matrix, part, col):
                    if not p.dynamic:
                        return w16(p.slots[matrix], part, col)
                    base = (p.slots + matrix + (2 * half if p.two_experts else 0)) * SLOT + part * MAT + col
                    return arena[:, ds(off + base, 128)]

                def first(i, st, place):
                    half, f = divmod(st, FC)
                    off, start = place
                    if p is cs and f == 0:
                        pe.wait_ge(s["x_lo"], i * 2 + (half + 1))
                    if p is es[0] and f == 0:
                        pe.wait_ge(s["x1_lo"], i * 4 + (2 * half + 2))
                    for g in range(2 if p.gated else 1):
                        if p is cs and isinstance(i, int) and i == 0 and st == 0:
                            pe.wait_ge(s["w_first_lo"], g + 1)
                        bank, col = p.bank(st, g)
                        for k in range(KC):
                            for n, (wp, xp) in enumerate(SPLIT):
                                last = mm(ps[:, bank, col:col + p.n], weight(off, half, g, wp, k * F + f * 128),
                                          xh[:, xp, k, ds(start, p.n)],
                                          start=(k == 0 and n == 0), stop=(k == KC - 1 and n == 2))
                    last.then_inc(p.l1, 1)

                def second(i, st, place):
                    half, f = divmod(st, FC)
                    if f == 0 and not (isinstance(i, int) and i == 0):
                        pe.wait_ge(p.ev, i * 2 + (half - 1))
                    if p is cs and isinstance(i, int) and i == 0 and st == 0:
                        pe.wait_ge(s["w_first_lo"], 3)
                    if p is es[0] and isinstance(i, int) and i == 0 and st == 0:
                        pe.wait_ge(s["x1"], NA)
                    pe.wait_ge(p.h, i * 16 + (st + 1))
                    for m in range(2):
                        for n, (wp, hp) in enumerate(SPLIT):
                            last = mm(ps[:, 4 + 2 * half + m, 0:p.n],
                                      weight(place[0], half, 2 if p.gated else 1, wp, f * D + m * 128),
                                      hid[:, st % 4, hp, 0:p.n], start=(f == 0 and n == 0),
                                      stop=(f == FC - 1 and n == 2))
                    if f == FC - 1:
                        last.then_inc(p.l2, 1)

                def body(i, lastone):
                    here = at_chunk(i, 0)
                    place = (here, here if p.two_experts else at_chunk(i, 1))
                    ahead = None if lastone else at_chunk(i + 1, 0)
                    for st in range(16):
                        second(i, st, place[st // FC])
                        nxt = st + p.lead
                        if nxt < 16:
                            first(i, nxt, place[nxt // FC])
                        elif not lastone:
                            first(i + 1, nxt - 16, ahead)

                place0 = at_chunk(0, 0)
                for st in range(p.lead):
                    first(0, st, place0)
                body(0, False)
                with pe.Fori(1, p.iters - 1) as i:
                    body(i, False)
                body(p.iters - 1, True)

            def gate(kc_in, n_out, turn, p_last):
                pe.wait_ge(s["gw_in"], 32 * turn)
                pe.wait_ge(p_last.feat_done, p_last.nst)
                pe.wait_ge(p_last.ev, p_last.nev)
                for m in range(2):
                    for k in range(kc_in):
                        last = mm(ps[:, m, 0:B], gate_w1[:, k, m * 128:(m + 1) * 128], gate_in[:, k // KC, k % KC, 0:B],
                                  start=(k == 0), stop=(k == kc_in - 1))
                last.then_inc(s["gate_mm"], 1)
                pe.wait_ge(s["gate_rdy"], 2 * turn)

                for j in range(n_out):
                    for k in range(2):
                        last = mm(ps[:, 2, j * B:(j + 1) * B], gate_rep[:, j, k, :], gate_hid[:, k, :],
                                  start=(k == 0), stop=(k == 1))
                last.then_inc(s["gate_mm"], 1)

            ffn(cs)
            ffn(ce)
            gate(4, 2, 1, ce)

            def wide_products(dst, w, m, data):
                for k in range(KC):
                    for j, (wp, xp) in enumerate(SPLIT):
                        last = mm(dst, w16(ATTN_W, wp, (w * KC + k) * D + m * 128), data(xp, k),
                                  start=(k == 0 and j == 0), stop=(k == KC - 1 and j == 2))
                return last

            def attn(c, new, old):
                if new:
                    pe.wait_ge(s["y_lo"], c + 1)
                    for w in range(2):
                        if w == 1 and (not isinstance(c, int) or c >= 2):
                            pe.wait_ge(s["x1"], c - 1)
                        for m in range(2):
                            last = wide_products(ps[:, 4 + w, m * CH:(m + 1) * CH], w, m,
                                                 lambda xp, k: yd[:, xp, k, :, 0, :])
                        last.then_inc(s["qk_mm"], 1)
                    if old:
                        pe.wait_ge(s["v_lo"], c)
                    for b in range(GB):
                        for k in range(KC):
                            for j, (yp, wp) in enumerate(SPLIT):
                                last = mm(ps[:, 6 + b // 2, (b % 2) * D:(b % 2 + 1) * D],
                                          yd[:, yp, k, b, :, :].rearrange("p r n -> p (r n)"),
                                          w16(ATTN_W, wp, (2 * KC + k) * D, D),
                                          start=(k == 0 and j == 0), stop=(k == KC - 1 and j == 2))
                    last.then_inc(s["v_mm"], 1)
                if old:
                    for r in range(2):
                        pe.wait_ge(s["p_ready"], c * 2 + (r - 1))
                        for hb in range(2):
                            for q in range(4):
                                hp = hb * 4 + q
                                last = nc.tensor.transpose(ps[:, 2 * r + hb, q * 128:(q + 1) * 128],
                                                           prob[:, r, hp * 128:(hp + 1) * 128], ident[:, :])
                            last.then_inc(s["t_mm"], 1)
                    if new:
                        pe.wait_ge(s["qk_lo"], c * 2 + 1)
                    else:
                        pe.wait_ge(s["v_lo"], c)
                    for b in range(GB):
                        r, b2 = divmod(b, 2)
                        if b2 == 0:
                            pe.wait_ge(s["pt_lo"], c * 4 + (2 * r - 2))
                        for hp in range(8):
                            o, n0 = 32 * (hp % 4), (hp // 4) * CH + b * S
                            for j, (vp, pp) in enumerate(SPLIT):
                                col = hp * 128 + b2 * S
                                last = mm(ps[o:o + 32, 4, n0:n0 + S], vbd[:, vp, b, hp * 32:(hp + 1) * 32],
                                          pt[:, r, pp, col:col + S], start=(j == 0), stop=(j == 2))
                    last.then_inc(s["pv_mm"], 1)
                if new:
                    pe.wait_ge(s["kbd"], c + 1)
                    pe.wait_ge(s["kbd_act"], c + 1)
                    for r in range(2):
                        for m in range(2):
                            for b2 in range(2):
                                b = 2 * r + b2
                                for j, (kp, qp) in enumerate(SPLIT):
                                    mm(ps[b2 * 64:b2 * 64 + 64, 2 * r + m, :], qh[:, qp, m, b * S:(b + 1) * S],
                                       kbd[:, kp, m, b, :, :].rearrange("p h n -> p (h n)"),
                                       start=(j == 0), stop=False, skip_group_check=True)
                            last = mm(ps[:, 2 * r + m, :], identb[:, :], causal[:, :, :].rearrange("p h n -> p (h n)"),
                                      start=False, stop=True, skip_group_check=True)
                        last.then_inc(s["s_mm"], 1)
                if old:
                    pe.wait_ge(s["o_lo"], c)
                    if new:
                        pe.wait_ge(s["qk_lo"], c * 2 + 2)
                    else:
                        pe.wait_ge(s["x1"], c - 1)
                    for m in range(2):
                        last = wide_products(ps[:, 5, m * CH:(m + 1) * CH], 3, m, lambda xp, k: oh_[:, xp, k, :])
                    last.then_inc(s["wo_mm"], 1)

            pe.wait_ge(s["w_ready"], 12)
            attn(0, True, False)
            attn(1, True, True)
            with pe.Fori(2, NA) as c:
                attn(c, True, True)
            attn(NA, False, True)

            for p in es:
                ffn(p)
            ffn(ee)
            gate(8, 4, 2, ee)

            def router_in(c, f):
                if f >= 4:
                    pe.wait_ge(s["r_lo"], c * 16 + (f - 3))
                for k in range(KC):
                    for n, (wp, xp) in enumerate(SPLIT):
                        last = mm(ps[:, f % 4, :], w16(R_W1, wp, k * F + f * 128), xh[:, xp, k, ds(c * 512, 512)],
                                  start=(k == 0 and n == 0), stop=(k == KC - 1 and n == 2))
                last.then_inc(s["r_mm"], 1)

            def router_mid(c, fo):
                if fo >= 2:
                    pe.wait_ge(s["r_lo"], c * 16 + (8 + fo - 1))
                for k in range(FC):
                    if fo == 0:
                        pe.wait_ge(s["r_lo"], c * 16 + (k + 1))
                    for n, (wp, xp) in enumerate(SPLIT):
                        last = mm(ps[:, 4 + fo % 2, :], w16(R_W2[k // 2], wp, (k % 2) * F + fo * 128), h1[:, k, xp, :],
                                  start=(k == 0 and n == 0), stop=(k == FC - 1 and n == 2))
                last.then_inc(s["r_mm"], 1)

            def router_out(c):
                pe.wait_ge(s["r_lo"], c * 16 + 16)
                if not isinstance(c, int) or c > 0:
                    pe.wait_ge(s["logit"], c)
                for t in range(4):
                    for fo in range(FC):
                        for n, (wp, xp) in enumerate(SPLIT):
                            last = mm(ps[:, 6, t * NE:(t + 1) * NE], h2[:, fo, xp, t * 128:(t + 1) * 128],
                                      w3[:, wp, fo, :], start=(fo == 0 and n == 0), stop=(fo == FC - 1 and n == 2))
                last.then_inc(s["l_mm"], 1)

            def router(c, previous):
                pe.wait_ge(s["z_lo"], c * 2 + 2)
                for f in range(FC):
                    router_in(c, f)
                if previous:
                    router_out(c - 1)
                for fo in range(FC):
                    router_mid(c, fo)

            pe.wait_ge(s["w_ready"], 29)
            pe.wait_ge(s["w3"], 1)
            pe.wait_ge(s["gates"], 2)
            router(0, False)
            with pe.Fori(1, 8) as c:
                router(c, True)
            router_out(7)

            pe.wait_ge(s["oh"], 1)
            mm(ps[:, 0, 0:NP * NE], upperb[:, :], oh16.rearrange("p t e -> p (t e)"), start=True,
               stop=True).then_inc(s["pos_mm"], 1)

            pe.wait_ge(s["slot_oh"], 3)

            def dispatch(t, u, fresh):
                if not fresh:
                    pe.wait_ge(s["zt"], t + (u - 1))
                for h in range(2):
                    for k in range(KC):
                        c0 = (h * KC + k) * 128
                        last = nc.tensor.transpose(zt_ps[u][:, c0:c0 + 128], xh[:, h, k, ds((t + u) * 128, 128)],
                                                   ident16[:, :])
                last.then_inc(s["zt_mm"], 1)
                if not fresh:
                    pe.wait_ge(s["ct"], t + (u - 1))
                for h in range(2):
                    last = nc.tensor.transpose(ct_ps[u][:, h * 128:(h + 1) * 128],
                                               dsc[:, h, ds(t + u, 1), :].rearrange("p t s -> p (t s)"), ident16[:, :])
                last.then_inc(s["ct_mm"], 1)
                if not fresh:
                    pe.wait_ge(s["xe_hi"], t * 2 + (2 * u - 2))
                    pe.wait_ge(s["xe_lo"], t * 2 + (2 * u - 2))
                pe.wait_ge(s["zt"], t + (u + 1))
                for h in range(2):
                    for k in range(KC):
                        last = mm(ps[:, 2 + 2 * u + h, k * 2 * SLOTS:(k + 1) * 2 * SLOTS], ztok[:, u, h, k, :],
                                  d01[:, ds(t + u, 1), :, :].rearrange("p t b s -> p (t b s)"), start=True, stop=True)
                last.then_inc(s["dp_mm"], 1)
            dispatch(0, 0, True)
            dispatch(0, 1, True)
            with pe.Fori(1, NP // 2) as half_t:
                t = half_t * 2
                dispatch(t, 0, False)
                dispatch(t, 1, False)

            pe.wait_ge(s["xe_hi"], 2 * NP)
            pe.wait_ge(s["xe_lo"], 2 * NP)
            pe.wait_ge(s["ct"], NP)

            def expert_in(e, par, st):
                half, f = divmod(st, FC)
                n, c0 = len(TILES[half]) * 128, TILES[half][0] * 128
                if st == 0:
                    if isinstance(e, int) and e == 0:
                        pe.wait_ge(s["w_ready"], FIRST_MOE)
                    else:
                        pe.wait_ge(s["mw_lo"], e * 2)
                for k in range(KC):
                    for j, (wp, xp) in enumerate(SPLIT):
                        last = mm(ps[:, st % 2, 0:n], w16(MOE_W[par][0], wp, k * F + f * 128),
                                  xe[:, xp, k, ds(e * PER_E + c0, n)],
                                  start=(k == 0 and j == 0), stop=(k == KC - 1 and j == 2))
                last.then_inc(s["m_mm"], 1)

            def expert_out(e, par, st):
                half, f = divmod(st, FC)
                if f == 0 and not (isinstance(e, int) and e == 0):
                    pe.wait_ge(s["ev"], e * 5 + (-2 if half == 0 else 0))
                pe.wait_ge(s["m_lo"], e * 16 + (st + 1))
                for i_t, t in enumerate(TILES[half]):
                    for j, (hp, wp) in enumerate(SPLIT):
                        last = mm(ps[:, 3 + t, 0:D], hid[:, st % 4, hp, i_t * 128:(i_t + 1) * 128],
                                  w16(MOE_W[par][1], wp, f * D, D), start=(f == 0 and j == 0),
                                  stop=(f == FC - 1 and j == 2))
                if f == FC - 1:
                    last.then_inc(s["m_out"], 1)

            def expert(e, par, lastone=False):
                for st in range(16):
                    expert_out(e, par, st)
                    if st + 2 < 16:
                        expert_in(e, par, st + 2)
                    elif not lastone:
                        expert_in(e + 1, 1 - par, st - 14)
            for st in range(2):
                expert_in(0, 0, st)
            expert(0, 0)
            expert(1, 1)
            with pe.Fori(1, NE // 2 - 1) as half_e:
                e = half_e * 2
                expert(e, 0)
                expert(e + 1, 1)
            expert(NE - 2, 0)
            expert(NE - 1, 1, True)

            pe.wait_ge(s["ev"], 5 * NE)

            def combine(q, u):
                if not (isinstance(q, int) and q == 0):
                    pe.wait_ge(s["fin"], q * 4 + (u - 3))
                for b2 in range(2):
                    for m in range(2):
                        for j, (ep, cp) in enumerate(SPLIT):
                            last = mm(ps[:, u, (b2 * KC + m) * S:(b2 * KC + m + 1) * S],
                                      ebf[0:SLOTS, ds(q * (8 * 2 * D) + ((2 * u + b2) * 2 * D + ep * D + m * 128), 128)],
                                      ct[0:SLOTS, cp, ds(q * 4 + u, 1), b2 * S:(b2 + 1) * S].rearrange("p t n -> p (t n)"),
                                      start=(j == 0), stop=(j == 2))
                last.then_inc(s["fin_mm"], 1)

            for g in range(4):
                pe.wait_ge(s[f"fin_in{g}"], 16)
                if g == 0:
                    for q in range(2):
                        for u in range(4):
                            combine(q, u)
                else:
                    with pe.Fori(2 * g, 2 * g + 2) as q:
                        for u in range(4):
                            combine(q, u)

        @block.scalar
        def _(act):
            fn = nc.scalar.activation
            act.dma_start(first_stage[1], a["c_swi1"]).then_inc(s["w_first_in1"], 16)
            act.dma_start(first_stage[2], a["c_swo"]).then_inc(s["w_first_in2"], 16)
            act.wait_ge(s["soft_sub"], 1)
            fn(gate_vec, gate_vec, ACT.Exp, scale=10.0).then_inc(s["soft_exp"], 1)

            act.wait_ge(s["perm"], 1)
            for j in range(1, 8, 2):
                b = act.value_load(tbl[0:1, ds(j + T_PERM, 1)], min_val=0, max_val=B - 1)
                act.dma_start(xf[:, 0, :, j * S:(j + 1) * S],
                              a["x"][ds(b, 1)].rearrange("b p (k n) -> p (b k) n", k=KC)).then_inc(s["x_in0"], 16)
            for i in range(3):
                act.wait_ge(s[f"w_first_in{i}"], 16)
                fn(w16(C_SHARE[i], 0, 0, MAT), first_stage[i], ACT.Copy, scale=SW).then_inc(s["w_first_hi"], 1)

            def x_group(g, u):
                act.wait_ge(s[f"x_in{u}"], (g - u) * 64 + 128)
                act.wait_ge(s["tables"], 1)
                fn(xh[:, 0, :, ds(g * 512, 512)], xf[:, u, :, :], ACT.Copy, scale=SX).then_inc(s["x_hi"], 1)
            x_group(0, 0)
            x_group(1, 1)

            def ffn(p):
                def hidden(i, st):
                    act.wait_ge(p.l1, i * 16 + (st + 1))
                    bank, col = p.bank(st, 0)
                    if p.gated:
                        fn(p.gbuf(st), ps[:, bank, col:col + p.n], ACT.Gelu_apprx_tanh, scale=1 / SH).then_inc(p.g, 1)
                        act.wait_ge(p.mul, i * 16 + (st + 1))
                        fn(hid[:, st % 4, 0, 0:p.n], p.fbuf(st), ACT.Copy).then_inc(p.hi, 1)
                    else:
                        fn(hid[:, st % 4, 0, 0:p.n], ps[:, bank, col:col + p.n], ACT.Relu).then_inc(p.hi, 1)

                def evacuate(i, half):
                    act.wait_ge(p.l2, i * 2 + (half + 1))
                    if half == 0 and isinstance(i, int) and i == 0 and before(p) is not None:
                        act.wait_ge(before(p).st, 16 * before(p).nst)
                    if p.two_experts:
                        if half == 0:
                            if not (isinstance(i, int) and i == 0):
                                act.wait_ge(p.st, i * 16)
                            act.wait_ge(s["consts"], 1)
                            fn(outb[:, :, 0:p.n], ps[:, 4:6, 0:p.n], ACT.Copy,
                               scale=wab[:, 0, ds(i, 1)]).then_inc(p.ev, 1)
                        return
                    if not (isinstance(i, int) and i == 0 and half == 0):
                        act.wait_ge(p.st, i * 32 + 16 * half)
                    fn(outb[:, :, 0:p.n], ps[:, 4 + 2 * half:6 + 2 * half, 0:p.n], ACT.Copy,
                       scale=1 / SO).then_inc(p.ev, 1)

                def body(i, first, lastone):
                    for st in range(16):
                        hidden(i, st)
                        if st == 1 and not first:
                            evacuate(i - 1, 1)
                        if st == 9:
                            evacuate(i, 0)
                        if p is cs and not lastone and st in (3, 11):
                            x_group(i * 2 + (2 if st == 3 else 3), 0 if st == 3 else 1)
                body(0, True, False)
                with act.Fori(1, p.iters - 1) as i:
                    body(i, False, False)
                body(p.iters - 1, False, True)
                evacuate(p.iters - 1, 1)

            def gate(turn):
                act.wait_ge(s["soft_sub"], 1 + turn)
                fn(gates[:, :, 0:2 * turn], gates[:, :, 0:2 * turn], ACT.Exp).then_inc(s["soft_exp"], 1)

            ffn(cs)
            ffn(ce)
            gate(1)

            def y_parts(c):
                act.wait_ge(s["y_sum"], c + 1)
                if not isinstance(c, int) or c > 0:
                    act.wait_ge(s["v_mm"], c)
                fn(yd[:, 0, :, :, :, :].rearrange("p k b r n -> p (k b) r n"), y_twice, ACT.Copy,
                   scale=SY).then_inc(s["y_hi"], 1)

            def attn(c, new, old, fin, more):
                if old:
                    for r in range(2):
                        act.wait_ge(s["sub"], c * 2 + (r - 1))
                        fn(prob[:, r, :], prob[:, r, :], ACT.Exp, scale=0.25 / (SQ * SQ)).then_inc(s["exp"], 1)
                if fin:
                    act.wait_ge(s["x1"], c - 1)
                    act.wait_ge(ce.l2, 2 * ce.iters)
                    fn(xh[:, 0, :, ds((c - 2) * CH, CH)], x1, ACT.Copy, scale=SX).then_inc(s["x1_hi"], 1)
                if new:
                    for w, dst in enumerate((qh, kh)):
                        act.wait_ge(s["qk_mm"], c * 2 + (w + 1))
                        for m in range(KC):
                            last = fn(dst[:, 0, m, :], ps[:, 4 + w, m * CH:(m + 1) * CH], ACT.Identity,
                                      bias=ab[:, w, m:m + 1])
                        last.then_inc(s["qk_hi"], 1)
                    act.wait_ge(s["qk_lo"], c * 2 + 2)
                    for h in range(KBD_DVE, 8):
                        last = fn(kbd_head(h), kh_batches, ACT.Copy, scale=head_mask[:, h:h + 1])
                    last.then_inc(s["kbd_act"], 1)
                if old:
                    for r in range(2):
                        for hb in range(2):
                            act.wait_ge(s["t_mm"], c * 4 + (2 * r + hb - 3))
                            fn(pt[:, r, 0, hb * 512:(hb + 1) * 512], ps[:, 2 * r + hb, :], ACT.Copy
                               ).then_inc(s["pt_hi"], 1)
                if more:
                    y_parts(c + 1)
                if old:
                    act.wait_ge(s["pv_mm"], c)
                    for m in range(KC):
                        last = fn(oh_[:, 0, m, :], ps[:, 4, m * CH:(m + 1) * CH], ACT.Identity, bias=ab[:, 2, m:m + 1])
                    last.then_inc(s["o_hi"], 1)
                if new:
                    act.wait_ge(s["v_mm"], c + 1)
                    for r in range(2):
                        for j in range(2):
                            last = fn(vb(0, r, j), vp(r, j), ACT.Copy, scale=half_mask[:, j:j + 1])
                    last.then_inc(s["v_hi"], 1)
                if old:
                    act.wait_ge(s["xin_in"], c * 64)
                    for k in range(KC):
                        last = fn(xin[:, k, :], xin[:, k, :], ACT.Identity, bias=ab[:, 3, k:k + 1])
                    last.then_inc(s["xb"], 1)

            y_parts(0)
            attn(0, True, False, False, True)
            attn(1, True, True, False, True)
            with act.Fori(2, NA - 1) as c:
                attn(c, True, True, True, True)
            attn(NA - 1, True, True, True, False)
            attn(NA, False, True, True, False)
            attn(NA + 1, False, False, True, False)

            for p in es:
                ffn(p)
            ffn(ee)
            gate(2)

            def z_parts(k):
                act.wait_ge(s["z_sum"], k + 1)
                act.wait_ge(ee.l2, 2 * ee.iters)
                fn(xh[:, 0, :, ds(k * CH, CH)], zsrc[:, 0, :, :], ACT.Copy, scale=SZ).then_inc(s["z_hi"], 1)

            def rhidden(c, st, fresh):
                act.wait_ge(s["r_mm"], c * 16 + (st + 1))
                if st < FC:
                    src, dst, b_, scale = ps[:, st % 4, :], h1[:, st, 0, :], rb1[:, st:st + 1], 1.0
                else:
                    fo = st - FC
                    src, dst, b_, scale = ps[:, 4 + fo % 2, :], h2[:, fo, 0, :], rb2[:, fo:fo + 1], 1 / SW
                if not (fresh and st < 2):
                    act.wait_ge(s["r_lo"], c * 16 + (st - 1))
                fn(gt[:, (st % 2) * 512:(st % 2 + 1) * 512], src, ACT.Relu, bias=b_, scale=scale)
                fn(dst, src, ACT.Relu, bias=b_, scale=scale).then_inc(s["r_hi"], 1)

            def router(c, fresh, more):
                for st in range(16):
                    rhidden(c, st, fresh)
                    if more and st in (8, 11):
                        z_parts(c * 2 + (2 if st == 8 else 3))
            z_parts(0)
            z_parts(1)
            router(0, True, True)
            with act.Fori(1, 7) as c:
                router(c, False, True)
            router(7, False, False)

            act.wait_ge(s["soft_sub"], 4)
            fn(score, score, ACT.Exp).then_inc(s["soft_exp"], 1)

            act.wait_ge(s["slot_oh"], 1)
            fn(d01[:, :, 0, :], dtmp, ACT.Copy, scale=half_mask[:, 0:1])
            fn(d01[:, :, 1, :], dtmp, ACT.Copy, scale=half_mask[:, 1:2]).then_inc(s["d01"], 1)
            act.wait_ge(s["slot_oh"], 2)
            fn(dsc[:, 0, :, :], dtmp, ACT.Copy, scale=SCW).then_inc(s["d01"], 1)

            def dispatch(t, u):
                act.wait_ge(s["ct_mm"], t + (u + 1))
                act.wait_ge(s["slot_oh"], 3)
                fn(ct[0:SLOTS, :, ds(t + u, 1), :].rearrange("p h t n -> p (h t) n"),
                   ct_ps[u].rearrange("p (h n) -> p h n", h=2), ACT.Copy).then_inc(s["ct"], 1)
                act.wait_ge(s["dp_mm"], t + (u + 1))
                act.wait_ge(s["slot_oh"], 3)
                for k in range(KC):
                    fn(xe_pair(0, k, t, u), dp(u, 0, k), ACT.Copy).then_inc(s["xe_hi"], 1)
            with act.Fori(0, NP // 2) as half_t:
                t = half_t * 2
                dispatch(t, 0)
                dispatch(t, 1)

            def ehidden(e, st):
                half, f = divmod(st, FC)
                n = len(TILES[half]) * 128
                act.wait_ge(s["m_mm"], e * 16 + (st + 1))
                b_ = eb1_now[:, f:f + 1]
                fn(egt[:, st % 4, 0:n], ps[:, st % 2, 0:n], ACT.Relu, bias=b_)
                fn(hid[:, st % 4, 0, 0:n], ps[:, st % 2, 0:n], ACT.Relu, bias=b_).then_inc(s["m_hi"], 1)

            def eout(e, half):
                for t in TILES[half]:
                    act.wait_ge(s["ev"], e * 5 + (t + 1))
                    if t == 4:
                        act.wait_ge(s["eo_st0"], e * 64 + 32)
                    elif not (isinstance(e, int) and e == 0):
                        act.wait_ge(s[f"eo_st{t}"], e * (64 if t == 0 else 32))
                    fn(eo[:, t % 4, 0, :], ev[:, t % 2, :], ACT.Copy).then_inc(s["eo_hi"], 1)

            def expert(e, fresh=False):
                if not fresh:
                    act.wait_ge(s["m_hi"], e * 16)
                act.wait_ge(s["consts"], 1)
                fn(eb1_now, eb1[:, ds(e * FC, FC)], ACT.Copy).then_inc(s["eb1"], 1)
                act.wait_ge(s["eb1"], e + 1)
                for st in range(16):
                    ehidden(e, st)
                    if st == 1 and not fresh:
                        eout(e - 1, 1)
                    if st == 9:
                        eout(e, 0)
            expert(0, True)
            with act.Fori(1, NE) as e:
                expert(e)
            eout(NE - 1, 1)

            for t in range(4):
                act.wait_ge(s[f"eo_st{t}"], 32 * NE * (2 if t == 0 else 1))
            for g in range(4):
                act.dma_start(ebf[0:SLOTS, g * 16 * 2 * D:(g + 1) * 16 * 2 * D].rearrange("p (b c) -> p b c", b=16),
                              eout_d[16 * g:16 * g + 16].rearrange("b e n c -> (e n) b c")).then_inc(s[f"fin_in{g}"], 16)

            def out_store(q, u):
                b = act.value_load(tbl[0:1, ds(q * 8 + (2 * u + 1 + T_PERM), 1)], min_val=0, max_val=B - 1)
                act.wait_ge(s["fin"], q * 4 + (u + 1))
                act.dma_start(a["out"][ds(b, 1)].rearrange("b p (k n) -> p (b k) n", k=KC),
                              yo[:, u, 1, :, :]).then_inc(s[f"fin_st{u}"], 16)
            with act.Fori(0, NP // 4) as q:
                for u in range(4):
                    out_store(q, u)

        @block.vector
        def _(dve):
            v = nc.vector
            links = [0]

            def link(ins):
                ins.then_inc(s["dve"], 1)
                links[0] += 1
                dve.wait_ge(s["dve"], links[0])

            dve.wait_ge(s["iotas"], 2)
            v.memset(ones, 1.0)
            link(v.tensor_scalar(upper[:, :], row[:, :], pidx[:, 0:1], None, ALU.is_gt))
            dve.wait_ge(s["small_in"], 32)
            link(v.tensor_copy(itok_f, itok_i))
            v.tensor_scalar(type_oh, row[0:B, 0:TYPES], itok_f, None, ALU.is_equal).then_inc(s["order_oh"], 1)
            gv = gate_vec.rearrange("p (t e) -> p t e", t=TYPES)
            link(v.reduce_max(gsum, gv, AX.X))
            v.tensor_tensor(gv, gv, gsum.unsqueeze(2).to_broadcast([128, TYPES, E2]), ALU.subtract).then_inc(s["soft_sub"], 1)
            dve.wait_ge(s["order_mm"], 1)
            v.memset(starts[:, 0:1], 0.0)
            link(v.tensor_copy(cnt, ps[:, 0, 0:TYPES]))
            v.tensor_copy(starts[:, 1:2], cnt[:, 0:1])
            link(v.tensor_tensor(starts[:, 2:3], cnt[:, 0:1], cnt[:, 1:2], ALU.add))
            link(v.tensor_tensor(tmp3[0:B, :], ps[0:B, 1, 0:TYPES], starts[0:B, :], ALU.add))
            link(v.tensor_tensor(tmp3[0:B, :], tmp3[0:B, :], type_oh, ALU.mult))
            link(v.reduce_sum(rank, tmp3[0:B, :], AX.X))
            v.tensor_scalar(batch_oh, row[0:B, 0:B], rank, None, ALU.is_equal).then_inc(s["order_oh"], 1)
            lt = scr[:, 0:3 * 16].rearrange("p (t j) -> p t j", t=TYPES)
            link(v.tensor_scalar(scr[:, 64:80], row[:, 0:16], float(GB), None, ALU.mult))
            link(v.tensor_tensor(lt, scr[:, 64:80].unsqueeze(1).to_broadcast([128, TYPES, 16]),
                                 cnt.unsqueeze(2).to_broadcast([128, TYPES, 16]), ALU.is_lt))
            link(v.reduce_sum(nchunks, lt, AX.X))
            dve.wait_ge(s["order_mm"], 2)
            v.tensor_copy(tbl[0:1, T_PERM:T_PERM + B], ps[0:1, 2, 0:B]).then_inc(s["perm"], 1)
            link(v.tensor_tensor(nchunks[:, 1:2], nchunks[:, 0:1], nchunks[:, 1:2], ALU.add))
            p0, p1, start, typ, t_ = (scr[:, 96 + 20 * j:116 + 20 * j] for j in range(5))
            v.tensor_scalar(p0, row[:, 0:20], nchunks[:, 0:1], None, ALU.is_ge)
            link(v.tensor_scalar(p1, row[:, 0:20], nchunks[:, 1:2], None, ALU.is_ge))
            link(v.tensor_tensor(typ, p0, p1, ALU.add))
            link(v.tensor_scalar(scr[:, 200:202], nchunks[:, 0:2], -float(GB), None, ALU.mult))
            link(v.tensor_tensor(scr[:, 200:202], scr[:, 200:202], starts[:, 1:3], ALU.add))
            link(v.tensor_tensor(scr[:, 201:202], scr[:, 201:202], scr[:, 200:201], ALU.subtract))
            link(v.tensor_scalar(start, row[:, 0:20], float(GB), None, ALU.mult))
            link(v.tensor_scalar(t_, p0, scr[:, 200:201], None, ALU.mult))
            link(v.tensor_tensor(start, start, t_, ALU.add))
            link(v.tensor_scalar(t_, p1, scr[:, 201:202], None, ALU.mult))
            link(v.tensor_tensor(start, start, t_, ALU.add))
            link(v.tensor_scalar(start, start, float(B), None, ALU.min))
            v.tensor_copy(tbl[:, T_POS:T_POS + 20], start)
            v.tensor_scalar(tbl[:, T_START:T_START + 20], start, float(S), None, ALU.mult)
            v.tensor_scalar(tbl[:, T_OFFC:T_OFFC + 20], typ, float(3 * SLOT), None, ALU.mult)
            v.tensor_scalar(tbl[:, T_OFFE:T_OFFE + 20], typ, float(2 * SLOT), None, ALU.mult).then_inc(s["tables"], 1)
            for i in range(3):
                dve.wait_ge(s["w_first_hi"], i + 1)
                v.scalar_tensor_tensor(w16(C_SHARE[i], 1, 0, MAT), first_stage[i], SW, w16(C_SHARE[i], 0, 0, MAT),
                                       ALU.mult, ALU.subtract).then_inc(s["w_first_lo"], 1)

            def x_group(g, u):
                dve.wait_ge(s["x_hi"], g + 1)
                v.scalar_tensor_tensor(xh[:, 1, :, ds(g * 512, 512)], xf[:, u, :, :], SX, xh[:, 0, :, ds(g * 512, 512)],
                                       ALU.mult, ALU.subtract).then_inc(s["x_lo"], 1)
            x_group(0, 0)
            x_group(1, 1)

            dve.wait_ge(s["soft_exp"], 1)
            link(v.reduce_sum(gsum, gv, AX.X))
            link(v.reciprocal(gsum, gsum))
            link(v.tensor_scalar(gsum, gsum, 1 / SO, None, ALU.mult))
            link(v.tensor_tensor(gv, gv, gsum.unsqueeze(2).to_broadcast([128, TYPES, E2]), ALU.mult))
            for e in range(2):
                link(v.tensor_scalar(t_, p0, -1.0, 1.0, ALU.mult, ALU.add))
                link(v.tensor_scalar(wab[:, e, :], t_, gv[:, 0, e:e + 1], None, ALU.mult))
                link(v.tensor_tensor(t_, p0, p1, ALU.subtract))
                link(v.scalar_tensor_tensor(wab[:, e, :], t_, gv[:, 1, 1 + e:2 + e], wab[:, e, :], ALU.mult, ALU.add))
                link(v.scalar_tensor_tensor(wab[:, e, :], p1, gv[:, 2, 2 + e:3 + e], wab[:, e, :], ALU.mult, ALU.add))

            v.memset(xh[:, :, :, NT:NTP], 0.0)
            link(v.tensor_scalar(ident[:, :], row[:, :], pidx[:, 0:1], None, ALU.is_equal))
            v.tensor_copy(ident16[:, :], ident[:, :])
            v.tensor_copy(identb[:, :], ident[:, :])
            link(v.tensor_copy(upperb[:, :], upper[:, :]))
            v.memset(upperb[0:64, 64:128], 0.0)
            link(v.tensor_scalar(half_mask[:, 1:2], pidx[:, 0:1], 64.0, None, ALU.is_ge))
            v.tensor_scalar(half_mask[:, 0:1], half_mask[:, 1:2], -1.0, 1.0, ALU.mult, ALU.add)
            link(v.scalar_tensor_tensor(gsum[:, 0:1], half_mask[:, 1:2], -64.0, pidx[:, 0:1], ALU.mult, ALU.add))
            link(v.tensor_scalar(scr[:, 0:64], row[:, 0:64], gsum[:, 0:1], MASKED, ALU.is_gt, ALU.mult))
            v.tensor_copy(causal[:, :, :], scr[:, 0:64].unsqueeze(1).to_broadcast([128, 8, S]))
            link(v.tensor_scalar(t_[:, 0:8], row[:, 0:8], float(HD), pidx[:, 0:1], ALU.mult, ALU.subtract))
            v.tensor_scalar(typ[:, 0:8], t_[:, 0:8], -float(HD), None, ALU.is_gt)
            link(v.tensor_scalar(t_[:, 0:8], t_[:, 0:8], 0.0, None, ALU.is_le))
            v.tensor_tensor(head_mask[:, :], t_[:, 0:8], typ[:, 0:8], ALU.mult)
            dve.wait_ge(s["bias_in"], 32)
            v.tensor_scalar(bias[:, 0:6], bias[:, 0:6], SQ, None, ALU.mult)
            v.tensor_scalar(bias[:, 8:88], bias[:, 8:88], SR, None, ALU.mult).then_inc(s["consts"], 1)

            def ffn(p):
                def hidden(i, st):
                    bank, col = p.bank(st, 1 if p.gated else 0)
                    src, n = ps[:, bank, col:col + p.n], i * 16 + (st + 1)
                    if p.gated:
                        dve.wait_ge(p.g, n)
                        v.tensor_tensor(p.fbuf(st), src, p.gbuf(st), ALU.mult).then_inc(p.mul, 1)
                        dve.wait_ge(p.hi, n)
                        v.tensor_tensor(hid[:, st % 4, 1, 0:p.n], p.fbuf(st), hid[:, st % 4, 0, 0:p.n],
                                        ALU.subtract).then_inc(p.h, 1)
                    else:
                        dve.wait_ge(p.hi, n)
                        v.scalar_tensor_tensor(hid[:, st % 4, 1, 0:p.n], src, 0.0, hid[:, st % 4, 0, 0:p.n],
                                               ALU.max, ALU.subtract).then_inc(p.h, 1)

                def evacuate(i, half):
                    if p.two_experts:
                        if half == 0:
                            return
                        dve.wait_ge(p.l2, i * 2 + 2)
                        dve.wait_ge(p.ev, i * 2 + 1)
                        v.scalar_tensor_tensor(outb[:, :, 0:p.n], ps[:, 6:8, 0:p.n], wab[:, 1, ds(i, 1)],
                                               outb[:, :, 0:p.n], ALU.mult, ALU.add).then_inc(p.ev, 1)

                def feature(i, half):
                    if p.two_experts:
                        if half == 0:
                            return
                        dve.wait_ge(p.ev, i * 2 + 2)
                    else:
                        dve.wait_ge(p.ev, i * 2 + (half + 1))
                    nb = p.n // S
                    if p.dynamic:
                        c = i if p.two_experts else i * 2 + half
                        b0 = dve.value_load(tbl[0:1, ds(c + T_POS, 1)], min_val=0, max_val=B)
                    else:
                        b0 = (i * 2 + half) * nb
                    v.tensor_copy(gate_in[:, p.feat, :, ds(b0, nb)], outb[:, :, 0:p.n:S]).then_inc(p.feat_done, 1)

                def body(i, first, lastone):
                    for st in range(16):
                        hidden(i, st)
                        if st == 1 and not first:
                            evacuate(i - 1, 1)
                        if st == 9:
                            evacuate(i, 0)
                        if st == 3 and not first:
                            feature(i - 1, 1)
                        if st == 11:
                            feature(i, 0)
                        if p is cs and not lastone and st in (3, 11):
                            x_group(i * 2 + (2 if st == 3 else 3), 0 if st == 3 else 1)
                body(0, True, False)
                with dve.Fori(1, p.iters - 1) as i:
                    body(i, False, False)
                body(p.iters - 1, False, True)
                evacuate(p.iters - 1, 1)
                feature(p.iters - 1, 1)

            def gate(n_out, turn):
                dve.wait_ge(s["gw_in"], 32 * turn)
                for j in range(n_out):
                    last = v.tensor_copy(gate_rep[:, j, :, :], (gate_w2 if turn == 2 else gate_w2c)[:, :, j:j + 1]
                                         .to_broadcast([128, 2, 128]))
                last.then_inc(s["gate_rdy"], 1)
                dve.wait_ge(s["gate_mm"], 2 * turn - 1)
                v.tensor_scalar(gate_hid, ps[:, 0:2, 0:B], 0.0, None, ALU.max).then_inc(s["gate_rdy"], 1)
                dve.wait_ge(s["gate_mm"], 2 * turn)
                logits = ps[:, 2, 0:n_out * B].rearrange("p (j b) -> p b j", j=n_out)
                g = gates[:, :, 0:n_out]
                over_j = gate_mx.unsqueeze(2).to_broadcast([128, B, n_out])
                link(v.reduce_max(gate_mx, logits, AX.X))
                v.tensor_tensor(g, logits, over_j, ALU.subtract).then_inc(s["soft_sub"], 1)
                dve.wait_ge(s["soft_exp"], 1 + turn)
                link(v.reduce_sum(gate_mx, g, AX.X))
                link(v.reciprocal(gate_mx, gate_mx))
                link(v.tensor_tensor(g, g, over_j, ALU.mult))
                dve.sem_inc(s["gates"], 1)

            ffn(cs)
            ffn(ce)
            gate(2, 1)

            def y_low(c):
                dve.wait_ge(s["y_hi"], c + 1)
                two = yd[:, :, :, :, :, :].rearrange("p h k b r n -> p h (k b) r n")
                for twice in range(2):
                    last = v.scalar_tensor_tensor(two[:, 1, :, twice, :], ex.rearrange("p k (b n) -> p (k b) n", b=GB), SY,
                                                  two[:, 0, :, twice, :], ALU.mult, ALU.subtract)
                last.then_inc(s["y_lo"], 1)

            def softmax_shift(c, r):
                dve.wait_ge(s["s_mm"], c * 2 + (r - 1))
                sc = ps[:, 2 * r:2 * r + 2, :].rearrange("p a (h n) -> p (a h) n", n=S)
                v.reduce_max(mx[:, r, :], sc, AX.X).then_inc(s["mx"], 1)
                dve.wait_ge(s["mx"], c * 2 + (r - 1))
                v.tensor_tensor(heads(prob[:, r, :]), sc, mx[:, r, :].unsqueeze(2).to_broadcast([128, H, S]),
                                ALU.subtract).then_inc(s["sub"], 1)

            def softmax_sum(c, r):
                dve.wait_ge(s["exp"], c * 2 + (r - 1))
                v.reduce_sum(sm[:, r, :], heads(prob[:, r, :]), AX.X).then_inc(s["norm"], 1)
                dve.wait_ge(s["norm"], c * 4 + (2 * r - 3))
                v.reciprocal(rs[:, r, :], sm[:, r, :]).then_inc(s["norm"], 1)

            def qk_low(c, w, dst):
                dve.wait_ge(s["qk_hi"], c * 2 + (w + 1))
                for m in range(KC):
                    last = v.scalar_tensor_tensor(dst[:, 1, m, :], ps[:, 4 + w, m * CH:(m + 1) * CH],
                                                  ab[:, w, m:m + 1], dst[:, 0, m, :], ALU.add, ALU.subtract)
                last.then_inc(s["qk_lo"], 1)

            def attn(c, new, old, fin, more):
                if old:
                    softmax_shift(c, 0)
                    softmax_shift(c, 1)
                if fin:
                    dve.wait_ge(s["wo_mm"], c - 1)
                    dve.wait_ge(s["xb"], c - 1)
                    if not isinstance(c, int) or c >= 3:
                        dve.wait_ge(s["x1_lo"], c - 2)
                        dve.wait_ge(s["x1_out"], c * 16 - 32)
                    v.scalar_tensor_tensor(x1.rearrange("p k n -> p (k n)"), ps[:, 5, :], 1 / (SQ * SA),
                                           xin.rearrange("p k n -> p (k n)"), ALU.mult, ALU.add).then_inc(s["x1"], 1)
                if old:
                    softmax_sum(c, 0)
                if fin:
                    dve.wait_ge(s["x1_hi"], c - 1)
                    cols = ds((c - 2) * CH, CH)
                    v.scalar_tensor_tensor(xh[:, 1, :, cols], x1, SX, xh[:, 0, :, cols],
                                           ALU.mult, ALU.subtract).then_inc(s["x1_lo"], 1)
                if new:
                    qk_low(c, 0, qh)
                if old:
                    softmax_sum(c, 1)
                if new:
                    qk_low(c, 1, kh)
                    dve.wait_ge(s["qk_lo"], c * 2 + 2)
                    for h in range(KBD_DVE):
                        last = v.tensor_scalar(kbd_head(h), kh_batches, head_mask[:, h:h + 1], None, ALU.mult)
                    last.then_inc(s["kbd"], 1)
                if old:
                    for r in range(2):
                        for hb in range(2):
                            dve.wait_ge(s["pt_hi"], c * 4 + (2 * r + hb - 3))
                            cols = slice(hb * 512, (hb + 1) * 512)
                            v.tensor_tensor(pt[:, r, 1, cols], ps[:, 2 * r + hb, :], pt[:, r, 0, cols],
                                            ALU.subtract).then_inc(s["pt_lo"], 1)
                if more:
                    y_low(c + 1)
                if old:
                    dve.wait_ge(s["o_hi"], c)
                    for m in range(KC):
                        last = v.scalar_tensor_tensor(oh_[:, 1, m, :], ps[:, 4, m * CH:(m + 1) * CH], ab[:, 2, m:m + 1],
                                                      oh_[:, 0, m, :], ALU.add, ALU.subtract)
                    last.then_inc(s["o_lo"], 1)
                if new:
                    dve.wait_ge(s["v_hi"], c + 1)
                    for r in range(2):
                        for j in range(2):
                            last = v.scalar_tensor_tensor(vb(1, r, j), vp(r, j), half_mask[:, j:j + 1], vb(0, r, j),
                                                          ALU.mult, ALU.subtract)
                    last.then_inc(s["v_lo"], 1)

            y_low(0)
            attn(0, True, False, False, True)
            attn(1, True, True, False, True)
            with dve.Fori(2, NA - 1) as c:
                attn(c, True, True, True, True)
            attn(NA - 1, True, True, True, False)
            attn(NA, False, True, True, False)
            attn(NA + 1, False, False, True, False)

            for p in es:
                ffn(p)
            ffn(ee)
            gate(4, 2)

            dve.wait_ge(s["w3_in"], 16)
            raw = misc[:, 2400:2464].rearrange("p (f e) -> p f e", f=FC)
            link(v.tensor_scalar(w3[:, 0, :, :], raw, SW, None, ALU.mult))
            v.scalar_tensor_tensor(w3[:, 1, :, :], raw, SW, w3[:, 0, :, :], ALU.mult, ALU.subtract).then_inc(s["w3"], 1)

            def z_make(k):
                dve.wait_ge(s["z_in"], k * 64 + 64)
                for j in range(4):
                    last = weighted(v, zsrc[:, j, :, :], k * GB, GB, j)
                last.then_inc(s["zchain"], 1)
                dve.wait_ge(s["zchain"], k * 2 + 1)
                v.tensor_tensor(zsrc[:, 0:2, :, :].rearrange("p j k n -> p j (k n)"),
                                zsrc[:, 0:2, :, :].rearrange("p j k n -> p j (k n)"),
                                zsrc[:, 2:4, :, :].rearrange("p j k n -> p j (k n)"), ALU.add).then_inc(s["zchain"], 1)
                dve.wait_ge(s["zchain"], k * 2 + 2)
                v.tensor_tensor(zsrc[:, 0, :, :], zsrc[:, 0, :, :], zsrc[:, 1, :, :], ALU.add).then_inc(s["z_sum"], 1)
                dve.wait_ge(s["z_hi"], k + 1)
                cols = ds(k * CH, CH)
                v.scalar_tensor_tensor(xh[:, 1, :, cols], zsrc[:, 0, :, :], SZ, xh[:, 0, :, cols],
                                       ALU.mult, ALU.subtract).then_inc(s["z_lo"], 1)

            def logits(c):
                dve.wait_ge(s["l_mm"], c + 1)
                v.scalar_tensor_tensor(logit[:, ds(c * 4, 4), :], ps[:, 6, 0:4 * NE].rearrange("p (t e) -> p t e", t=4),
                                       1 / (SR * SW), rb3.unsqueeze(1).to_broadcast([128, 4, NE]),
                                       ALU.mult, ALU.add).then_inc(s["logit"], 1)

            def router(c, previous, more):
                for st in range(16):
                    dve.wait_ge(s["r_hi"], c * 16 + (st + 1))
                    dst = h1[:, st, :, :] if st < FC else h2[:, st - FC, :, :]
                    v.tensor_tensor(dst[:, 1, :], gt[:, (st % 2) * 512:(st % 2 + 1) * 512], dst[:, 0, :],
                                    ALU.subtract).then_inc(s["r_lo"], 1)
                    if previous and st == 7:
                        logits(c - 1)
                    if more and st in (8, 11):
                        z_make(c * 2 + (2 if st == 8 else 3))
            z_make(0)
            z_make(1)
            router(0, False, True)
            with dve.Fori(1, 7) as c:
                router(c, True, True)
            router(7, True, False)
            logits(7)

            def over_e(x):
                return x.unsqueeze(2).to_broadcast([128, NP, NE])
            m1 = top8[:, :, 0:1].rearrange("p t e -> p (t e)")
            dve.wait_ge(s["logit"], 8)
            link(v.reduce_max(m1, logit, AX.X))
            v.tensor_tensor(score, logit, over_e(m1), ALU.subtract).then_inc(s["soft_sub"], 1)
            dve.wait_ge(s["soft_exp"], 4)
            link(v.reduce_sum(m1, score, AX.X))
            link(v.reciprocal(m1, m1))
            link(v.tensor_tensor(score, score, over_e(m1), ALU.mult))
            for t in range(NP):
                last = v.max(top8[:, t, :], score[:, t, :])
            link(last)
            for t in range(NP):
                last = v.max_index(index8[:, t, :], top8[:, t, :], score[:, t, :])
            link(last)
            experts = row[:, 0:NE].unsqueeze(1).to_broadcast([128, NP, NE])
            link(v.tensor_copy(pos, index8))
            for n, o in enumerate((oh0, oh1)):
                last = v.tensor_tensor(o, experts, over_e(pos[:, :, n:n + 1].rearrange("p t e -> p (t e)")), ALU.is_equal)
            link(last)
            link(v.tensor_tensor(oh0, oh0, oh1, ALU.add))
            v.tensor_copy(oh16, oh0).then_inc(s["oh"], 1)
            dve.wait_ge(s["pos_mm"], 1)
            flat = lambda x: x.rearrange("p t e -> p (t e)")
            link(v.tensor_copy(flat(pos), ps[:, 0, 0:NP * NE]))
            te = lambda x: flat(x).unsqueeze(2).to_broadcast([128, NP * NE, CAP])
            dt = dtmp.rearrange("p t (e n) -> p (t e) n", n=CAP)
            link(v.tensor_tensor(dt, te(pos), row[:, 0:CAP].unsqueeze(1).to_broadcast([128, NP * NE, CAP]), ALU.is_equal))
            v.tensor_tensor(dt, dt, te(oh0), ALU.mult).then_inc(s["slot_oh"], 1)
            dve.wait_ge(s["d01"], 1)
            v.tensor_tensor(dt, dt, te(score), ALU.mult).then_inc(s["slot_oh"], 1)
            dve.wait_ge(s["d01"], 2)
            dve.wait_ge(s["slot_oh"], 2)
            v.scalar_tensor_tensor(dsc[:, 1, :, :], dtmp, SCW, dsc[:, 0, :, :], ALU.mult, ALU.subtract
                                   ).then_inc(s["slot_oh"], 1)

            def dispatch(t, u):
                dve.wait_ge(s["zt_mm"], t + (u + 1))
                v.tensor_copy(ztok[:, u, :, :, :].rearrange("p h k n -> p (h k n)"), zt_ps[u]).then_inc(s["zt"], 1)
                dve.wait_ge(s["dp_mm"], t + (u + 1))
                for k in range(KC):
                    v.tensor_copy(xe_pair(1, k, t, u), dp(u, 1, k)).then_inc(s["xe_lo"], 1)
            with dve.Fori(0, NP // 2) as half_t:
                t = half_t * 2
                dispatch(t, 0)
                dispatch(t, 1)

            dve.wait_ge(s["eb2_in"], 16)
            v.tensor_scalar(misc[:, 4608:6656], misc[:, 4608:6656], SEO, None, ALU.mult).then_inc(s["eb2"], 1)
            dve.wait_ge(s["eb2"], 1)

            def eout(e, half):
                for t in TILES[half]:
                    dve.wait_ge(s["m_out"], e * 2 + (half + 1))
                    if t >= 2:
                        dve.wait_ge(s["eo_lo"], e * 5 + (t - 1))
                    elif t == 0 and not (isinstance(e, int) and e == 0):
                        dve.wait_ge(s["eo_lo"], e * 5)
                    v.scalar_tensor_tensor(ev[:, t % 2, :], ps[:, 3 + t, 0:D], SEO / (SR * SW), misc[:, ds(e * D + 4608, D)],
                                           ALU.mult, ALU.add).then_inc(s["ev"], 1)
                    dve.wait_ge(s["eo_hi"], e * 5 + (t + 1))
                    v.tensor_tensor(eo[:, t % 4, 1, :], ev[:, t % 2, :], eo[:, t % 4, 0, :], ALU.subtract).then_inc(s["eo_lo"], 1)

            def expert(e, par, fresh=False, lastone=False):
                for st in range(16):
                    n = len(TILES[st // FC]) * 128
                    dve.wait_ge(s["m_hi"], e * 16 + (st + 1))
                    v.tensor_tensor(hid[:, st % 4, 1, 0:n], egt[:, st % 4, 0:n],
                                    hid[:, st % 4, 0, 0:n], ALU.subtract).then_inc(s["m_lo"], 1)
                    if st == 1 and not fresh:
                        eout(e - 1, 1)
                    if st == 9:
                        eout(e, 0)
                    if st in (6, 12) and not lastone:
                        w, slot = (0, MOE_W[1 - par][0]) if st == 6 else (1, MOE_W[1 - par][1])
                        dve.wait_ge(s["mw_hi"], e * 2 + (w + 1))
                        v.scalar_tensor_tensor(w16(slot, 1, 0, MAT), wstage[:, (FIRST_MOE + w) % 2, :], SW,
                                               w16(slot, 0, 0, MAT), ALU.mult, ALU.subtract).then_inc(s["mw_lo"], 1)
            expert(0, 0, fresh=True)
            expert(1, 1)
            with dve.Fori(1, NE // 2 - 1) as half_e:
                e = half_e * 2
                expert(e, 0)
                expert(e + 1, 1)
            expert(NE - 2, 0)
            expert(NE - 1, 1, lastone=True)
            eout(NE - 1, 1)

            def output(q, u):
                dve.wait_ge(s["fin_mm"], q * 4 + (u + 1))
                if not (isinstance(q, int) and q == 0):
                    dve.wait_ge(s[f"fin_st{u}"], q * 32)
                for b2 in range(2):
                    last = v.scalar_tensor_tensor(yo[:, u, b2, :, :],
                                                  ps[:, u, b2 * 128:(b2 + 1) * 128].rearrange("p (k n) -> p k n", k=KC),
                                                  1 / (SEO * SCW), x1f[:, :, ds(q * 512 + (2 * u + b2) * S, S)],
                                                  ALU.mult, ALU.add)
                last.then_inc(s["fin"], 1)
            dve.wait_ge(s["x1_in"], 16)
            for u in range(4):
                output(0, u)
            with dve.Fori(1, NP // 4) as q:
                for u in range(4):
                    output(q, u)


_NAMES = ("itok", "gv", "bias", "rb3", "x", "c_swi0", "c_swi1", "c_swo", "c_wi0", "c_wi1", "c_wo", "c_g0", "c_g1",
          "a_w", "e_wi", "e_wo", "e_swi", "e_swo", "e_g1", "e_g2", "r_w1", "r_w2", "r_w3", "m_w1", "m_w2", "eb2")


def kernel(**inputs):
    import concourse.bacc as bacc
    from concourse.bass_utils import run_bass_kernel_spmd

    g = {k.replace("L0_", ""): np.asarray(v) for k, v in inputs.items()}

    def rows(w):
        *lead, r, n = w.shape
        return np.ascontiguousarray(np.moveaxis(w.reshape(*lead, r // 128, 128, n), -2, -3)).reshape(*lead, 128, -1)

    def cols(b):
        return np.moveaxis(b.reshape(-1, b.shape[-1] // 128, 128), -1, 0).reshape(128, -1)

    arrays = {
        "itok": g["itok_B_0_2"].astype(np.int32).reshape(B, 1),
        "gv": g["cond2_gate_vecs"].reshape(-1),
        "bias": np.concatenate([cols(g[n]) for n in ("attn_bq", "attn_bk", "attn_bv", "attn_bo", "ffn_rb1", "ffn_rb2",
                                                     "ffn_eb1")], axis=1),
        "rb3": g["ffn_rb3"],
        "x": g["x"].reshape(B, S, KC, 128).transpose(0, 3, 2, 1).reshape(B, 128, KC * S),
        "c_swi0": rows(g["cond_sWi0"]), "c_swi1": rows(g["cond_sWi1"]), "c_swo": rows(g["cond_sWo"]),
        "c_wi0": rows(g["cond_Wi0"]), "c_wi1": rows(g["cond_Wi1"]), "c_wo": rows(g["cond_Wo"]),
        "c_g0": rows(g["cond_g0"]), "c_g1": rows(g["cond_g1"]),
        "a_w": np.concatenate([rows(g[f"attn_W{c}"].T) for c in "qkvo"], axis=1),
        "e_wi": rows(g["cond2_expert_wi"]), "e_wo": rows(g["cond2_expert_wo"]),
        "e_swi": rows(g["cond2_share_wi"]), "e_swo": rows(g["cond2_share_wo"]),
        "e_g1": rows(g["cond2_gate_w1"]), "e_g2": rows(g["cond2_gate_w2"]),
        "r_w1": rows(g["ffn_rW1"]), "r_w2": rows(g["ffn_rW2"].reshape(4, 2 * 128, F)), "r_w3": rows(g["ffn_rW3"]),
        "m_w1": rows(g["ffn_eW1"]), "m_w2": rows(g["ffn_eW2"]),
        "eb2": g["ffn_eb2"].reshape(-1),
    }
    nc = bacc.Bacc("TRN2", target_bir_lowering=False, num_devices=1)
    feeds, a = {}, {}
    for n in _NAMES:
        arr = np.ascontiguousarray(arrays[n])
        feeds[f"in_{n}"] = arr
        a[n] = nc.dram_tensor(f"in_{n}", arr.shape, mybir.dt.from_np(arr.dtype), kind="ExternalInput").ap()
    a["out"] = nc.dram_tensor("out_x", (B, 128, KC * S), F32, kind="ExternalOutput").ap()
    build(nc, a)
    got = np.asarray(run_bass_kernel_spmd(nc, [feeds], core_ids=[0]).results[0]["out_x"])
    return np.ascontiguousarray(got.reshape(B, 128, KC, S).transpose(0, 3, 2, 1)).reshape(B, S, D)
```

```python
import numpy as np
import concourse.bass as bass
from concourse import mybir
from contextlib import ExitStack

F32, F16, BF16, I32, U32 = (mybir.dt.float32, mybir.dt.float16, mybir.dt.bfloat16,
                            mybir.dt.int32, mybir.dt.uint32)
ALU = mybir.AluOpType
ACT = mybir.ActivationFunctionType
AX = mybir.AxisListType
ds = bass.ds

B, S, D, F = 64, 64, 256, 1024
NT = B * S
KC, FC = D // 128, F // 128
H, HD = 16, 16
TYPES, E2 = 3, 4
NE, CAP = 8, int(S / 8 * 1.25)
GB = 4
CH = GB * S
NCH = (B + TYPES * (GB - 1)) // GB
NTP = NT + CH
MAT = 2048
SLOT = 2 * MAT
NSLOT = 15
SLOTS = NE * CAP
NA = B // GB
NP = B // 2
FIRST_MOE = 31
TILES = ((0, 1, 2), (3, 4))
PER_E = B * CAP

SX, SW = 4.0, 64.0
SH = SX * SW
SO = SH * SW
SY, SA = 16.0, 16.0
SQ = SY * SA
SZ = 8.0
SR = SZ * SW
SEO, SCW = 64.0, 16.0
MASKED = -1e30
FIN_ST = (0, 0, 1, 1, 2, 2, 2, 3)
KBD_DVE = 6

C_SHARE = (0, 1, 2)
C_EXP = 3
E_SHARE = ((12, 13), (1, 2), (11, 14))
E_EXP = 3
ATTN_W = 0
R_W1, R_W2 = 0, (12, 13, 1, 2)
MOE_W = ((11, 14), (10, 0))
ATTN_WORK = 3
HID_SLOT = 14
H1_SLOT, H2_SLOT, ZSRC_SLOT = 3, 5, 7
XE_SLOT, CT_SLOT, SEL_SLOT = 3, 8, 10


def build(nc, a):
    ctx = ExitStack()
    with ctx:
        def sb(name, shape, dt):
            return ctx.enter_context(nc.sbuf_tensor(name, shape, dt))

        def sem(name):
            return ctx.enter_context(nc.semaphore(name))

        def scratch(name, shape, dt):
            return nc.dram_tensor(name, shape, dt, kind="Internal").ap()

        arena = sb("arena", [128, NSLOT * SLOT], F16)
        xh = sb("xh", [128, 2, KC, NTP], F16)
        wstage = sb("wstage", [128, 2, MAT], F32)
        misc = sb("misc", [128, 6656], F32)
        row = sb("row", [128, 128], F32)
        pidx = sb("pidx", [128, 1], F32)
        ident = sb("ident", [128, 128], F32)
        ident16 = sb("ident16", [128, 128], F16)
        identb = sb("identb", [128, 128], BF16)
        upper = sb("upper", [128, 128], F32)
        upperb = sb("upperb", [128, 128], BF16)
        causal = sb("causal", [128, 8, S], BF16)
        head_mask = sb("head_mask", [128, 8], F32)
        half_mask = sb("half_mask", [128, 2], F32)
        tbl = sb("tbl", [128, 148], I32)
        wab = sb("wab", [128, 2, 20], F32)
        small = sb("small", [128, 232], F32)
        gate_in = sb("gate_in", [128, 4, KC, B + GB], F32)
        gates = sb("gates", [128, B, 4], F32)
        bias = sb("bias", [128, 8 + 16 + 64], F32)

        outb = misc[:, 0:1024].rearrange("p (m n) -> p m n", m=2)
        gt = misc[:, 1024:2048]
        hid = misc[:, 2560:4608].bitcast(F16).rearrange("p (s h n) -> p s h n", s=4, h=2)
        xf = misc[:, 4608:6656].rearrange("p (u k n) -> p u k n", u=2, k=KC)

        ps = ctx.enter_context(nc.psum_tensor("ps", [128, 8, 512], F32))

        def region(slot, nbytes, dt, at=0):
            lo = slot * SLOT + at // 2
            v = arena[:, lo:lo + nbytes // 2]
            return v if dt == F16 else v.bitcast(dt)

        hidden_f32 = region(HID_SLOT, 4096, F32)
        first_stage = [region(11 + i, 8192, F32) for i in range(3)]
        at = [0]

        def attn_buf(nbytes, dt):
            v = region(ATTN_WORK, nbytes, dt, at[0])
            at[0] += nbytes
            assert at[0] <= 8 * SLOT * 2
            return v
        ex = attn_buf(2048, F32).rearrange("p (k n) -> p k n", k=KC)
        sh = attn_buf(2048, F32).rearrange("p (k n) -> p k n", k=KC)
        xin = attn_buf(2048, F32).rearrange("p (k n) -> p k n", k=KC)
        x1 = attn_buf(2048, F32).rearrange("p (k n) -> p k n", k=KC)
        yd = attn_buf(4096, F16).rearrange("p (h k b r n) -> p h k b r n", h=2, k=KC, b=GB, r=2)
        qh = attn_buf(2048, F16).rearrange("p (h k n) -> p h k n", h=2, k=KC)
        kh = attn_buf(2048, F16).rearrange("p (h k n) -> p h k n", h=2, k=KC)
        kbd = attn_buf(16384, F16).rearrange("p (h m b e n) -> p h m b e n", h=2, m=KC, b=GB, e=8)
        vbd = attn_buf(4096, F16).rearrange("p (h b c) -> p h b c", h=2, b=GB)
        prob = attn_buf(8192, F32).rearrange("p (r n) -> p r n", r=2)
        pt = attn_buf(8192, F16).rearrange("p (r h n) -> p r h n", r=2, h=2)
        oh_ = attn_buf(2048, F16).rearrange("p (h k n) -> p h k n", h=2, k=KC)

        def vp(r, j):
            return ps[:, 6 + r, :].rearrange("p (g c) -> p g c", c=2 * HD)[:, :, j * HD:(j + 1) * HD]

        def vb(part, r, j):
            return vbd[:, part, 2 * r:2 * r + 2, :].rearrange("p b (g c) -> p (b g) c", c=2 * HD)[
                :, :, j * HD:(j + 1) * HD]
        mx = small[:, 0:32].rearrange("p (r n) -> p r n", r=2)
        sm = small[:, 32:64].rearrange("p (r n) -> p r n", r=2)
        rs = small[:, 64:96].rearrange("p (r n) -> p r n", r=2)

        h1 = region(H1_SLOT, 16384, F16).rearrange("p (f h n) -> p f h n", f=FC, h=2)
        h2 = region(H2_SLOT, 16384, F16).rearrange("p (f h n) -> p f h n", f=FC, h=2)
        zsrcs = region(ZSRC_SLOT, 16384, F32).rearrange("p (u j k n) -> p u j k n", u=2, j=4, k=KC)
        w3 = small[:, 128:192].bitcast(F16).rearrange("p (f c) -> p f c", f=FC)
        def sel(i):
            return region(SEL_SLOT, 1024, F32, 1024 * i).rearrange("p (t e) -> p t e", t=NP)
        logit, score, top8, oh0, oh1, pos = (sel(i) for i in range(6))
        index8 = region(SEL_SLOT, 1024, U32, 1024 * 6).rearrange("p (t e) -> p t e", t=NP)
        oh16 = region(SEL_SLOT, 512, BF16, 1024 * 7).rearrange("p (t e) -> p t e", t=NP)
        d01 = misc[:, 0:2560].bitcast(F16).rearrange("p (t b s) -> p t b s", t=NP, b=2)
        dsc = misc[:, 2560:5120].bitcast(F16).rearrange("p (h t s) -> p h t s", h=2, t=NP)
        ztok = misc[:, 5120:5632].bitcast(F16).rearrange("p (u h k n) -> p u h k n", u=2, h=2, k=KC)
        dtmp = region(XE_SLOT, 10240, F32).rearrange("p (t s) -> p t s", t=NP)
        dtmp2 = region(XE_SLOT + 2, 10240, F32).rearrange("p (t s) -> p t s", t=NP)
        xe = region(XE_SLOT, 40960, F16).rearrange("p (h k n) -> p h k n", h=2, k=KC)
        ct = region(CT_SLOT, 16384, F16).rearrange("p (h t n) -> p h t n", h=2, t=NP)
        eo = misc[:, 0:1024].bitcast(F16).rearrange("p (u h n) -> p u h n", u=4, h=2)
        ev = misc[:, 2048:2048 + 2 * D].rearrange("p (u n) -> p u n", u=2)
        zt_ps = [ps[:, u, 0:256].bitcast(F16) for u in range(2)]
        ct_ps = [ps[0:SLOTS, 6 + u, 0:128].bitcast(F16) for u in range(2)]

        def xe_pair(part, k, t, u):
            v = xe[:, part, k, :].rearrange("p (e n b) -> p e b n", e=NE, n=CAP)
            return v[:, :, ds((t + u) * 2, 2), :]

        def dp(u, part, k):
            return ps[:, 2 + 2 * u + part, k * 2 * SLOTS:(k + 1) * 2 * SLOTS].rearrange(
                "p (b e n) -> p e b n", b=2, e=NE)
        ebf = region(0, B * 2 * D * 2, F16)
        x1f = xh[:, :, :, :].rearrange("p h k n -> p (h k n)").bitcast(F32)[:, 0:KC * NT].rearrange(
            "p (k n) -> p k n", k=KC)
        yo = misc[:, 3072:5120].rearrange("p (u b k n) -> p u b k n", u=8, b=2, k=KC)
        egt = region(1, 4 * 384 * 4, F32).rearrange("p (u n) -> p u n", u=4)

        ab = bias[:, 0:8].rearrange("p (w k) -> p w k", w=4)
        rb1, rb2 = bias[:, 8:16], bias[:, 16:24]
        eb1 = bias[:, 24:88]
        rb3 = small[:, 96:104]
        part_sum = small[:, 0:4 * NE].rearrange("p (t e) -> p t e", t=4)
        slot_row = small[:, 112:122]
        eb1_now = small[:, 104:112]
        itok_i, itok_f, rank = small[0:B, 192:193].bitcast(I32), small[0:B, 193:194], small[0:B, 194:195]
        gate_vec, type_oh, cnt = small[:, 196:208], small[0:B, 208:211], small[:, 212:215]
        starts, nchunks = small[:, 216:219], small[:, 220:223]
        gsum, tmp3 = small[:, 224:227], small[:, 228:231]
        scr = misc[:, 256:512]
        ones = misc[:, 0:128]
        batch_oh = misc[0:B, 128:192]
        gate_w1 = misc[:, 4608:6656].rearrange("p (k n) -> p k n", k=4 * KC)
        gate_w2 = misc[:, 1024:1032].rearrange("p (k j) -> p k j", k=2)
        gate_w2c = misc[:, 1024:1028].rearrange("p (k j) -> p k j", k=2)
        gate_hid = misc[:, 2048:2176].rearrange("p (k n) -> p k n", k=2)
        gate_rep = misc[:, 2560:3584].rearrange("p (j k n) -> p j k n", j=4, k=2)
        gate_mx = misc[:, 2304:2368]
        T_START, T_OFFC, T_OFFE, T_POS, T_PERM = 0, 20, 40, 64, 84

        cshare_d = scratch("cshare_d", [128, KC, NTP], F32)
        cexp_d = scratch("cexp_d", [128, KC, NTP], F32)
        x1_d = scratch("x1_d", [128, KC, NT], F32)
        src_d = [scratch(f"src{j}_d", [128, KC, NTP], F32) for j in range(4)]
        eout_d = scratch("eout_d", [B, NE, CAP, 2 * D], F16)

        s = {n: sem(n) for n in (
            "iotas", "dve", "small_in", "bias_in", "order_oh", "order_mm", "soft_sub", "soft_exp",
            "tables", "perm", "consts",
            "w_first_in0", "w_first_in1", "w_first_in2", "w_first_hi", "w_first_lo", "w_in", "wchain", "mw_hi", "mw_lo", "w_ready", "x_half", "x_in0", "x_in1", "x_hi", "x_lo",
            "gw_in", "gate_mm", "gate_rdy", "gates",
            "exsh_in", "y_mul", "y_sum", "y_hi", "y_lo", "qk_mm", "qk_hi", "qk_lo", "kbd", "kbd_act", "s_mm",
            "mx", "sub", "exp", "norm", "p_ready", "t_mm", "pt_hi", "pt_lo", "pv_mm", "o_hi", "o_lo",
            "v_mm", "v_hi", "v_lo", "wo_mm", "xin_in", "xb", "x1", "x1_hi", "x1_lo", "x1_out",
            "z_in0", "z_in1", "zchain", "z_sum", "z_hi", "z_lo", "r_mm", "r_hi", "r_lo", "l_mm", "lpart", "logit",
            "w3_in", "w3",
            "oh", "pos_mm", "slot_oh", "d01", "zt_mm", "zt", "dp_mm", "xe_hi", "xe_lo", "ct_mm", "ct",
            "eb1", "eb2_in", "m_mm", "m_hi", "m_lo", "m_out", "ev", "eo_hi", "eo_lo", "eo_st0", "eo_st1", "eo_st2", "eo_st3",
            "fin_in0", "fin_in1", "fin_in2", "fin_in3", "fin_mm", "fin", "fin_st0", "fin_st1", "fin_st2", "fin_st3", "x1_in")}

        class FfnPass:
            def __init__(self, name, iters, n, gated, dynamic, two_experts, slots, need_w, out_d, feat):
                self.name, self.iters, self.n, self.gated = name, iters, n, gated
                self.dynamic, self.two_experts, self.slots, self.need_w = dynamic, two_experts, slots, need_w
                self.out_d, self.feat = out_d, feat
                self.lead = 2 if gated and n == 512 else 3
                self.l1, self.hi, self.h, self.l2, self.ev, self.feat_done, self.st = (
                    sem(f"{name}_{x}") for x in ("l1", "hi", "hidden", "l2", "evac", "feat", "store"))
                if gated:
                    self.g, self.mul = sem(f"{name}_gelu"), sem(f"{name}_mul")
                self.nev = 2 * iters
                self.nst = iters if two_experts else 2 * iters

            def bank(self, st, gate):
                if self.gated and self.n == 512:
                    return 2 * (st % 2) + gate, 0
                return st % 4, gate * self.n

            def fbuf(self, st):
                u = st % (1024 // self.n)
                return hidden_f32[:, u * self.n:(u + 1) * self.n]

            def gbuf(self, st):
                return gt[:, (st % 2) * 512:(st % 2) * 512 + 512] if self.n == 512 \
                    else gt[:, (st % 4) * 256:(st % 4) * 256 + 256]

        cs = FfnPass("cs", B // 16, 512, True, False, False, C_SHARE, 0, cshare_d, 1)
        ce = FfnPass("ce", NCH // 2, CH, True, True, False, C_EXP, 9, cexp_d, 0)
        es = [FfnPass(f"s{j}", B // 16, 512, False, False, False, E_SHARE[j], 11 + (0, 3, 5)[j], src_d[1 + j], 1 + j)
              for j in range(3)]
        ee = FfnPass("ee", NCH, CH, False, True, True, E_EXP, 24, src_d[0], 0)
        passes = [cs, ce] + es + [ee]

        def before(p):
            return {"ce": cs, "s1": es[0], "s2": es[1], "ee": es[2]}.get(p.name)

        def w16(slot, part, col, width=128):
            lo = slot * SLOT + part * MAT + col
            return arena[:, lo:lo + width]

        SPLIT = ((0, 0), (0, 1), (1, 0))

        y_twice = ex.rearrange("p k (b n) -> p (k b) n", b=GB).unsqueeze(2).to_broadcast([128, KC * GB, 2, S])

        def kbd_head(h):
            return kbd.rearrange("p h m b e n -> p (h m b) e n")[:, :, h, :]
        kh_batches = kh.rearrange("p h k (b n) -> p (h k b) n", b=GB)

        def heads(x):
            return x.rearrange("p (h n) -> p h n", h=H)

        def weighted(engine, buf, b0, nb, j):
            b4 = buf.rearrange("p k (b n) -> p k b n", b=nb)
            g = gates[:, ds(b0, nb), j:j + 1].rearrange("p b j -> p (b j)").unsqueeze(1).unsqueeze(3)
            return engine.tensor_tensor(b4, b4, g.to_broadcast([128, KC, nb, S]), ALU.mult)

        block = ctx.enter_context(nc.Block())

        @block.gpsimd
        def _(pool):
            nc.gpsimd.iota(row[:, :], [[1, 128]], base=0, channel_multiplier=0,
                           allow_small_or_imprecise_dtypes=True).then_inc(s["iotas"], 1)
            nc.gpsimd.iota(pidx[:, :], [[1, 1]], base=0, channel_multiplier=1,
                           allow_small_or_imprecise_dtypes=True).then_inc(s["iotas"], 1)

            loads = []
            for t in range(TYPES):
                loads += [(a[n][t], C_EXP + 3 * t + i, SW, (s["w_first_lo"], 3) if t == 2 and i == 2 else None) for i, n in enumerate(("c_wi0", "c_wi1", "c_wo"))]
            loads += [(a["e_swi"][0], 12, SW, None), (a["e_swo"][0], 13, SW, None)]
            loads += [(a["a_w"], ATTN_W, SA, (cs.l2, 2 * cs.iters))]
            loads += [(a["e_swi"][1], 1, SW, None), (a["e_swo"][1], 2, SW, None)]
            loads += [(a["e_swi"][2], 11, SW, (ce.l2, 2 * ce.iters)), (a["e_swo"][2], 14, SW, None)]
            for e in range(E2):
                loads += [(a["e_wi"][e], E_EXP + 2 * e, SW, (s["x1_out"], 16 * (B // GB)) if e == 0 else None),
                          (a["e_wo"][e], E_EXP + 2 * e + 1, SW, None)]
            loads += [(a["r_w1"], R_W1, SW, None)]
            loads += [(a["r_w2"][0], R_W2[0], SW, (es[0].l2, 2 * es[0].iters)), (a["r_w2"][1], R_W2[1], SW, None)]
            loads += [(a["r_w2"][2], R_W2[2], SW, (es[1].l2, 2 * es[1].iters)), (a["r_w2"][3], R_W2[3], SW, None)]
            loads += [(a["m_w1"][0], MOE_W[0][0], SW, (es[2].l2, 2 * es[2].iters)), (a["m_w2"][0], MOE_W[0][1], SW, None)]
            for e in range(1, NE):
                wait = (s["slot_oh"], 3) if e == 1 else (s["m_out"], 2 * (e - 1))
                loads += [(a["m_w1"][e], MOE_W[e % 2][0], SW, wait), (a["m_w2"][e], MOE_W[e % 2][1], SW, None)]

            def fetch(i):
                pool.dma_start(wstage[:, i % 2, :], loads[i][0]).then_inc(s["w_in"], 16)

            def cut_up(i):
                _, slot, scale, wait = loads[i]
                pool.wait_ge(s["w_in"], 16 * (i + 1))
                if i + 1 < len(loads):
                    if i >= 1:
                        if i > FIRST_MOE:
                            pool.wait_ge(s["mw_lo"], i - FIRST_MOE)
                        else:
                            pool.wait_ge(s["w_ready"], i)
                    fetch(i + 1)
                if wait is not None:
                    pool.wait_ge(*wait)
                st = wstage[:, i % 2, :]
                hi, lo = (arena[:, slot * SLOT + h * MAT:slot * SLOT + (h + 1) * MAT] for h in (0, 1))
                if i >= FIRST_MOE:
                    nc.gpsimd.tensor_scalar(hi, st, scale, None, ALU.mult).then_inc(s["mw_hi"], 1)
                    return
                nc.gpsimd.tensor_scalar(st, st, scale, None, ALU.mult).then_inc(s["wchain"], 1)
                pool.wait_ge(s["wchain"], 2 * i + 1)
                nc.gpsimd.tensor_copy(hi, st).then_inc(s["wchain"], 1)
                pool.wait_ge(s["wchain"], 2 * i + 2)
                nc.gpsimd.tensor_tensor(lo, st, hi, ALU.subtract).then_inc(s["w_ready"], 1)

            pool.wait_ge(s["perm"], 1)
            for j in range(1, 8, 2):
                b = pool.value_load(tbl[0:1, ds(j + T_PERM, 1)], min_val=0, max_val=B - 1)
                pool.dma_start(xf[:, 0, :, j * S:(j + 1) * S],
                               a["x"][ds(b, 1)].rearrange("b p (k n) -> p (b k) n", k=KC)).then_inc(s["x_half"], 16)
            fetch(0)
            for i in range(14):
                cut_up(i)

            def y_make(c):
                pool.wait_ge(s["exsh_in"], c * 32 + 32)
                weighted(nc.gpsimd, ex, c * GB, GB, 0)
                weighted(nc.gpsimd, sh, c * GB, GB, 1).then_inc(s["y_mul"], 1)
                pool.wait_ge(s["y_mul"], c + 1)
                nc.gpsimd.tensor_tensor(ex, ex, sh, ALU.add).then_inc(s["y_sum"], 1)

            def normalise(c, r):
                pool.wait_ge(s["norm"], c * 4 + (2 * r - 2))
                p_ = heads(prob[:, r, :])
                nc.gpsimd.tensor_tensor(p_, p_, rs[:, r, :].unsqueeze(2).to_broadcast([128, H, S]),
                                        ALU.mult).then_inc(s["p_ready"], 1)

            pool.wait_ge(s["gates"], 1)
            def y_low(c):
                pool.wait_ge(s["y_hi"], c + 1)
                two = yd[:, :, :, :, :, :].rearrange("p h k b r n -> p h (k b) r n")
                for twice in range(2):
                    last = nc.gpsimd.tensor_tensor(two[:, 1, :, twice, :], ex.rearrange("p k (b n) -> p (k b) n", b=GB),
                                                   two[:, 0, :, twice, :], ALU.subtract)
                last.then_inc(s["y_lo"], 1)

            for c in range(2):
                y_make(c)
                y_low(c)
            with pool.Fori(1, NA - 1) as c:
                y_make(c + 1)
                normalise(c, 0)
                normalise(c, 1)
                y_low(c + 1)
            for c in (NA - 1, NA):
                normalise(c, 0)
                normalise(c, 1)

            for i in range(14, len(loads)):
                cut_up(i)

            with pool.Fori(0, NP // 8) as q:
                for u in (7,):
                    for b2 in range(2):
                        b = pool.value_load(tbl[0:1, ds(q * 16 + (2 * u + b2 + T_PERM), 1)], min_val=0, max_val=B - 1)
                        pool.wait_ge(s["fin"], q * 8 + (u + 1))
                        pool.dma_start(a["out"][ds(b, 1)].rearrange("b p (k n) -> p (b k) n", k=KC),
                                       yo[:, u, b2, :, :]).then_inc(s[f"fin_st{FIN_ST[u]}"], 16)

        @block.sync
        def _(sp):
            sp.dma_start(itok_i, a["itok"]).then_inc(s["small_in"], 16)
            sp.dma_start(gate_vec, a["gv"].partition_broadcast(128)).then_inc(s["small_in"], 16)
            sp.dma_start(first_stage[0], a["c_swi0"]).then_inc(s["w_first_in0"], 16)
            sp.wait_ge(s["perm"], 1)

            def load_x(dst, position):
                b = sp.value_load(tbl[0:1, ds(position + T_PERM, 1)], min_val=0, max_val=B - 1)
                return sp.dma_start(dst, a["x"][ds(b, 1)].rearrange("b p (k n) -> p (b k) n", k=KC))

            def g_is_first(g, u):
                return isinstance(g, int) and g == 0 and u == 0

            def x_group(g, u, fresh=False):
                if not fresh:
                    sp.wait_ge(s["x_lo"], g * 2 + (u - 1))
                    sp.wait_ge(s["tables"], 1)
                for j in range(0, 8, 2 if g_is_first(g, u) else 1):
                    load_x(xf[:, u, :, j * S:(j + 1) * S], g * 16 + (8 * u + j)).then_inc(s[f"x_in{u}"], 16)

            def stores(p):
                def store(i, half, n):
                    if p.dynamic:
                        c = i if p.two_experts else i * 2 + half
                        first = sp.value_load(tbl[0:1, ds(c + T_POS, 1)], min_val=0, max_val=B) * S
                    else:
                        first = (i * 2 + half) * 512
                    sp.wait_ge(p.feat_done, n + 1)
                    sp.dma_start(p.out_d[:, :, ds(first, p.n)], outb[:, :, 0:p.n]).then_inc(p.st, 16)
                if p is cs:
                    x_group(0, 0, True)
                    sp.dma_start(first_stage[2], a["c_swo"]).then_inc(s["w_first_in2"], 16)
                    x_group(0, 1, True)
                    sp.dma_start(bias[:, :], a["bias"]).then_inc(s["bias_in"], 16)
                    sp.dma_start(rb3, a["rb3"].partition_broadcast(128)).then_inc(s["bias_in"], 16)
                    x_group(1, 0)
                    x_group(1, 1)
                    store(0, 0, 0)
                    with sp.Fori(1, p.iters - 1) as i:
                        x_group(i + 1, 0)
                        store(i - 1, 1, i * 2 - 1)
                        x_group(i + 1, 1)
                        store(i, 0, i * 2)
                    store(p.iters - 2, 1, p.iters * 2 - 3)
                    store(p.iters - 1, 0, p.iters * 2 - 2)
                    store(p.iters - 1, 1, p.iters * 2 - 1)
                elif p.two_experts:
                    with sp.Fori(0, p.iters) as i:
                        store(i, 0, i)
                else:
                    with sp.Fori(0, p.iters) as i:
                        store(i, 0, i * 2)
                        store(i, 1, i * 2 + 1)
                sp.wait_ge(p.st, 16 * p.nst)

            stores(cs)
            stores(ce)
            sp.wait_ge(s["x_lo"], 8)
            sp.dma_start(misc[:, 4608:5632], a["c_g0"]).then_inc(s["gw_in"], 16)
            sp.dma_start(misc[:, 1024:1028], a["c_g1"]).then_inc(s["gw_in"], 16)

            def exsh(c):
                sp.dma_start(ex, cexp_d[:, :, ds(c * CH, CH)]).then_inc(s["exsh_in"], 16)
                sp.dma_start(sh, cshare_d[:, :, ds(c * CH, CH)]).then_inc(s["exsh_in"], 16)

            def xin_load(c):
                for j in range(GB):
                    load_x(xin[:, :, j * S:(j + 1) * S], c * GB + j).then_inc(s["xin_in"], 16)

            def x1_store(c):
                sp.wait_ge(s["x1_lo"], c + 1)
                sp.dma_start(x1_d[:, :, ds(c * CH, CH)], x1).then_inc(s["x1_out"], 16)

            exsh(0)
            xin_load(0)
            for c in range(1, 4):
                sp.wait_ge(s["y_lo"], c)
                exsh(c)
            with sp.Fori(2, NA - 2) as c:
                x1_store(c - 2)
                xin_load(c - 1)
                sp.wait_ge(s["y_lo"], c + 2)
                exsh(c + 2)
            for c in range(NA - 2, NA + 2):
                x1_store(c - 2)
                if c - 1 < NA:
                    xin_load(c - 1)

            sp.wait_ge(s["gates"], 1)
            sp.dma_start(misc[:, 4608:6656], a["e_g1"]).then_inc(s["gw_in"], 16)
            sp.dma_start(misc[:, 1024:1032], a["e_g2"]).then_inc(s["gw_in"], 16)
            sp.dma_start(misc[:, 2400:2464], a["r_w3"]).then_inc(s["w3_in"], 16)

            for p in es + [ee]:
                stores(p)

            def z_load(k, u):
                for j in range(4):
                    sp.dma_start(zsrcs[:, u, j, :, :], src_d[j][:, :, ds((k + u) * CH, CH)]).then_inc(s[f"z_in{u}"], 16)
            z_load(0, 0)
            z_load(0, 1)
            with sp.Fori(1, NT // CH // 2) as half_k:
                k = half_k * 2
                for u in range(2):
                    sp.wait_ge(s["z_lo"], k + (u - 1))
                    z_load(k, u)

            sp.wait_ge(s["ct"], NP)
            sp.wait_ge(s["xe_hi"], 2 * NP)
            sp.wait_ge(s["xe_lo"], 2 * NP)
            sp.dma_start(misc[:, 4608:6656], a["eb2"].partition_broadcast(128)).then_inc(s["eb2_in"], 16)
            sp.wait_ge(s["zt_mm"], NP)
            sp.dma_start(x1f, x1_d).then_inc(s["x1_in"], 16)
            with sp.Fori(0, NE) as e:
                for t in range(5):
                    sp.wait_ge(s["eo_lo"], e * 5 + (t + 1))
                    for h in range(2):
                        sp.dma_start(eout_d[:, ds(e, 1), 2 * t + h, :].rearrange("b e c -> b (e c)"),
                                     eo[h * 64:(h + 1) * 64, t % 4, :, :].rearrange("p h n -> p (h n)")
                                     ).then_inc(s[f"eo_st{t % 4}"], 16)
            def out_store(q, u):
                b = sp.value_load(tbl[0:1, ds(q * 16 + (2 * u + T_PERM), 1)], min_val=0, max_val=B - 1)
                sp.wait_ge(s["fin"], q * 8 + (u + 1))
                sp.dma_start(a["out"][ds(b, 1)].rearrange("b p (k n) -> p (b k) n", k=KC),
                             yo[:, u, 0, :, :]).then_inc(s[f"fin_st{FIN_ST[u]}"], 16)
            with sp.Fori(0, NP // 8) as q:
                for u in range(7):
                    out_store(q, u)
            for u in range(4):
                sp.wait_ge(s[f"fin_st{u}"], 32 * FIN_ST.count(u) * (NP // 8))

        @block.tensor
        def _(pe):
            mm = nc.tensor.matmul
            pe.wait_ge(s["order_oh"], 1)
            mm(ps[:, 0, 0:TYPES], ones[0:B, :], type_oh, start=True, stop=True)
            mm(ps[0:B, 1, 0:TYPES], upper[0:B, 0:B], type_oh, start=True, stop=True).then_inc(s["order_mm"], 1)
            pe.wait_ge(s["order_oh"], 2)
            mm(ps[0:1, 2, 0:B], pidx[0:B, 0:1], batch_oh, start=True, stop=True).then_inc(s["order_mm"], 1)

            carried = [pe.alloc_register(n) for n in ("chunk_weights", "chunk_start")]

            def carry(place):
                for reg, value in zip(carried, place):
                    pe.reg_mov(reg, value)

            def ffn(p):
                if p is cs:
                    pe.wait_ge(s["tables"], 1)
                else:
                    pe.wait_ge(s["w_ready"], p.need_w)
                if p is ce:
                    pe.wait_ge(s["consts"], 1)
                if p is es[0]:
                    pe.wait_ge(s["pt_lo"], 4 * NA)
                prev = before(p)
                if prev is not None:
                    pe.wait_ge(prev.ev, prev.nev)

                def at_chunk(i, half):
                    if not p.dynamic:
                        return 0, (i * 2 + half) * 512
                    c = i if p.two_experts else i * 2 + half
                    first = pe.value_load(tbl[0:1, ds(c + T_START, 1)], min_val=0, max_val=NT)
                    off = pe.value_load(tbl[0:1, ds(c + (T_OFFE if p.two_experts else T_OFFC), 1)],
                                        min_val=0, max_val=6 * SLOT)
                    return off, first

                def weight(off, half, matrix, part, col):
                    if not p.dynamic:
                        return w16(p.slots[matrix], part, col)
                    base = (p.slots + matrix + (2 * half if p.two_experts else 0)) * SLOT + part * MAT + col
                    return arena[:, ds(off + base, 128)]

                def first(i, st, place):
                    half, f = divmod(st, FC)
                    off, start = place
                    if p is cs and f == 0:
                        pe.wait_ge(s["x_lo"], i * 2 + (half + 1))
                    if p is es[0] and f == 0:
                        pe.wait_ge(s["x1_lo"], i * 4 + (2 * half + 2))
                    for g in range(2 if p.gated else 1):
                        if p is cs and isinstance(i, int) and i == 0 and st == 0:
                            pe.wait_ge(s["w_first_lo"], g + 1)
                        bank, col = p.bank(st, g)
                        for k in range(KC):
                            for n, (wp, xp) in enumerate(SPLIT):
                                last = mm(ps[:, bank, col:col + p.n], weight(off, half, g, wp, k * F + f * 128),
                                          xh[:, xp, k, ds(start, p.n)],
                                          start=(k == 0 and n == 0), stop=(k == KC - 1 and n == 2))
                    last.then_inc(p.l1, 1)

                def second(i, st, place):
                    half, f = divmod(st, FC)
                    if f == 0 and not (isinstance(i, int) and i == 0):
                        pe.wait_ge(p.ev, i * 2 + (half - 1))
                    if p is cs and isinstance(i, int) and i == 0 and st == 0:
                        pe.wait_ge(s["w_first_lo"], 3)
                    if p is es[0] and isinstance(i, int) and i == 0 and st == 0:
                        pe.wait_ge(s["x1"], NA)
                    pe.wait_ge(p.h, i * 16 + (st + 1))
                    for m in range(2):
                        for n, (wp, hp) in enumerate(SPLIT):
                            last = mm(ps[:, 4 + 2 * half + m, 0:p.n],
                                      weight(place[0], half, 2 if p.gated else 1, wp, f * D + m * 128),
                                      hid[:, st % 4, hp, 0:p.n], start=(f == 0 and n == 0),
                                      stop=(f == FC - 1 and n == 2))
                    if f == FC - 1:
                        last.then_inc(p.l2, 1)

                def body(i, lastone):
                    if p.dynamic:
                        place = [tuple(pe.snap(reg, min_val=0, max_val=top)
                                       for reg, top in zip(carried, (6 * SLOT, NT)))] * 2
                    else:
                        place = [at_chunk(i, 0)] * 2
                    for st in range(16):
                        if st == 3 and not p.two_experts:
                            place[1] = at_chunk(i, 1)
                        if st == 11 and not lastone:
                            ahead = at_chunk(i + 1, 0)
                        second(i, st, place[st // FC])
                        nxt = st + p.lead
                        if nxt < 16:
                            first(i, nxt, place[nxt // FC])
                        elif not lastone:
                            first(i + 1, nxt - 16, ahead)
                    if p.dynamic and not lastone:
                        carry(ahead)

                place0 = at_chunk(0, 0)
                if p.dynamic:
                    carry(place0)
                for st in range(p.lead):
                    first(0, st, place0)
                body(0, False)
                with pe.Fori(1, p.iters - 1) as i:
                    body(i, False)
                body(p.iters - 1, True)

            def gate(kc_in, n_out, turn, p_last):
                pe.wait_ge(s["gw_in"], 32 * turn)
                pe.wait_ge(p_last.feat_done, p_last.nst)
                pe.wait_ge(p_last.ev, p_last.nev)
                for m in range(2):
                    for k in range(kc_in):
                        last = mm(ps[:, m, 0:B], gate_w1[:, k, m * 128:(m + 1) * 128], gate_in[:, k // KC, k % KC, 0:B],
                                  start=(k == 0), stop=(k == kc_in - 1))
                last.then_inc(s["gate_mm"], 1)
                pe.wait_ge(s["gate_rdy"], 2 * turn)

                for j in range(n_out):
                    for k in range(2):
                        last = mm(ps[:, 2, j * B:(j + 1) * B], gate_rep[:, j, k, :], gate_hid[:, k, :],
                                  start=(k == 0), stop=(k == 1))
                last.then_inc(s["gate_mm"], 1)

            ffn(cs)
            ffn(ce)
            gate(4, 2, 1, ce)

            def wide_products(dst, w, m, data):
                for k in range(KC):
                    for j, (wp, xp) in enumerate(SPLIT):
                        last = mm(dst, w16(ATTN_W, wp, (w * KC + k) * D + m * 128), data(xp, k),
                                  start=(k == 0 and j == 0), stop=(k == KC - 1 and j == 2))
                return last

            def scores(r):
                for m in range(2):
                    for b2 in range(2):
                        b = 2 * r + b2
                        for j, (kp, qp) in enumerate(SPLIT):
                            mm(ps[b2 * 64:b2 * 64 + 64, 2 * r + m, :], qh[:, qp, m, b * S:(b + 1) * S],
                               kbd[:, kp, m, b, :, :].rearrange("p h n -> p (h n)"),
                               start=(j == 0), stop=False, skip_group_check=True)
                    last = mm(ps[:, 2 * r + m, :], identb[:, :], causal[:, :, :].rearrange("p h n -> p (h n)"),
                              start=False, stop=True, skip_group_check=True)
                last.then_inc(s["s_mm"], 1)

            def output_product(c, new):
                pe.wait_ge(s["o_lo"], c)
                if new:
                    pe.wait_ge(s["qk_lo"], c * 2 + 2)
                else:
                    pe.wait_ge(s["x1"], c - 1)
                for m in range(2):
                    last = wide_products(ps[:, 5, m * CH:(m + 1) * CH], 3, m, lambda xp, k: oh_[:, xp, k, :])
                last.then_inc(s["wo_mm"], 1)

            def attn(c, new, old):
                if new:
                    pe.wait_ge(s["y_lo"], c + 1)
                    for w in range(2):
                        if w == 1 and (not isinstance(c, int) or c >= 2):
                            pe.wait_ge(s["x1"], c - 1)
                        for m in range(2):
                            last = wide_products(ps[:, 4 + w, m * CH:(m + 1) * CH], w, m,
                                                 lambda xp, k: yd[:, xp, k, :, 0, :])
                        last.then_inc(s["qk_mm"], 1)
                    if old:
                        pe.wait_ge(s["v_lo"], c)
                    for b in range(GB):
                        for k in range(KC):
                            for j, (yp, wp) in enumerate(SPLIT):
                                last = mm(ps[:, 6 + b // 2, (b % 2) * D:(b % 2 + 1) * D],
                                          yd[:, yp, k, b, :, :].rearrange("p r n -> p (r n)"),
                                          w16(ATTN_W, wp, (2 * KC + k) * D, D),
                                          start=(k == 0 and j == 0), stop=(k == KC - 1 and j == 2))
                    last.then_inc(s["v_mm"], 1)
                if old:
                    for r in range(2):
                        pe.wait_ge(s["p_ready"], c * 2 + (r - 1))
                        for hb in range(2):
                            for q in range(4):
                                hp = hb * 4 + q
                                last = nc.tensor.transpose(ps[:, 2 * r + hb, q * 128:(q + 1) * 128],
                                                           prob[:, r, hp * 128:(hp + 1) * 128], ident[:, :])
                            last.then_inc(s["t_mm"], 1)
                    if new:
                        pe.wait_ge(s["qk_lo"], c * 2 + 1)
                    else:
                        pe.wait_ge(s["v_lo"], c)
                    for b in range(GB):
                        r, b2 = divmod(b, 2)
                        if b2 == 0:
                            pe.wait_ge(s["pt_lo"], c * 4 + (2 * r - 2))
                        for hp in range(8):
                            o, n0 = 32 * (hp % 4), (hp // 4) * CH + b * S
                            for j, (vp, pp) in enumerate(SPLIT):
                                col = hp * 128 + b2 * S
                                last = mm(ps[o:o + 32, 4, n0:n0 + S], vbd[:, vp, b, hp * 32:(hp + 1) * 32],
                                          pt[:, r, pp, col:col + S], start=(j == 0), stop=(j == 2))
                    last.then_inc(s["pv_mm"], 1)
                if new:
                    pe.wait_ge(s["kbd"], c + 1)
                    pe.wait_ge(s["kbd_act"], c * 2 + 2)
                    scores(0)
                if old:
                    output_product(c, new)
                if new:
                    scores(1)

            pe.wait_ge(s["w_ready"], 12)
            attn(0, True, False)
            attn(1, True, True)
            with pe.Fori(2, NA) as c:
                attn(c, True, True)
            attn(NA, False, True)

            for p in es:
                ffn(p)
            ffn(ee)
            gate(8, 4, 2, ee)

            def router_in(c, f):
                if f >= 4:
                    pe.wait_ge(s["r_lo"], c * 16 + (f - 3))
                for k in range(KC):
                    for n, (wp, xp) in enumerate(SPLIT):
                        last = mm(ps[:, f % 4, :], w16(R_W1, wp, k * F + f * 128), xh[:, xp, k, ds(c * 512, 512)],
                                  start=(k == 0 and n == 0), stop=(k == KC - 1 and n == 2))
                last.then_inc(s["r_mm"], 1)

            def router_mid(c, fo):
                if fo >= 2:
                    pe.wait_ge(s["r_lo"], c * 16 + (8 + fo - 1))
                for k in range(FC):
                    if fo == 0:
                        pe.wait_ge(s["r_lo"], c * 16 + (k + 1))
                    for n, (wp, xp) in enumerate(SPLIT):
                        last = mm(ps[:, 4 + fo % 2, :], w16(R_W2[k // 2], wp, (k % 2) * F + fo * 128), h1[:, k, xp, :],
                                  start=(k == 0 and n == 0), stop=(k == FC - 1 and n == 2))
                last.then_inc(s["r_mm"], 1)

            def router_out(c):
                pe.wait_ge(s["r_lo"], c * 16 + 16)
                if not isinstance(c, int) or c > 0:
                    pe.wait_ge(s["logit"], c)
                for t in range(4):
                    for fo in range(FC):
                        for hp in ((0, 1) if fo == 0 else (1, 0)):
                            n = NE if hp else 2 * NE
                            last = mm(ps[:, 6, t * 2 * NE:t * 2 * NE + n], h2[:, fo, hp, t * 128:(t + 1) * 128],
                                      w3[:, fo, 0:n], start=(fo == 0 and hp == 0),
                                      stop=(fo == FC - 1 and hp == 0), skip_group_check=True)
                last.then_inc(s["l_mm"], 1)

            def router(c, previous):
                pe.wait_ge(s["z_lo"], c * 2 + 2)
                for f in range(FC):
                    router_in(c, f)
                if previous:
                    router_out(c - 1)
                for fo in range(FC):
                    router_mid(c, fo)

            pe.wait_ge(s["w_ready"], 29)
            pe.wait_ge(s["w3"], 1)
            pe.wait_ge(s["gates"], 2)
            router(0, False)
            with pe.Fori(1, 8) as c:
                router(c, True)
            router_out(7)

            pe.wait_ge(s["oh"], 1)
            mm(ps[:, 0, 0:NP * NE], upperb[:, :], oh16.rearrange("p t e -> p (t e)"), start=True,
               stop=True).then_inc(s["pos_mm"], 1)

            pe.wait_ge(s["d01"], 1)

            def turn(t, u):
                fresh, v_ = isinstance(t, int) and t + u < 2, u % 2
                if not fresh:
                    pe.wait_ge(s["zt"], t + (u - 1))
                for h in range(2):
                    for k in range(KC):
                        c0 = (h * KC + k) * 128
                        last = nc.tensor.transpose(zt_ps[v_][:, c0:c0 + 128], xh[:, h, k, ds((t + u) * 128, 128)],
                                                   ident16[:, :])
                last.then_inc(s["zt_mm"], 1)
                if not fresh:
                    pe.wait_ge(s["ct"], t + (u - 1))
                if fresh and u == 0:
                    pe.wait_ge(s["slot_oh"], 3)
                for h in range(2):
                    last = nc.tensor.transpose(ct_ps[v_][:, h * 128:(h + 1) * 128],
                                               dsc[:, h, ds(t + u, 1), :].rearrange("p t s -> p (t s)"), ident16[:, :])
                last.then_inc(s["ct_mm"], 1)

            def gather(t, u):
                if not isinstance(t, int) or t > 0:
                    pe.wait_ge(s["xe_hi"], t * 2 + (2 * u - 2))
                    pe.wait_ge(s["xe_lo"], t * 2 + (2 * u - 2))
                pe.wait_ge(s["zt"], t + (u + 1))
                for h in range(2):
                    for k in range(KC):
                        last = mm(ps[:, 2 + 2 * u + h, k * 2 * SLOTS:(k + 1) * 2 * SLOTS], ztok[:, u, h, k, :],
                                  d01[:, ds(t + u, 1), :, :].rearrange("p t b s -> p (t b s)"), start=True, stop=True)
                last.then_inc(s["dp_mm"], 1)

            def dispatch(t, lastone=False):
                turn(t, 1)
                gather(t, 0)
                if not lastone:
                    turn(t, 2)
                gather(t, 1)
            turn(0, 0)
            dispatch(0)
            with pe.Fori(1, NP // 2 - 1) as half_t:
                dispatch(half_t * 2)
            dispatch(NP - 2, True)

            pe.wait_ge(s["xe_hi"], 2 * NP)
            pe.wait_ge(s["xe_lo"], 2 * NP)
            pe.wait_ge(s["ct"], NP)

            def expert_in(e, par, st):
                half, f = divmod(st, FC)
                n, c0 = len(TILES[half]) * 128, TILES[half][0] * 128
                if st == 0:
                    if isinstance(e, int) and e == 0:
                        pe.wait_ge(s["w_ready"], FIRST_MOE)
                    else:
                        pe.wait_ge(s["mw_lo"], e * 2)
                for k in range(KC):
                    for j, (wp, xp) in enumerate(SPLIT):
                        last = mm(ps[:, st % 2, 0:n], w16(MOE_W[par][0], wp, k * F + f * 128),
                                  xe[:, xp, k, ds(e * PER_E + c0, n)],
                                  start=(k == 0 and j == 0), stop=(k == KC - 1 and j == 2))
                last.then_inc(s["m_mm"], 1)

            def expert_out(e, par, st):
                half, f = divmod(st, FC)
                if f == 0 and not (isinstance(e, int) and e == 0):
                    pe.wait_ge(s["ev"], e * 5 + (-2 if half == 0 else 0))
                pe.wait_ge(s["m_lo"], e * 16 + (st + 1))
                for i_t, t in enumerate(TILES[half]):
                    for j, (hp, wp) in enumerate(SPLIT):
                        last = mm(ps[:, 3 + t, 0:D], hid[:, st % 4, hp, i_t * 128:(i_t + 1) * 128],
                                  w16(MOE_W[par][1], wp, f * D, D), start=(f == 0 and j == 0),
                                  stop=(f == FC - 1 and j == 2))
                if f == FC - 1:
                    last.then_inc(s["m_out"], 1)

            def expert(e, par, lastone=False):
                for st in range(16):
                    expert_out(e, par, st)
                    if st + 2 < 16:
                        expert_in(e, par, st + 2)
                    elif not lastone:
                        expert_in(e + 1, 1 - par, st - 14)
            for st in range(2):
                expert_in(0, 0, st)
            expert(0, 0)
            expert(1, 1)
            with pe.Fori(1, NE // 2 - 1) as half_e:
                e = half_e * 2
                expert(e, 0)
                expert(e + 1, 1)
            expert(NE - 2, 0)
            expert(NE - 1, 1, True)

            pe.wait_ge(s["ev"], 5 * NE)

            def combine(q, u):
                if not (isinstance(q, int) and q == 0):
                    pe.wait_ge(s["fin"], q * 8 + (u - 7))
                for b2 in range(2):
                    for m in range(2):
                        for j, (ep, cp) in enumerate(SPLIT):
                            lo = ((2 * u + b2) * 2 + ep) * D + m * 128
                            last = mm(ps[:, u, (b2 * KC + m) * S:(b2 * KC + m + 1) * S],
                                      ebf_q[0:SLOTS, ds(q, 1), lo:lo + 128].rearrange("p q c -> p (q c)"),
                                      ct_q[0:SLOTS, cp, ds(q, 1), u, b2 * S:(b2 + 1) * S].rearrange("p q n -> p (q n)"),
                                      start=(j == 0), stop=(j == 2))
                last.then_inc(s["fin_mm"], 1)

            ebf_q = ebf.rearrange("p (q c) -> p q c", c=16 * 2 * D)
            ct_q = ct.rearrange("p h (q u) n -> p h q u n", u=8)
            pe.wait_ge(s["fin_in0"], 16)
            for u in range(8):
                combine(0, u)
            for g in range(1, 4):
                pe.wait_ge(s[f"fin_in{g}"], 16)
            with pe.Fori(1, NP // 8) as q:
                for u in range(8):
                    combine(q, u)

        @block.scalar
        def _(act):
            fn = nc.scalar.activation
            act.wait_ge(s["small_in"], 32)
            act.dma_start(first_stage[1], a["c_swi1"]).then_inc(s["w_first_in1"], 16)
            act.wait_ge(s["soft_sub"], 1)
            fn(gate_vec, gate_vec, ACT.Exp, scale=10.0).then_inc(s["soft_exp"], 1)

            def first_weights(i):
                act.wait_ge(s[f"w_first_in{i}"], 16)
                fn(w16(C_SHARE[i], 0, 0, MAT), first_stage[i], ACT.Copy, scale=SW).then_inc(s["w_first_hi"], 1)
            first_weights(0)
            first_weights(1)

            def x_group(g, u):
                if isinstance(g, int) and g == 0:
                    act.wait_ge(s["x_half"], 64)
                act.wait_ge(s[f"x_in{u}"], (g - u) * 64 + (128 if u else 64))
                act.wait_ge(s["tables"], 1)
                fn(xh[:, 0, :, ds(g * 512, 512)], xf[:, u, :, :], ACT.Copy, scale=SX).then_inc(s["x_hi"], 1)
            x_group(0, 0)
            first_weights(2)
            x_group(1, 1)

            def ffn(p):
                def hidden(i, st):
                    act.wait_ge(p.l1, i * 16 + (st + 1))
                    bank, col = p.bank(st, 0)
                    if p.gated:
                        fn(p.gbuf(st), ps[:, bank, col:col + p.n], ACT.Gelu_apprx_tanh, scale=1 / SH).then_inc(p.g, 1)
                        act.wait_ge(p.mul, i * 16 + (st + 1))
                        fn(hid[:, st % 4, 0, 0:p.n], p.fbuf(st), ACT.Copy).then_inc(p.hi, 1)
                    else:
                        fn(hid[:, st % 4, 0, 0:p.n], ps[:, bank, col:col + p.n], ACT.Relu).then_inc(p.hi, 1)

                def evacuate(i, half):
                    act.wait_ge(p.l2, i * 2 + (half + 1))
                    if half == 0 and isinstance(i, int) and i == 0 and before(p) is not None:
                        act.wait_ge(before(p).st, 16 * before(p).nst)
                    if p.two_experts:
                        if half == 0:
                            if not (isinstance(i, int) and i == 0):
                                act.wait_ge(p.st, i * 16)
                            act.wait_ge(s["consts"], 1)
                            fn(outb[:, :, 0:p.n], ps[:, 4:6, 0:p.n], ACT.Copy,
                               scale=wab[:, 0, ds(i, 1)]).then_inc(p.ev, 1)
                        return
                    if not (isinstance(i, int) and i == 0 and half == 0):
                        act.wait_ge(p.st, i * 32 + 16 * half)
                    fn(outb[:, :, 0:p.n], ps[:, 4 + 2 * half:6 + 2 * half, 0:p.n], ACT.Copy,
                       scale=1 / SO).then_inc(p.ev, 1)

                def body(i, first, lastone):
                    for st in range(16):
                        hidden(i, st)
                        if st == 1 and not first:
                            evacuate(i - 1, 1)
                        if st == 9:
                            evacuate(i, 0)
                        if p is cs and not lastone and st in (3, 11):
                            x_group(i * 2 + (2 if st == 3 else 3), 0 if st == 3 else 1)
                body(0, True, False)
                with act.Fori(1, p.iters - 1) as i:
                    body(i, False, False)
                body(p.iters - 1, False, True)
                evacuate(p.iters - 1, 1)

            def gate(turn):
                act.wait_ge(s["soft_sub"], 1 + turn)
                fn(gates[:, :, 0:2 * turn], gates[:, :, 0:2 * turn], ACT.Exp).then_inc(s["soft_exp"], 1)

            ffn(cs)
            ffn(ce)
            gate(1)

            def y_parts(c):
                act.wait_ge(s["y_sum"], c + 1)
                if not isinstance(c, int) or c > 0:
                    act.wait_ge(s["v_mm"], c)
                fn(yd[:, 0, :, :, :, :].rearrange("p k b r n -> p (k b) r n"), y_twice, ACT.Copy
                   ).then_inc(s["y_hi"], 1)

            def attn(c, new, old, fin, more):
                if old:
                    for r in range(2):
                        act.wait_ge(s["sub"], c * 2 + (r - 1))
                        fn(prob[:, r, :], prob[:, r, :], ACT.Exp, scale=0.25 / (SQ * SQ)).then_inc(s["exp"], 1)
                if fin:
                    act.wait_ge(s["x1"], c - 1)
                    act.wait_ge(ce.l2, 2 * ce.iters)
                    fn(xh[:, 0, :, ds((c - 2) * CH, CH)], x1, ACT.Copy, scale=SX).then_inc(s["x1_hi"], 1)
                if new:
                    for w, dst in enumerate((qh, kh)):
                        act.wait_ge(s["qk_mm"], c * 2 + (w + 1))
                        for m in range(KC):
                            last = fn(dst[:, 0, m, :], ps[:, 4 + w, m * CH:(m + 1) * CH], ACT.Identity,
                                      bias=ab[:, w, m:m + 1])
                        last.then_inc(s["qk_hi"], 1)
                for r in range(2):
                    if old:
                        for hb in range(2):
                            act.wait_ge(s["t_mm"], c * 4 + (2 * r + hb - 3))
                            fn(pt[:, r, 0, hb * 512:(hb + 1) * 512], ps[:, 2 * r + hb, :], ACT.Copy
                               ).then_inc(s["pt_hi"], 1)
                    if new:
                        act.wait_ge(s["qk_lo"], c * 2 + 2)
                        h = KBD_DVE + r
                        fn(kbd_head(h), kh_batches, ACT.Copy, scale=head_mask[:, h:h + 1]).then_inc(s["kbd_act"], 1)
                if more:
                    y_parts(c + 1)
                if old:
                    act.wait_ge(s["pv_mm"], c)
                    for m in range(KC):
                        last = fn(oh_[:, 0, m, :], ps[:, 4, m * CH:(m + 1) * CH], ACT.Identity, bias=ab[:, 2, m:m + 1])
                    last.then_inc(s["o_hi"], 1)
                if new:
                    act.wait_ge(s["v_mm"], c + 1)
                    for r in range(2):
                        for j in range(2):
                            last = fn(vb(0, r, j), vp(r, j), ACT.Copy, scale=half_mask[:, j:j + 1])
                    last.then_inc(s["v_hi"], 1)
                if old:
                    act.wait_ge(s["xin_in"], c * 64)
                    for k in range(KC):
                        last = fn(xin[:, k, :], xin[:, k, :], ACT.Identity, bias=ab[:, 3, k:k + 1])
                    last.then_inc(s["xb"], 1)

            y_parts(0)
            attn(0, True, False, False, True)
            attn(1, True, True, False, True)
            with act.Fori(2, NA - 1) as c:
                attn(c, True, True, True, True)
            attn(NA - 1, True, True, True, False)
            attn(NA, False, True, True, False)
            attn(NA + 1, False, False, True, False)

            for p in es:
                ffn(p)
            ffn(ee)
            gate(2)

            def z_parts(k, u):
                zsrc = zsrcs[:, u]
                act.wait_ge(s["z_sum"], k + 1)
                act.wait_ge(ee.l2, 2 * ee.iters)
                fn(xh[:, 0, :, ds(k * CH, CH)], zsrc[:, 0, :, :], ACT.Copy, scale=SZ).then_inc(s["z_hi"], 1)

            def rhidden(c, st, fresh):
                act.wait_ge(s["r_mm"], c * 16 + (st + 1))
                if st < FC:
                    src, dst, b_, scale = ps[:, st % 4, :], h1[:, st, 0, :], rb1[:, st:st + 1], 1.0
                else:
                    fo = st - FC
                    src, dst, b_, scale = ps[:, 4 + fo % 2, :], h2[:, fo, 0, :], rb2[:, fo:fo + 1], 1 / SW
                if not (fresh and st < 2):
                    act.wait_ge(s["r_lo"], c * 16 + (st - 1))
                fn(gt[:, (st % 2) * 512:(st % 2 + 1) * 512], src, ACT.Relu, bias=b_, scale=scale)
                fn(dst, src, ACT.Relu, bias=b_, scale=scale).then_inc(s["r_hi"], 1)

            def router(c, fresh, more):
                for st in range(16):
                    rhidden(c, st, fresh)
                    if more and st in (8, 11):
                        z_parts(c * 2 + (2 if st == 8 else 3), 0 if st == 8 else 1)
            z_parts(0, 0)
            z_parts(1, 1)
            router(0, True, True)
            with act.Fori(1, 7) as c:
                router(c, False, True)
            router(7, False, False)

            act.wait_ge(s["soft_sub"], 4)
            fn(score, score, ACT.Exp).then_inc(s["soft_exp"], 1)

            act.wait_ge(s["slot_oh"], 1)
            fn(d01[:, :, 0, :], dtmp, ACT.Copy, scale=half_mask[:, 0:1])
            fn(d01[:, :, 1, :], dtmp, ACT.Copy, scale=half_mask[:, 1:2]).then_inc(s["d01"], 1)

            def turn(t, u):
                act.wait_ge(s["ct_mm"], t + (u + 1))
                act.wait_ge(s["slot_oh"], 3)
                fn(ct[0:SLOTS, :, ds(t + u, 1), :].rearrange("p h t n -> p (h t) n"),
                   ct_ps[u % 2].rearrange("p (h n) -> p h n", h=2), ACT.Copy).then_inc(s["ct"], 1)

            def gather(t, u):
                act.wait_ge(s["dp_mm"], t + (u + 1))
                act.wait_ge(s["slot_oh"], 3)
                for k in range(KC):
                    fn(xe_pair(0, k, t, u), dp(u, 0, k), ACT.Copy).then_inc(s["xe_hi"], 1)

            def dispatch(t, lastone=False):
                turn(t, 1)
                gather(t, 0)
                if not lastone:
                    turn(t, 2)
                gather(t, 1)
            turn(0, 0)
            with act.Fori(0, NP // 2 - 1) as half_t:
                dispatch(half_t * 2)
            dispatch(NP - 2, True)

            def ehidden(e, st):
                half, f = divmod(st, FC)
                n = len(TILES[half]) * 128
                act.wait_ge(s["m_mm"], e * 16 + (st + 1))
                b_ = eb1_now[:, f:f + 1]
                fn(egt[:, st % 4, 0:n], ps[:, st % 2, 0:n], ACT.Relu, bias=b_)
                fn(hid[:, st % 4, 0, 0:n], ps[:, st % 2, 0:n], ACT.Relu, bias=b_).then_inc(s["m_hi"], 1)

            def eout(e, half, tiles=None):
                for t in (tiles or TILES[half]):
                    act.wait_ge(s["ev"], e * 5 + (t + 1))
                    if t == 4:
                        act.wait_ge(s["eo_st0"], e * 64 + 32)
                    elif not (isinstance(e, int) and e == 0):
                        act.wait_ge(s[f"eo_st{t}"], e * (64 if t == 0 else 32))
                    fn(eo[:, t % 4, 0, :], ev[:, t % 2, :], ACT.Copy).then_inc(s["eo_hi"], 1)

            def expert(e, fresh=False):
                if not fresh:
                    act.wait_ge(s["m_hi"], e * 16)
                act.wait_ge(s["consts"], 1)
                fn(eb1_now, eb1[:, ds(e * FC, FC)], ACT.Copy).then_inc(s["eb1"], 1)
                act.wait_ge(s["eb1"], e + 1)
                for st in range(16):
                    ehidden(e, st)
                    if st in (1, 2) and not fresh:
                        eout(e - 1, 1, (2 + st,))
                    if st in (8, 9, 10):
                        eout(e, 0, (st - 8,))
            expert(0, True)
            with act.Fori(1, NE) as e:
                expert(e)
            eout(NE - 1, 1)

            for t in range(4):
                act.wait_ge(s[f"eo_st{t}"], 32 * NE * (2 if t == 0 else 1))
            for g in range(4):
                act.dma_start(ebf[0:SLOTS, g * 16 * 2 * D:(g + 1) * 16 * 2 * D].rearrange("p (b c) -> p b c", b=16),
                              eout_d[16 * g:16 * g + 16].rearrange("b e n c -> (e n) b c")).then_inc(s[f"fin_in{g}"], 16)

            def out_store(q, u):
                b = act.value_load(tbl[0:1, ds(q * 16 + (2 * u + 1 + T_PERM), 1)], min_val=0, max_val=B - 1)
                act.wait_ge(s["fin"], q * 8 + (u + 1))
                act.dma_start(a["out"][ds(b, 1)].rearrange("b p (k n) -> p (b k) n", k=KC),
                              yo[:, u, 1, :, :]).then_inc(s[f"fin_st{FIN_ST[u]}"], 16)
            with act.Fori(0, NP // 8) as q:
                for u in range(7):
                    out_store(q, u)

        @block.vector
        def _(dve):
            v = nc.vector
            links = [0]

            def link(ins):
                ins.then_inc(s["dve"], 1)
                links[0] += 1
                dve.wait_ge(s["dve"], links[0])

            dve.wait_ge(s["iotas"], 2)
            v.memset(ones, 1.0)
            link(v.tensor_scalar(upper[:, :], row[:, :], pidx[:, 0:1], None, ALU.is_gt))
            dve.wait_ge(s["small_in"], 32)
            link(v.tensor_copy(itok_f, itok_i))
            v.tensor_scalar(type_oh, row[0:B, 0:TYPES], itok_f, None, ALU.is_equal).then_inc(s["order_oh"], 1)
            gv = gate_vec.rearrange("p (t e) -> p t e", t=TYPES)
            link(v.reduce_max(gsum, gv, AX.X))
            v.tensor_tensor(gv, gv, gsum.unsqueeze(2).to_broadcast([128, TYPES, E2]), ALU.subtract).then_inc(s["soft_sub"], 1)
            dve.wait_ge(s["order_mm"], 1)
            v.memset(starts[:, 0:1], 0.0)
            link(v.tensor_copy(cnt, ps[:, 0, 0:TYPES]))
            v.tensor_copy(starts[:, 1:2], cnt[:, 0:1])
            link(v.tensor_tensor(starts[:, 2:3], cnt[:, 0:1], cnt[:, 1:2], ALU.add))
            link(v.tensor_tensor(tmp3[0:B, :], ps[0:B, 1, 0:TYPES], starts[0:B, :], ALU.add))
            link(v.tensor_tensor(tmp3[0:B, :], tmp3[0:B, :], type_oh, ALU.mult))
            link(v.reduce_sum(rank, tmp3[0:B, :], AX.X))
            v.tensor_scalar(batch_oh, row[0:B, 0:B], rank, None, ALU.is_equal).then_inc(s["order_oh"], 1)
            lt = scr[:, 0:3 * 16].rearrange("p (t j) -> p t j", t=TYPES)
            link(v.tensor_scalar(scr[:, 64:80], row[:, 0:16], float(GB), None, ALU.mult))
            link(v.tensor_tensor(lt, scr[:, 64:80].unsqueeze(1).to_broadcast([128, TYPES, 16]),
                                 cnt.unsqueeze(2).to_broadcast([128, TYPES, 16]), ALU.is_lt))
            link(v.reduce_sum(nchunks, lt, AX.X))
            dve.wait_ge(s["order_mm"], 2)
            v.tensor_copy(tbl[0:1, T_PERM:T_PERM + B], ps[0:1, 2, 0:B]).then_inc(s["perm"], 1)
            link(v.tensor_tensor(nchunks[:, 1:2], nchunks[:, 0:1], nchunks[:, 1:2], ALU.add))
            p0, p1, start, typ, t_ = (scr[:, 96 + 20 * j:116 + 20 * j] for j in range(5))
            v.tensor_scalar(p0, row[:, 0:20], nchunks[:, 0:1], None, ALU.is_ge)
            link(v.tensor_scalar(p1, row[:, 0:20], nchunks[:, 1:2], None, ALU.is_ge))
            link(v.tensor_tensor(typ, p0, p1, ALU.add))
            link(v.tensor_scalar(scr[:, 200:202], nchunks[:, 0:2], -float(GB), None, ALU.mult))
            link(v.tensor_tensor(scr[:, 200:202], scr[:, 200:202], starts[:, 1:3], ALU.add))
            link(v.tensor_tensor(scr[:, 201:202], scr[:, 201:202], scr[:, 200:201], ALU.subtract))
            link(v.tensor_scalar(start, row[:, 0:20], float(GB), None, ALU.mult))
            link(v.tensor_scalar(t_, p0, scr[:, 200:201], None, ALU.mult))
            link(v.tensor_tensor(start, start, t_, ALU.add))
            link(v.tensor_scalar(t_, p1, scr[:, 201:202], None, ALU.mult))
            link(v.tensor_tensor(start, start, t_, ALU.add))
            link(v.tensor_scalar(start, start, float(B), None, ALU.min))
            v.tensor_copy(tbl[:, T_POS:T_POS + 20], start)
            v.tensor_scalar(tbl[:, T_START:T_START + 20], start, float(S), None, ALU.mult)
            v.tensor_scalar(tbl[:, T_OFFC:T_OFFC + 20], typ, float(3 * SLOT), None, ALU.mult)
            v.tensor_scalar(tbl[:, T_OFFE:T_OFFE + 20], typ, float(2 * SLOT), None, ALU.mult).then_inc(s["tables"], 1)
            def first_weights(i):
                dve.wait_ge(s["w_first_hi"], i + 1)
                v.scalar_tensor_tensor(w16(C_SHARE[i], 1, 0, MAT), first_stage[i], SW, w16(C_SHARE[i], 0, 0, MAT),
                                       ALU.mult, ALU.subtract).then_inc(s["w_first_lo"], 1)

            def x_group(g, u):
                dve.wait_ge(s["x_hi"], g + 1)
                v.scalar_tensor_tensor(xh[:, 1, :, ds(g * 512, 512)], xf[:, u, :, :], SX, xh[:, 0, :, ds(g * 512, 512)],
                                       ALU.mult, ALU.subtract).then_inc(s["x_lo"], 1)
            first_weights(0)
            first_weights(1)
            x_group(0, 0)
            first_weights(2)
            x_group(1, 1)

            dve.wait_ge(s["soft_exp"], 1)
            link(v.reduce_sum(gsum, gv, AX.X))
            link(v.reciprocal(gsum, gsum))
            link(v.tensor_scalar(gsum, gsum, 1 / SO, None, ALU.mult))
            link(v.tensor_tensor(gv, gv, gsum.unsqueeze(2).to_broadcast([128, TYPES, E2]), ALU.mult))
            for e in range(2):
                link(v.tensor_scalar(t_, p0, -1.0, 1.0, ALU.mult, ALU.add))
                link(v.tensor_scalar(wab[:, e, :], t_, gv[:, 0, e:e + 1], None, ALU.mult))
                link(v.tensor_tensor(t_, p0, p1, ALU.subtract))
                link(v.scalar_tensor_tensor(wab[:, e, :], t_, gv[:, 1, 1 + e:2 + e], wab[:, e, :], ALU.mult, ALU.add))
                link(v.scalar_tensor_tensor(wab[:, e, :], p1, gv[:, 2, 2 + e:3 + e], wab[:, e, :], ALU.mult, ALU.add))

            v.memset(xh[:, :, :, NT:NTP], 0.0)
            link(v.tensor_scalar(ident[:, :], row[:, :], pidx[:, 0:1], None, ALU.is_equal))
            v.tensor_copy(ident16[:, :], ident[:, :])
            v.tensor_copy(identb[:, :], ident[:, :])
            link(v.tensor_copy(upperb[:, :], upper[:, :]))
            v.memset(upperb[0:64, 64:128], 0.0)
            link(v.tensor_scalar(half_mask[:, 1:2], pidx[:, 0:1], 64.0, None, ALU.is_ge))
            v.tensor_scalar(half_mask[:, 0:1], half_mask[:, 1:2], -1.0, 1.0, ALU.mult, ALU.add)
            link(v.scalar_tensor_tensor(gsum[:, 0:1], half_mask[:, 1:2], -64.0, pidx[:, 0:1], ALU.mult, ALU.add))
            link(v.tensor_scalar(scr[:, 0:64], row[:, 0:64], gsum[:, 0:1], MASKED, ALU.is_gt, ALU.mult))
            v.tensor_copy(causal[:, :, :], scr[:, 0:64].unsqueeze(1).to_broadcast([128, 8, S]))
            link(v.tensor_scalar(t_[:, 0:8], row[:, 0:8], float(HD), pidx[:, 0:1], ALU.mult, ALU.subtract))
            v.tensor_scalar(typ[:, 0:8], t_[:, 0:8], -float(HD), None, ALU.is_gt)
            link(v.tensor_scalar(t_[:, 0:8], t_[:, 0:8], 0.0, None, ALU.is_le))
            v.tensor_tensor(head_mask[:, :], t_[:, 0:8], typ[:, 0:8], ALU.mult)
            v.tensor_scalar(slot_row, row[:, 0:CAP], -64.0, None, ALU.add)
            dve.wait_ge(s["bias_in"], 32)
            v.tensor_scalar(bias[:, 0:6], bias[:, 0:6], SQ, None, ALU.mult)
            v.tensor_scalar(bias[:, 8:88], bias[:, 8:88], SR, None, ALU.mult).then_inc(s["consts"], 1)

            def ffn(p):
                def hidden(i, st):
                    bank, col = p.bank(st, 1 if p.gated else 0)
                    src, n = ps[:, bank, col:col + p.n], i * 16 + (st + 1)
                    if p.gated:
                        dve.wait_ge(p.g, n)
                        v.tensor_tensor(p.fbuf(st), src, p.gbuf(st), ALU.mult).then_inc(p.mul, 1)
                        dve.wait_ge(p.hi, n)
                        v.tensor_tensor(hid[:, st % 4, 1, 0:p.n], p.fbuf(st), hid[:, st % 4, 0, 0:p.n],
                                        ALU.subtract).then_inc(p.h, 1)
                    else:
                        dve.wait_ge(p.hi, n)
                        v.scalar_tensor_tensor(hid[:, st % 4, 1, 0:p.n], src, 0.0, hid[:, st % 4, 0, 0:p.n],
                                               ALU.max, ALU.subtract).then_inc(p.h, 1)

                def evacuate(i, half):
                    if p.two_experts:
                        if half == 0:
                            return
                        dve.wait_ge(p.l2, i * 2 + 2)
                        dve.wait_ge(p.ev, i * 2 + 1)
                        v.scalar_tensor_tensor(outb[:, :, 0:p.n], ps[:, 6:8, 0:p.n], wab[:, 1, ds(i, 1)],
                                               outb[:, :, 0:p.n], ALU.mult, ALU.add).then_inc(p.ev, 1)

                def feature(i, half):
                    if p.two_experts:
                        if half == 0:
                            return
                        dve.wait_ge(p.ev, i * 2 + 2)
                    else:
                        dve.wait_ge(p.ev, i * 2 + (half + 1))
                    nb = p.n // S
                    if p.dynamic:
                        c = i if p.two_experts else i * 2 + half
                        b0 = dve.value_load(tbl[0:1, ds(c + T_POS, 1)], min_val=0, max_val=B)
                    else:
                        b0 = (i * 2 + half) * nb
                    v.tensor_copy(gate_in[:, p.feat, :, ds(b0, nb)], outb[:, :, 0:p.n:S]).then_inc(p.feat_done, 1)

                def body(i, first, lastone):
                    for st in range(16):
                        hidden(i, st)
                        if st == 1 and not first:
                            evacuate(i - 1, 1)
                        if st == 9:
                            evacuate(i, 0)
                        if st == 3 and not first:
                            feature(i - 1, 1)
                        if st == 11:
                            feature(i, 0)
                        if p is cs and not lastone and st in (3, 11):
                            x_group(i * 2 + (2 if st == 3 else 3), 0 if st == 3 else 1)
                body(0, True, False)
                with dve.Fori(1, p.iters - 1) as i:
                    body(i, False, False)
                body(p.iters - 1, False, True)
                evacuate(p.iters - 1, 1)
                feature(p.iters - 1, 1)

            def gate(n_out, turn):
                dve.wait_ge(s["gw_in"], 32 * turn)
                for j in range(n_out):
                    last = v.tensor_copy(gate_rep[:, j, :, :], (gate_w2 if turn == 2 else gate_w2c)[:, :, j:j + 1]
                                         .to_broadcast([128, 2, 128]))
                last.then_inc(s["gate_rdy"], 1)
                dve.wait_ge(s["gate_mm"], 2 * turn - 1)
                v.tensor_scalar(gate_hid, ps[:, 0:2, 0:B], 0.0, None, ALU.max).then_inc(s["gate_rdy"], 1)
                dve.wait_ge(s["gate_mm"], 2 * turn)
                logits = ps[:, 2, 0:n_out * B].rearrange("p (j b) -> p b j", j=n_out)
                g = gates[:, :, 0:n_out]
                over_j = gate_mx.unsqueeze(2).to_broadcast([128, B, n_out])
                link(v.reduce_max(gate_mx, logits, AX.X))
                v.tensor_tensor(g, logits, over_j, ALU.subtract).then_inc(s["soft_sub"], 1)
                dve.wait_ge(s["soft_exp"], 1 + turn)
                link(v.reduce_sum(gate_mx, g, AX.X))
                link(v.reciprocal(gate_mx, gate_mx))
                if turn == 1:
                    link(v.tensor_scalar(gate_mx, gate_mx, SY, None, ALU.mult))
                link(v.tensor_tensor(g, g, over_j, ALU.mult))
                dve.sem_inc(s["gates"], 1)

            ffn(cs)
            ffn(ce)
            gate(2, 1)

            def softmax_shift(c, r):
                dve.wait_ge(s["s_mm"], c * 2 + (r - 1))
                sc = ps[:, 2 * r:2 * r + 2, :].rearrange("p a (h n) -> p (a h) n", n=S)
                v.reduce_max(mx[:, r, :], sc, AX.X).then_inc(s["mx"], 1)
                dve.wait_ge(s["mx"], c * 2 + (r - 1))
                v.tensor_tensor(heads(prob[:, r, :]), sc, mx[:, r, :].unsqueeze(2).to_broadcast([128, H, S]),
                                ALU.subtract).then_inc(s["sub"], 1)

            def softmax_sum(c, r):
                dve.wait_ge(s["exp"], c * 2 + (r - 1))
                v.reduce_sum(sm[:, r, :], heads(prob[:, r, :]), AX.X).then_inc(s["norm"], 1)
                dve.wait_ge(s["norm"], c * 4 + (2 * r - 3))
                v.reciprocal(rs[:, r, :], sm[:, r, :]).then_inc(s["norm"], 1)

            def qk_low(c, w, dst):
                dve.wait_ge(s["qk_hi"], c * 2 + (w + 1))
                for m in range(KC):
                    last = v.scalar_tensor_tensor(dst[:, 1, m, :], ps[:, 4 + w, m * CH:(m + 1) * CH],
                                                  ab[:, w, m:m + 1], dst[:, 0, m, :], ALU.add, ALU.subtract)
                last.then_inc(s["qk_lo"], 1)

            def attn(c, new, old, fin, more):
                if old:
                    softmax_shift(c, 0)
                if fin:
                    dve.wait_ge(s["wo_mm"], c - 1)
                    dve.wait_ge(s["xb"], c - 1)
                    if not isinstance(c, int) or c >= 3:
                        dve.wait_ge(s["x1_lo"], c - 2)
                        dve.wait_ge(s["x1_out"], c * 16 - 32)
                    v.scalar_tensor_tensor(x1.rearrange("p k n -> p (k n)"), ps[:, 5, :], 1 / (SQ * SA),
                                           xin.rearrange("p k n -> p (k n)"), ALU.mult, ALU.add).then_inc(s["x1"], 1)
                if old:
                    softmax_shift(c, 1)
                    softmax_sum(c, 0)
                if fin:
                    dve.wait_ge(s["x1_hi"], c - 1)
                    cols = ds((c - 2) * CH, CH)
                    v.scalar_tensor_tensor(xh[:, 1, :, cols], x1, SX, xh[:, 0, :, cols],
                                           ALU.mult, ALU.subtract).then_inc(s["x1_lo"], 1)
                if new:
                    qk_low(c, 0, qh)
                if old:
                    softmax_sum(c, 1)
                if new:
                    qk_low(c, 1, kh)
                    dve.wait_ge(s["qk_lo"], c * 2 + 2)
                for r in range(2):
                    if old:
                        for hb in range(2):
                            dve.wait_ge(s["pt_hi"], c * 4 + (2 * r + hb - 3))
                            cols = slice(hb * 512, (hb + 1) * 512)
                            v.tensor_tensor(pt[:, r, 1, cols], ps[:, 2 * r + hb, :], pt[:, r, 0, cols],
                                            ALU.subtract).then_inc(s["pt_lo"], 1)
                    if new:
                        for h in ((0, 1, 2) if r == 0 else range(3, KBD_DVE)):
                            last = v.tensor_scalar(kbd_head(h), kh_batches, head_mask[:, h:h + 1], None, ALU.mult)
                        if r == 1:
                            last.then_inc(s["kbd"], 1)
                if old:
                    dve.wait_ge(s["o_hi"], c)
                    for m in range(KC):
                        last = v.scalar_tensor_tensor(oh_[:, 1, m, :], ps[:, 4, m * CH:(m + 1) * CH], ab[:, 2, m:m + 1],
                                                      oh_[:, 0, m, :], ALU.add, ALU.subtract)
                    last.then_inc(s["o_lo"], 1)
                if new:
                    dve.wait_ge(s["v_hi"], c + 1)
                    for r in range(2):
                        for j in range(2):
                            last = v.scalar_tensor_tensor(vb(1, r, j), vp(r, j), half_mask[:, j:j + 1], vb(0, r, j),
                                                          ALU.mult, ALU.subtract)
                    last.then_inc(s["v_lo"], 1)

            attn(0, True, False, False, True)
            attn(1, True, True, False, True)
            with dve.Fori(2, NA - 1) as c:
                attn(c, True, True, True, True)
            attn(NA - 1, True, True, True, False)
            attn(NA, False, True, True, False)
            attn(NA + 1, False, False, True, False)

            for p in es:
                ffn(p)
            ffn(ee)
            gate(4, 2)

            dve.wait_ge(s["w3_in"], 16)
            raw = misc[:, 2400:2464].rearrange("p (f e) -> p f e", f=FC)
            link(v.tensor_scalar(w3[:, :, 0:NE], raw, SW, None, ALU.mult))
            v.scalar_tensor_tensor(w3[:, :, NE:2 * NE], raw, SW, w3[:, :, 0:NE], ALU.mult, ALU.subtract).then_inc(s["w3"], 1)

            def z_make(c, u):
                k, zsrc = c * 2 + u, zsrcs[:, u]
                dve.wait_ge(s[f"z_in{u}"], c * 64 + 64)
                for j in range(4):
                    last = weighted(v, zsrc[:, j, :, :], k * GB, GB, j)
                last.then_inc(s["zchain"], 1)
                dve.wait_ge(s["zchain"], k * 2 + 1)
                v.tensor_tensor(zsrc[:, 0:2, :, :].rearrange("p j k n -> p j (k n)"),
                                zsrc[:, 0:2, :, :].rearrange("p j k n -> p j (k n)"),
                                zsrc[:, 2:4, :, :].rearrange("p j k n -> p j (k n)"), ALU.add).then_inc(s["zchain"], 1)
                dve.wait_ge(s["zchain"], k * 2 + 2)
                v.tensor_tensor(zsrc[:, 0, :, :], zsrc[:, 0, :, :], zsrc[:, 1, :, :], ALU.add).then_inc(s["z_sum"], 1)
                dve.wait_ge(s["z_hi"], k + 1)
                cols = ds(k * CH, CH)
                v.scalar_tensor_tensor(xh[:, 1, :, cols], zsrc[:, 0, :, :], SZ, xh[:, 0, :, cols],
                                       ALU.mult, ALU.subtract).then_inc(s["z_lo"], 1)

            def logits(c):
                dve.wait_ge(s["l_mm"], c + 1)
                l4 = ps[:, 6, 0:8 * NE].rearrange("p (t h e) -> p t h e", t=4, h=2)
                v.scalar_tensor_tensor(part_sum, l4[:, :, 0, :], 1 / (SR * SW), rb3.unsqueeze(1).to_broadcast([128, 4, NE]),
                                       ALU.mult, ALU.add).then_inc(s["lpart"], 1)
                dve.wait_ge(s["lpart"], c + 1)
                v.scalar_tensor_tensor(logit[:, ds(c * 4, 4), :], l4[:, :, 1, :], 1 / (SR * SW), part_sum,
                                       ALU.mult, ALU.add).then_inc(s["logit"], 1)

            def router(c, previous, more):
                for st in range(16):
                    dve.wait_ge(s["r_hi"], c * 16 + (st + 1))
                    dst = h1[:, st, :, :] if st < FC else h2[:, st - FC, :, :]
                    v.tensor_tensor(dst[:, 1, :], gt[:, (st % 2) * 512:(st % 2 + 1) * 512], dst[:, 0, :],
                                    ALU.subtract).then_inc(s["r_lo"], 1)
                    if previous and st == 7:
                        logits(c - 1)
                    if more and st in (8, 11):
                        z_make(c + 1, 0 if st == 8 else 1)
            z_make(0, 0)
            z_make(0, 1)
            router(0, False, True)
            with dve.Fori(1, 7) as c:
                router(c, True, True)
            router(7, True, False)
            logits(7)

            def over_e(x):
                return x.unsqueeze(2).to_broadcast([128, NP, NE])
            m1 = top8[:, :, 0:1].rearrange("p t e -> p (t e)")
            dve.wait_ge(s["logit"], 8)
            link(v.reduce_max(m1, logit, AX.X))
            v.tensor_tensor(score, logit, over_e(m1), ALU.subtract).then_inc(s["soft_sub"], 1)
            dve.wait_ge(s["soft_exp"], 4)
            link(v.reduce_sum(m1, score, AX.X))
            link(v.reciprocal(m1, m1))
            link(v.tensor_tensor(score, score, over_e(m1), ALU.mult))
            for t in range(NP):
                last = v.max(top8[:, t, :], score[:, t, :])
            link(last)
            for t in range(NP):
                last = v.max_index(index8[:, t, :], top8[:, t, :], score[:, t, :])
            link(last)
            experts = row[:, 0:NE].unsqueeze(1).to_broadcast([128, NP, NE])
            link(v.tensor_copy(pos, index8))
            for n, o in enumerate((oh0, oh1)):
                last = v.tensor_tensor(o, experts, over_e(pos[:, :, n:n + 1].rearrange("p t e -> p (t e)")), ALU.is_equal)
            link(last)
            link(v.tensor_tensor(oh0, oh0, oh1, ALU.add))
            v.tensor_copy(oh16, oh0).then_inc(s["oh"], 1)
            dve.wait_ge(s["pos_mm"], 1)
            flat = lambda x: x.rearrange("p t e -> p (t e)")
            link(v.tensor_copy(flat(pos), ps[:, 0, 0:NP * NE]))
            link(v.scalar_tensor_tensor(pos, oh0, -64.0, pos, ALU.mult, ALU.add))
            te = lambda x: flat(x).unsqueeze(2).to_broadcast([128, NP * NE, CAP])
            dt = dtmp.rearrange("p t (e n) -> p (t e) n", n=CAP)
            v.tensor_tensor(dt, te(pos), slot_row[:, :].unsqueeze(1).to_broadcast([128, NP * NE, CAP]), ALU.is_equal
                            ).then_inc(s["slot_oh"], 1)
            dve.wait_ge(s["slot_oh"], 1)
            dt2 = dtmp2.rearrange("p t (e n) -> p (t e) n", n=CAP)
            link(v.tensor_tensor(dt2, dt, te(score), ALU.mult))
            v.tensor_scalar(dsc[:, 0, :, :], dtmp2, SCW, None, ALU.mult).then_inc(s["slot_oh"], 1)
            dve.wait_ge(s["slot_oh"], 2)
            dve.wait_ge(s["d01"], 1)
            v.scalar_tensor_tensor(dsc[:, 1, :, :], dtmp2, SCW, dsc[:, 0, :, :], ALU.mult, ALU.subtract
                                   ).then_inc(s["slot_oh"], 1)

            def turn(t, u):
                dve.wait_ge(s["zt_mm"], t + (u + 1))
                v.tensor_copy(ztok[:, u % 2, :, :, :].rearrange("p h k n -> p (h k n)"), zt_ps[u % 2]).then_inc(s["zt"], 1)

            def gather(t, u):
                dve.wait_ge(s["dp_mm"], t + (u + 1))
                for k in range(KC):
                    v.tensor_copy(xe_pair(1, k, t, u), dp(u, 1, k)).then_inc(s["xe_lo"], 1)

            def dispatch(t, lastone=False):
                turn(t, 1)
                gather(t, 0)
                if not lastone:
                    turn(t, 2)
                gather(t, 1)
            turn(0, 0)
            with dve.Fori(0, NP // 2 - 1) as half_t:
                dispatch(half_t * 2)
            dispatch(NP - 2, True)

            dve.wait_ge(s["eb2_in"], 16)
            link(v.tensor_scalar(misc[:, 4608:6656], misc[:, 4608:6656], SEO, None, ALU.mult))

            def eout(e, half, tiles=None):
                for t in (tiles or TILES[half]):
                    dve.wait_ge(s["m_out"], e * 2 + (half + 1))
                    if t >= 2:
                        dve.wait_ge(s["eo_lo"], e * 5 + (t - 1))
                    elif t == 0 and not (isinstance(e, int) and e == 0):
                        dve.wait_ge(s["eo_lo"], e * 5)
                    v.scalar_tensor_tensor(ev[:, t % 2, :], ps[:, 3 + t, 0:D], SEO / (SR * SW), misc[:, ds(e * D + 4608, D)],
                                           ALU.mult, ALU.add).then_inc(s["ev"], 1)
                    dve.wait_ge(s["eo_hi"], e * 5 + (t + 1))
                    v.tensor_tensor(eo[:, t % 4, 1, :], ev[:, t % 2, :], eo[:, t % 4, 0, :], ALU.subtract).then_inc(s["eo_lo"], 1)

            def expert(e, par, fresh=False, lastone=False):
                for st in range(16):
                    n = len(TILES[st // FC]) * 128
                    dve.wait_ge(s["m_hi"], e * 16 + (st + 1))
                    v.tensor_tensor(hid[:, st % 4, 1, 0:n], egt[:, st % 4, 0:n],
                                    hid[:, st % 4, 0, 0:n], ALU.subtract).then_inc(s["m_lo"], 1)
                    if st in (1, 2) and not fresh:
                        eout(e - 1, 1, (2 + st,))
                    if st in (8, 9, 10):
                        eout(e, 0, (st - 8,))
                    if st in (5, 6, 12, 13) and not lastone:
                        w, h = int(st >= 12), st % 6 != 5 and st != 12
                        slot, cols = MOE_W[1 - par][w], slice(h * (MAT // 2), (h + 1) * (MAT // 2))
                        dve.wait_ge(s["mw_hi"], e * 2 + (w + 1))
                        last = v.scalar_tensor_tensor(w16(slot, 1, h * (MAT // 2), MAT // 2),
                                                      wstage[:, (FIRST_MOE + w) % 2, cols], SW,
                                                      w16(slot, 0, h * (MAT // 2), MAT // 2), ALU.mult, ALU.subtract)
                        if h:
                            last.then_inc(s["mw_lo"], 1)
            expert(0, 0, fresh=True)
            expert(1, 1)
            with dve.Fori(1, NE // 2 - 1) as half_e:
                e = half_e * 2
                expert(e, 0)
                expert(e + 1, 1)
            expert(NE - 2, 0)
            expert(NE - 1, 1, lastone=True)
            eout(NE - 1, 1)

            def output(q, u):
                dve.wait_ge(s["fin_mm"], q * 8 + (u + 1))
                if not (isinstance(q, int) and q == 0):
                    dve.wait_ge(s[f"fin_st{FIN_ST[u]}"], q * (32 * FIN_ST.count(FIN_ST[u])))
                for b2 in range(2):
                    last = v.scalar_tensor_tensor(yo[:, u, b2, :, :],
                                                  ps[:, u, b2 * 128:(b2 + 1) * 128].rearrange("p (k n) -> p k n", k=KC),
                                                  1 / (SEO * SCW), x1f[:, :, ds(q * 1024 + (2 * u + b2) * S, S)],
                                                  ALU.mult, ALU.add)
                last.then_inc(s["fin"], 1)
            dve.wait_ge(s["x1_in"], 16)
            for u in range(8):
                output(0, u)
            with dve.Fori(1, NP // 8) as q:
                for u in range(8):
                    output(q, u)


_NAMES = ("itok", "gv", "bias", "rb3", "x", "c_swi0", "c_swi1", "c_swo", "c_wi0", "c_wi1", "c_wo", "c_g0", "c_g1",
          "a_w", "e_wi", "e_wo", "e_swi", "e_swo", "e_g1", "e_g2", "r_w1", "r_w2", "r_w3", "m_w1", "m_w2", "eb2")


def kernel(**inputs):
    import concourse.bacc as bacc
    from concourse.bass_utils import run_bass_kernel_spmd

    g = {k.replace("L0_", ""): np.asarray(v) for k, v in inputs.items()}

    def rows(w):
        *lead, r, n = w.shape
        return np.ascontiguousarray(np.moveaxis(w.reshape(*lead, r // 128, 128, n), -2, -3)).reshape(*lead, 128, -1)

    def cols(b):
        return np.moveaxis(b.reshape(-1, b.shape[-1] // 128, 128), -1, 0).reshape(128, -1)

    arrays = {
        "itok": g["itok_B_0_2"].astype(np.int32).reshape(B, 1),
        "gv": g["cond2_gate_vecs"].reshape(-1),
        "bias": np.concatenate([cols(g[n]) for n in ("attn_bq", "attn_bk", "attn_bv", "attn_bo", "ffn_rb1", "ffn_rb2",
                                                     "ffn_eb1")], axis=1),
        "rb3": g["ffn_rb3"],
        "x": g["x"].reshape(B, S, KC, 128).transpose(0, 3, 2, 1).reshape(B, 128, KC * S),
        "c_swi0": rows(g["cond_sWi0"]), "c_swi1": rows(g["cond_sWi1"]), "c_swo": rows(g["cond_sWo"]),
        "c_wi0": rows(g["cond_Wi0"]), "c_wi1": rows(g["cond_Wi1"]), "c_wo": rows(g["cond_Wo"]),
        "c_g0": rows(g["cond_g0"]), "c_g1": rows(g["cond_g1"]),
        "a_w": np.concatenate([rows(g[f"attn_W{c}"].T) for c in "qkvo"], axis=1),
        "e_wi": rows(g["cond2_expert_wi"]), "e_wo": rows(g["cond2_expert_wo"]),
        "e_swi": rows(g["cond2_share_wi"]), "e_swo": rows(g["cond2_share_wo"]),
        "e_g1": rows(g["cond2_gate_w1"]), "e_g2": rows(g["cond2_gate_w2"]),
        "r_w1": rows(g["ffn_rW1"]), "r_w2": rows(g["ffn_rW2"].reshape(4, 2 * 128, F)), "r_w3": rows(g["ffn_rW3"]),
        "m_w1": rows(g["ffn_eW1"]), "m_w2": rows(g["ffn_eW2"]),
        "eb2": g["ffn_eb2"].reshape(-1),
    }
    nc = bacc.Bacc("TRN2", target_bir_lowering=False, num_devices=1)
    feeds, a = {}, {}
    for n in _NAMES:
        arr = np.ascontiguousarray(arrays[n])
        feeds[f"in_{n}"] = arr
        a[n] = nc.dram_tensor(f"in_{n}", arr.shape, mybir.dt.from_np(arr.dtype), kind="ExternalInput").ap()
    a["out"] = nc.dram_tensor("out_x", (B, 128, KC * S), F32, kind="ExternalOutput").ap()
    build(nc, a)
    got = np.asarray(run_bass_kernel_spmd(nc, [feeds], core_ids=[0]).results[0]["out_x"])
    return np.ascontiguousarray(got.reshape(B, 128, KC, S).transpose(0, 3, 2, 1)).reshape(B, S, D)
```
